# Optimizing a Trainium2 kernel written in Bass

```python
import numpy as np
import jax
import jax.numpy as jnp

def _softmax(x, axis=-1):
    return jax.nn.softmax(x, axis=axis)

def _gelu(x):
    return jax.nn.gelu(x, approximate=True)

def _silu(x):
    return jax.nn.silu(x)

def _sigmoid(x):
    return jax.nn.sigmoid(x)

def _layernorm(x, axis=-1, eps=1e-05):
    m = jnp.mean(x, axis=axis, keepdims=True)
    v = jnp.var(x, axis=axis, keepdims=True)
    return (x - m) / jnp.sqrt(v + eps)

def _scatter_add(tgt, idx, src, axis=0):
    return tgt.at[idx].add(src)

def _segment_sum(src, seg, n):
    return jax.ops.segment_sum(src, seg, n)
kernel_name = 'mk_gnn_preln_d4_gnn_r8_4fb028'

def setup_inputs(seed: int=0):
    np.random.seed(seed)
    _w = jnp.asarray

    def _rec_inputs():
        import jax
        import jax.numpy as jnp
        _gk = jax.random.key(seed)
        x = -0.0002117 + 1 * jax.random.normal(jax.random.fold_in(_gk, 1), (6250, 256), jnp.float32)
        _s = jax.random.randint(jax.random.fold_in(_gk, 2), (50000,), 0, 6250, jnp.int32)
        _d = jax.random.randint(jax.random.fold_in(_gk, 3), (50000,), 0, 6250, jnp.int32)
        _loop = jnp.arange(6250, dtype=jnp.int32)
        src = jnp.concatenate([_s, _d, _loop])
        dst = jnp.concatenate([_d, _s, _loop])
        _o = jnp.argsort(dst, stable=True)
        src = src[_o]
        dst = dst[_o]
        edge_type_8 = jax.random.randint(jax.random.fold_in(_gk, 13), (106250,), 0, 8, jnp.int32)
        return (x, src, dst, edge_type_8)
    x, src, dst, edge_type_8 = _rec_inputs()

    def _L0_gnn_setup():
        import jax, jax.numpy as jnp
        import numpy as np
        N_NODES = 12500
        N_EDGES = 400000
        IN_FEATS = 256
        OUT_FEATS = 256
        key = jax.random.key(seed)
        k1, k2, k3, k4 = jax.random.split(key, 4)
        x = jax.random.normal(k1, (N_NODES, IN_FEATS), dtype=jnp.float32)
        edge_index = jax.random.randint(k2, (2, N_EDGES), 0, N_NODES, dtype=jnp.int64)
        bound = 1.0 / np.sqrt(2 * IN_FEATS)
        W = jax.random.uniform(k3, (OUT_FEATS, 2 * IN_FEATS), minval=-bound, maxval=bound, dtype=jnp.float32)
        b = jax.random.uniform(k4, (OUT_FEATS,), minval=-bound, maxval=bound, dtype=jnp.float32)
        return {'x': x, 'edge_index': edge_index, 'W': W, 'b': b}
    _L0_gnn_all = _L0_gnn_setup()
    _L0_gnn_in = {k: v for k, v in _L0_gnn_all.items() if k in ('W', 'b')}
    del _L0_gnn_all

    def _L1_gnn_setup():
        import jax, jax.numpy as jnp
        import numpy as np
        N, E, H, R = (6250, 100000, 256, 8)
        LN_EPS = 1e-05

        def _rgcn_layer(node_states, edge_index, edge_type_ids, W_rel, W_root, bias, ln_gamma, ln_beta):
            n, h = node_states.shape
            r = W_rel.shape[0]
            src, dst = (edge_index[0], edge_index[1])
            seg = dst * r + edge_type_ids
            msgs = node_states[src]
            sums = jax.ops.segment_sum(msgs, seg, num_segments=n * r).reshape(n, r, h)
            counts = jax.ops.segment_sum(jnp.ones((src.shape[0],), node_states.dtype), seg, num_segments=n * r).reshape(n, r, 1)
            mean = sums / jnp.maximum(counts, 1.0)
            agg = jnp.einsum('nrh,rho->no', mean, W_rel)
            conv = agg + node_states @ W_root + bias
            updated = jax.nn.gelu(conv, approximate=False)
            x = updated + node_states
            mu = jnp.mean(x, axis=-1, keepdims=True)
            var = jnp.mean(jnp.square(x - mu), axis=-1, keepdims=True)
            return ln_gamma * (x - mu) * jax.lax.rsqrt(var + LN_EPS) + ln_beta
        key = jax.random.key(seed)
        ks = jax.random.split(key, 6)
        node_states = jax.random.normal(ks[0], (N, H), dtype=jnp.float32)
        edge_index = jax.random.randint(ks[1], (2, E), 0, N, dtype=jnp.int64)
        edge_type_ids = jax.random.randint(ks[2], (E,), 0, R, dtype=jnp.int64)
        scale = 1.0 / np.sqrt(H)
        W_rel = jax.random.normal(ks[3], (R, H, H), dtype=jnp.float32) * scale
        W_root = jax.random.normal(ks[4], (H, H), dtype=jnp.float32) * scale
        bias = jnp.zeros((H,), dtype=jnp.float32)
        ln_gamma = jnp.ones((H,), dtype=jnp.float32)
        ln_beta = jnp.zeros((H,), dtype=jnp.float32)
        return {'node_states': node_states, 'edge_index': edge_index, 'edge_type_ids': edge_type_ids, 'W_rel': W_rel, 'W_root': W_root, 'bias': bias, 'ln_gamma': ln_gamma, 'ln_beta': ln_beta}
    _L1_gnn_all = _L1_gnn_setup()
    _L1_gnn_in = {k: v for k, v in _L1_gnn_all.items() if k in ('W_rel', 'W_root', 'bias', 'ln_gamma', 'ln_beta')}
    del _L1_gnn_all

    def _L2_gnn_setup():
        import jax, jax.numpy as jnp
        import numpy as np
        NEG = -1000.0
        SLOPE = 0.01
        N_NODES, N_EDGES, D_IN, D_OUT, N_HEADS = (12500, 200000, 256, 64, 4)
        key = jax.random.key(seed)
        k0, k1, k2, k3, k4 = jax.random.split(key, 5)
        h = jax.random.normal(k0, (N_NODES, D_IN), jnp.float32)
        src = jax.random.randint(k1, (N_EDGES,), 0, N_NODES)
        dst = jax.random.randint(k2, (N_EDGES,), 0, N_NODES)
        W = jax.random.normal(k3, (N_HEADS, D_IN, D_OUT), jnp.float32) / np.sqrt(D_IN)
        att = jax.random.normal(k4, (N_HEADS, 2 * D_OUT), jnp.float32) / np.sqrt(2.0 * D_OUT)
        return {'h': h, 'W': W, 'att': att, 'src': src, 'dst': dst}
    _L2_gnn_all = _L2_gnn_setup()
    _L2_gnn_in = {k: v for k, v in _L2_gnn_all.items() if k in ('W', 'att')}
    del _L2_gnn_all

    def _L3_gnn_setup():
        import jax, jax.numpy as jnp
        import numpy as np
        N = 6250
        E = 100000
        F = 256
        H = 256

        def prelu(z, a):
            return jnp.where(z > 0, z, a * z)
        key = jax.random.key(seed)
        ks = jax.random.split(key, 8)
        sf = 1.0 / np.sqrt(F)
        sh = 1.0 / np.sqrt(H)
        return {'x': jax.random.normal(ks[0], (N, F), jnp.float32), 'senders': jax.random.randint(ks[1], (E,), 0, N, jnp.int32), 'receivers': jax.random.randint(ks[2], (E,), 0, N, jnp.int32), 'W_pre': jax.random.normal(ks[3], (F, H), jnp.float32) * sf, 'b_pre': jnp.zeros((H,), jnp.float32), 'alpha_pre': jnp.full((H,), 0.25, jnp.float32), 'W_mp': jax.random.normal(ks[4], (H, H), jnp.float32) * sh, 'b_mp': jnp.zeros((H,), jnp.float32), 'alpha_mp': jnp.full((H,), 0.25, jnp.float32), 'W_post': jax.random.normal(ks[5], (H, F), jnp.float32) * sh, 'b_post': jnp.zeros((F,), jnp.float32)}
    _L3_gnn_all = _L3_gnn_setup()
    _L3_gnn_in = {k: v for k, v in _L3_gnn_all.items() if k in ('W_pre', 'b_pre', 'alpha_pre', 'W_mp', 'b_mp', 'alpha_mp', 'W_post', 'b_post')}
    del _L3_gnn_all
    return {'x': x, 'src': src, 'dst': dst, 'edge_type_8': edge_type_8, 'L0_gnn_W': _L0_gnn_in['W'], 'L0_gnn_b': _L0_gnn_in['b'], 'L1_gnn_W_rel': _L1_gnn_in['W_rel'], 'L1_gnn_W_root': _L1_gnn_in['W_root'], 'L1_gnn_bias': _L1_gnn_in['bias'], 'L1_gnn_ln_gamma': _L1_gnn_in['ln_gamma'], 'L1_gnn_ln_beta': _L1_gnn_in['ln_beta'], 'L2_gnn_W': _L2_gnn_in['W'], 'L2_gnn_att': _L2_gnn_in['att'], 'L3_gnn_W_pre': _L3_gnn_in['W_pre'], 'L3_gnn_b_pre': _L3_gnn_in['b_pre'], 'L3_gnn_alpha_pre': _L3_gnn_in['alpha_pre'], 'L3_gnn_W_mp': _L3_gnn_in['W_mp'], 'L3_gnn_b_mp': _L3_gnn_in['b_mp'], 'L3_gnn_alpha_mp': _L3_gnn_in['alpha_mp'], 'L3_gnn_W_post': _L3_gnn_in['W_post'], 'L3_gnn_b_post': _L3_gnn_in['b_post']}

def reference(x, src, dst, edge_type_8, L0_gnn_W, L0_gnn_b, L1_gnn_W_rel, L1_gnn_W_root, L1_gnn_bias, L1_gnn_ln_gamma, L1_gnn_ln_beta, L2_gnn_W, L2_gnn_att, L3_gnn_W_pre, L3_gnn_b_pre, L3_gnn_alpha_pre, L3_gnn_W_mp, L3_gnn_b_mp, L3_gnn_alpha_mp, L3_gnn_W_post, L3_gnn_b_post):
    import jax
    import jax.numpy as jnp

    def _L0_gnn_ref(x, edge_index, W, b):
        import jax, jax.numpy as jnp
        import numpy as np
        N_NODES = 12500
        N_EDGES = 400000
        IN_FEATS = 256
        OUT_FEATS = 256
        dst, src = (edge_index[0], edge_index[1])
        agg = jnp.zeros_like(x).at[dst].set(x[src])
        h = jnp.concatenate((x, agg), axis=-1)
        return h @ W.T + b

    def _L1_gnn_ref(node_states, edge_index, edge_type_ids, W_rel, W_root, bias, ln_gamma, ln_beta):
        import jax, jax.numpy as jnp
        import numpy as np
        N, E, H, R = (6250, 100000, 256, 8)
        LN_EPS = 1e-05

        def _rgcn_layer(node_states, edge_index, edge_type_ids, W_rel, W_root, bias, ln_gamma, ln_beta):
            n, h = node_states.shape
            r = W_rel.shape[0]
            src, dst = (edge_index[0], edge_index[1])
            seg = dst * r + edge_type_ids
            msgs = node_states[src]
            sums = jax.ops.segment_sum(msgs, seg, num_segments=n * r).reshape(n, r, h)
            counts = jax.ops.segment_sum(jnp.ones((src.shape[0],), node_states.dtype), seg, num_segments=n * r).reshape(n, r, 1)
            mean = sums / jnp.maximum(counts, 1.0)
            agg = jnp.einsum('nrh,rho->no', mean, W_rel)
            conv = agg + node_states @ W_root + bias
            updated = jax.nn.gelu(conv, approximate=False)
            x = updated + node_states
            mu = jnp.mean(x, axis=-1, keepdims=True)
            var = jnp.mean(jnp.square(x - mu), axis=-1, keepdims=True)
            return ln_gamma * (x - mu) * jax.lax.rsqrt(var + LN_EPS) + ln_beta
        return _rgcn_layer(node_states, edge_index, edge_type_ids, W_rel, W_root, bias, ln_gamma, ln_beta)

    def _L2_gnn_ref(h, W, att, src, dst):
        import jax, jax.numpy as jnp
        import numpy as np
        NEG = -1000.0
        SLOPE = 0.01
        N_NODES, N_EDGES, D_IN, D_OUT, N_HEADS = (12500, 200000, 256, 64, 4)
        N = h.shape[0]
        H, _, F = W.shape
        z = jnp.einsum('nd,hdf->nhf', h, W)
        a_src, a_dst = (att[:, :F], att[:, F:])
        es = jnp.einsum('nhf,hf->nh', z, a_src)
        ed = jnp.einsum('nhf,hf->nh', z, a_dst)
        e = jax.nn.leaky_relu(es[src] + ed[dst], SLOPE)
        e = jnp.where(e == 0.0, NEG, e)
        m = jax.ops.segment_max(e, dst, num_segments=N)
        m = jnp.where(jnp.isfinite(m), m, 0.0)
        ex = jnp.exp(e - m[dst])
        denom = jax.ops.segment_sum(ex, dst, num_segments=N)
        safe = jnp.where(denom[dst] > 0.0, denom[dst], 1.0)
        alpha = ex / safe
        out = jax.ops.segment_sum(alpha[:, :, None] * z[src], dst, num_segments=N)
        return out.reshape(N, H * F)

    def _L3_gnn_ref(x, senders, receivers, W_pre, b_pre, alpha_pre, W_mp, b_mp, alpha_mp, W_post, b_post):
        import jax, jax.numpy as jnp
        import numpy as np
        N = 6250
        E = 100000
        F = 256
        H = 256

        def prelu(z, a):
            return jnp.where(z > 0, z, a * z)
        n = x.shape[0]
        h = prelu(x @ W_pre + b_pre, alpha_pre)
        m = h @ W_mp + b_mp
        agg = jax.ops.segment_sum(m[senders], receivers, num_segments=n)
        h2 = prelu(agg, alpha_mp) + h
        return jax.nn.relu(h2 @ W_post + b_post)
    edge_index = jnp.stack([src, dst])
    h = jnp.maximum(_layernorm(x, axis=-1), 0.0)
    x = x + _L0_gnn_ref(h, edge_index, L0_gnn_W, L0_gnn_b)
    h = jnp.maximum(_layernorm(x, axis=-1), 0.0)
    x = x + _L1_gnn_ref(h, edge_index, edge_type_8, L1_gnn_W_rel, L1_gnn_W_root, L1_gnn_bias, L1_gnn_ln_gamma, L1_gnn_ln_beta)
    h = jnp.maximum(_layernorm(x, axis=-1), 0.0)
    x = x + _L2_gnn_ref(h, L2_gnn_W, L2_gnn_att, src, dst)
    h = jnp.maximum(_layernorm(x, axis=-1), 0.0)
    x = x + _L3_gnn_ref(h, src, dst, L3_gnn_W_pre, L3_gnn_b_pre, L3_gnn_alpha_pre, L3_gnn_W_mp, L3_gnn_b_mp, L3_gnn_alpha_mp, L3_gnn_W_post, L3_gnn_b_post)
    return x

_drawn_inputs = setup_inputs


def setup_inputs(seed=0):
    import zlib

    import numpy as np

    out = dict(_drawn_inputs(seed))
    spreads = {'L1_gnn_bias': (0.0, 0.278),
     'L1_gnn_ln_gamma': (1.0, 0.2),
     'L1_gnn_ln_beta': (0.0, 0.1),
     'L3_gnn_b_pre': (0.0, 0.1),
     'L3_gnn_alpha_pre': (0.25, 0.2),
     'L3_gnn_b_mp': (0.0, 0.1),
     'L3_gnn_alpha_mp': (0.25, 0.2),
     'L3_gnn_b_post': (0.0, 0.469)}
    factors = {'L2_gnn_att': 3.905}
    for name, (base, spread) in spreads.items():
        noise = np.random.default_rng([zlib.crc32(name.encode()), seed]).standard_normal(out[name].shape)
        drawn = base * np.exp(spread * noise) if base else spread * noise
        out[name] = jnp.asarray(drawn.astype(out[name].dtype))
    for name, factor in factors.items():
        out[name] = (out[name] * factor).astype(out[name].dtype)
    return out
```

```python
import concourse.bass as bass
from concourse import mybir
from contextlib import ExitStack

FP32 = mybir.dt.float32
BF16 = mybir.dt.bfloat16
I32 = mybir.dt.int32
ALU = mybir.AluOpType
ACT = mybir.ActivationFunctionType
AX = mybir.AxisListType

N, D, E = 6250, 256, 106250
R, H, F = 8, 4, 64
P = 128
NT = 50
NP = NT * P
RT = 49
LAST = N - (RT - 1) * P
CH = -(-E // P)
EP = CH * P
CG = -(-CH // P)
FULLP = E // CH
REST = E - FULLP * CH
U = 16
ITEMS = -(-(CH + RT - 1) // U) * U
IG = -(-ITEMS // P)
LC, LCH = 125, 850
LG = -(-LCH // P)
LU = 8
LB = -(-LCH // LU)
NHI, NLO = 98, 64
PADDST = 8191.0
OOB = 60000.0
BIG = 1.0e30
EPS = 1e-5


def wait(eng, sem, value):
    if isinstance(value, int) and value <= 0:
        return
    eng.wait_ge(sem, value)


class Chain:

    def __init__(self, eng, sem, base=0):
        self.eng, self.sem, self.base, self.n = eng, sem, base, 0

    def __call__(self, ins):
        self.n += 1
        ins.then_inc(self.sem, 1)
        self.eng.wait_ge(self.sem, self.base + self.n)


def build(nc, A, out):
    top = ExitStack()
    with top:
        def dram(name, shape, dt=FP32):
            return nc.dram_tensor(name, shape, dt).ap()

        dst_d = dram("dst_d", (CH, P))
        src_d = dram("src_d", (CH, P))
        rel_d = dram("rel_d", (CH, P))
        wgt_d = dram("wgt_d", (CH, P))
        sc_d = [dram(f"sc_d{h}", (CH + 1, P)) for h in range(H)]
        ex_d = [dram(f"ex_d{h}", (CH, P)) for h in range(H)]
        last_d = dram("last_d", (NHI * NLO,))
        item_d = dram("item_d", (4, IG * P))
        h_d = dram("h_d", (NP, D))
        rel_t = dram("rel_t", (NP * R, D))
        z_t = dram("z_t", (NP, H * (F + 1)))
        att_t = dram("att_t", (NP, 2 * H))
        m_t = dram("m_t", (NP, D))
        agg_d = [dram(f"agg_d{l}", (NP, w)) for l, w in enumerate((D, H * (F + 1), D))]

        def sb(name, shape, dt=FP32, ctx=top):
            return ctx.enter_context(nc.sbuf_tensor(name, shape, dt))

        X = sb("X", [P, NT, D])
        Hh = sb("Hh", [P, NT, D])
        ident = sb("ident", [P, P])
        iota = sb("iota", [P, P])
        item_dst = sb("item_dst", [P, IG * P])
        item_rel = sb("item_rel", [P, IG * P], I32)
        item_src = sb("item_src", [P, IG * P], I32)
        item_wgt = sb("item_wgt", [P, IG * P])
        item_chunk = sb("item_chunk", [P, IG], I32)
        item_keep = sb("item_keep", [P, IG * P])
        item_row = sb("item_row", [1, IG * P], I32)
        eps_c = sb("eps_c", [P, 1])

        state = dict(nc=nc, A=A, out=out)
        env = dict(locals())
        setup(env)
        seg_weights(env)
        items(env)
        last_edges(env)
        layer0(env)
        layer1_tables(env)
        aggregate(env, "a1", 0, rel_t, D, N * R - 1, item_rel, "wgt")
        layer1_end(env)
        layer2_tables(env)
        edge_scores(env)
        softmax(env)
        score_items(env)
        aggregate(env, "a2", 1, z_t, H * (F + 1), N - 1, item_src, "ex")
        add_attention(env)
        layer3_tables(env)
        aggregate(env, "a3", 2, m_t, D, N - 1, item_src, None)
        layer3_end(env)


def agg_width(l):
    return H * (F + 1) if l == 1 else D


class Phase:

    def __init__(self, nc, name):
        self.nc, self.name, self.ctx, self.sems = nc, name, ExitStack(), []

    def __enter__(self):
        return self

    def __exit__(self, *a):
        self.ctx.close()
        self.nc.clear_and_free_semaphores(self.sems)
        self.nc.all_engine_barrier()

    def sb(self, name, shape, dt=FP32):
        return self.ctx.enter_context(self.nc.sbuf_tensor(f"{self.name}_{name}", shape, dt))

    def ps(self, name, shape, dt=FP32):
        return self.ctx.enter_context(self.nc.psum_tensor(f"{self.name}_{name}", shape, dt))

    def sem(self, name):
        self.sems.append(self.nc.alloc_semaphore(f"{self.name}_{name}"))
        return self.sems[-1]


def setup(env):
    nc, A = env["nc"], env["A"]
    X, ident, iota = env["X"], env["ident"], env["iota"]
    with Phase(nc, "su") as ph:
        di = ph.sb("di", [P, CH], I32)
        si = ph.sb("si", [P, CH], I32)
        ti = ph.sb("ti", [P, CH], I32)
        df, sf, tf = (ph.sb(n, [P, CH]) for n in ("df", "sf", "tf"))
        rl = ph.sb("rl", [P, CH])
        ones = ph.sb("ones", [P, P])
        cnt = ph.sb("cnt", [P, NT])
        bnd = ph.sb("bnd", [P, NT])
        bi = ph.sb("bi", [P, NT], I32)
        flo = ph.sb("flo", [P, NT])
        cei = ph.sb("cei", [P, NT])
        num = ph.sb("num", [P, NT])
        pre = ph.sb("pre", [P, NT])
        dlt = ph.sb("dlt", [P, NT])
        dd = ph.sb("dd", [P, NT])
        ii = ph.sb("ii", [P, IG])
        i1 = ph.sb("i1", [P, IG])
        it = ph.sb("it", [P, 4, IG])
        itT = ph.sb("itT", [IG, 4, P])
        jk = ph.sb("jk", [P, CH])
        krow = ph.sb("krow", [P, IG * P])
        rrow = ph.sb("rrow", [1, 3, IG * P])
        psb = ph.ps("psb", [P, NT])
        psi = ph.ps("psi", [IG, 4, P])
        dls, xl, cst, fill = ph.sem("edges_in"), ph.sem("x_in"), ph.sem("const"), ph.sem("filled")
        dv, cs, bs, its, itt, itc = (ph.sem(n) for n in ("dve", "counts", "bounds", "items", "itemsT", "itemsTc"))
        fst, put, back, pl, rdy = (ph.sem(n) for n in ("floats", "put", "back", "pool", "item_put"))
        with nc.Block() as block:
            @block.gpsimd
            def _(pool):
                chain = Chain(pool, pl)
                chain(pool.memset(ident[:, :], 0.0))
                chain(pool.affine_select(out=ident[:, :], in_=ident[:, :], compare_op=ALU.not_equal, fill=1.0,
                                         base=0, pattern=[[-1, P]], channel_multiplier=1))
                pool.iota(iota[:, :], pattern=[[1, P]], base=0, channel_multiplier=0,
                          allow_small_or_imprecise_dtypes=True).then_inc(cst, 1)
                pool.iota(ii[:, :], pattern=[[P, IG]], base=0, channel_multiplier=1,
                          allow_small_or_imprecise_dtypes=True).then_inc(cst, 1)
                pool.iota(i1[:, :], pattern=[[P, IG]], base=1, channel_multiplier=1,
                          allow_small_or_imprecise_dtypes=True).then_inc(cst, 1)
                pool.memset(ones[:, :], 1.0).then_inc(cst, 1)
                pool.memset(env["eps_c"][:, :], EPS).then_inc(cst, 1)
                pool.memset(X[:, RT - 1:NT, :], 0.0).then_inc(cst, 1)
                pool.wait_ge(cst, 6)

            @block.sync
            def _(sp):
                sp.wait_ge(fill, 3)
                full = FULLP * CH
                for t, name in ((di, "dst"), (si, "src"), (ti, "edge_type_8")):
                    sp.dma_start(t[0:FULLP, :], A[name][0:full].rearrange("(p f) -> p f", f=CH)).then_inc(dls, 16)
                    sp.dma_start(t[FULLP:FULLP + 1, 0:REST], A[name][full:E].rearrange("(a f) -> a f", a=1))\
                        .then_inc(dls, 16)
                sp.wait_ge(cst, 6)
                for c in range(0, RT - 1, 12):
                    sp.dma_start(X[:, c:c + 12, :], A["x"][c * P:(c + 12) * P, :].rearrange("(t p) d -> p t d", p=P))\
                        .then_inc(xl, 16)
                sp.dma_start(X[0:LAST, RT - 1, :], A["x"][(RT - 1) * P:N, :]).then_inc(xl, 16)
                for l in range(3):
                    w = agg_width(l)
                    for c in range(0, w, D):
                        sp.dma_start(env["agg_d"][l][RT * P:NP, c:min(c + D, w)], X[:, RT, 0:min(D, w - c)])\
                            .then_inc(put, 16)
                sp.wait_ge(fst, 1)
                for n, (t, d) in enumerate(((df, "dst_d"), (sf, "src_d"), (rl, "rel_d"))):
                    sp.dma_start(env[d].rearrange("c e -> (c e)").rearrange("(p f) -> p f", f=CH), t[:, :])\
                        .then_inc(put, 16)
                sp.wait_ge(itc, 1)
                for k in range(4):
                    sp.dma_start(env["item_d"][k, :].rearrange("(g p) -> g p", p=P), itT[:, k, :]).then_inc(rdy, 16)
                sp.wait_ge(rdy, 64)
                sp.dma_start(krow[:, :], env["item_d"][2:3, :].partition_broadcast(P)).then_inc(back, 16)
                sp.dma_start(rrow[0:1, 0, :], env["item_d"][1:2, :]).then_inc(back, 16)
                sp.dma_start(rrow[0:1, 1, :], env["item_d"][3:4, :]).then_inc(back, 16)
                sp.wait_ge(put, 48 + 64)
                sp.wait_ge(xl, 80)

            @block.vector
            def _(v):
                chain = Chain(v, dv)
                v.memset(di[:, :], int(PADDST)).then_inc(fill, 1)
                v.memset(si[:, :], 0).then_inc(fill, 1)
                v.memset(ti[:, :], 0).then_inc(fill, 1)
                v.wait_ge(fill, 3)
                v.wait_ge(dls, 16 * 6)
                chain(v.tensor_copy(df[:, :], di[:, :]))
                chain(v.tensor_copy(sf[:, :], si[:, :]))
                chain(v.tensor_copy(tf[:, :], ti[:, :]))
                v.scalar_tensor_tensor(out=rl[:, :], in0=sf[:, :], scalar=float(R), in1=tf[:, :],
                                       op0=ALU.mult, op1=ALU.add).then_inc(fst, 1)
                v.wait_ge(fst, 1)
                v.wait_ge(cst, 6)
                chain(v.memset(cnt[:, :], 0.0))
                for t in range(1, NT):
                    chain(v.tensor_scalar(jk[:, :], df[:, :], float(min(t * P, N)), 0.0, ALU.is_lt, ALU.add,
                                          accum_out=cnt[:, t:t + 1]))
                v.sem_inc(cs, 1)
                v.wait_ge(bs, 1)
                chain(v.tensor_copy(bnd[:, :], psb[:, :]))
                chain(v.tensor_copy(bi[:, :], bnd[:, :]))
                chain(v.tensor_scalar(bi[:, :], bi[:, :], 7, None, ALU.arith_shift_right))
                chain(v.tensor_copy(flo[:, :], bi[:, :]))
                chain(v.tensor_scalar(cei[:, :], bnd[:, :], float(P - 1), None, ALU.add))
                chain(v.tensor_copy(bi[:, :], cei[:, :]))
                chain(v.tensor_scalar(bi[:, :], bi[:, :], 7, None, ALU.arith_shift_right))
                chain(v.tensor_copy(cei[:, :], bi[:, :]))
                chain(v.memset(num[:, :], 0.0))
                chain(v.tensor_tensor(num[:, 1:NT], cei[:, 1:NT], flo[:, 0:NT - 1], ALU.subtract))
                chain(v.tensor_scalar(num[:, 1:NT], num[:, 1:NT], 1.0, None, ALU.max))
                chain(v.memset(dlt[:, :], 1.0))
                chain(v.tensor_tensor_scan(pre[:, :], dlt[:, :], num[:, :], 0.0, ALU.mult, ALU.add))
                chain(v.tensor_tensor(dlt[:, :], flo[:, :], pre[:, :], ALU.subtract))
                chain(v.tensor_copy(dd[:, 0:1], dlt[:, 0:1]))
                chain(v.tensor_tensor(dd[:, 1:NT], dlt[:, 1:NT], dlt[:, 0:NT - 1], ALU.subtract))
                for g in range(IG):
                    i = ii[:, g:g + 1]
                    chain(v.tensor_scalar(jk[:, 0:NT], pre[:, :], i, 0.0, ALU.is_le, ALU.add,
                                          accum_out=it[:, 1, g:g + 1]))
                    chain(v.scalar_tensor_tensor(out=jk[:, 0:NT], in0=pre[:, :], scalar=i, in1=dd[:, :],
                                                 op0=ALU.is_le, op1=ALU.mult, accum_out=it[:, 0, g:g + 1]))
                    chain(v.tensor_scalar(jk[:, 0:NT], pre[:, :], i, 0.0, ALU.is_equal, ALU.add,
                                          accum_out=it[:, 2, g:g + 1]))
                    chain(v.tensor_scalar(jk[:, 0:NT], pre[:, :], i1[:, g:g + 1], 0.0, ALU.is_equal, ALU.add,
                                          accum_out=it[:, 3, g:g + 1]))
                chain(v.tensor_tensor(it[:, 0, :], it[:, 0, :], ii[:, :], ALU.add))
                chain(v.tensor_scalar(it[:, 0, :], it[:, 0, :], float(CH - 1), None, ALU.min))
                chain(v.tensor_scalar(it[:, 1, :], it[:, 1, :], 1.0, None, ALU.subtract))
                v.sem_inc(its, 1)
                v.wait_ge(itt, 1)
                v.tensor_copy(itT[:, :, :], psi[:, :, :]).then_inc(itc, 1)
                v.wait_ge(back, 48)
                chain(v.tensor_scalar(env["item_keep"][:, :], krow[:, :], -1.0, 1.0, ALU.mult, ALU.add))
                chain(v.tensor_scalar(rrow[0:1, 0, :], rrow[0:1, 0, :], float(RT), None, ALU.subtract))
                chain(v.tensor_tensor(rrow[0:1, 0, :], rrow[0:1, 0, :], rrow[0:1, 1, :], ALU.mult))
                chain(v.tensor_scalar(rrow[0:1, 0, :], rrow[0:1, 0, :], float(RT), None, ALU.add))
                chain(v.tensor_copy(env["item_row"][0:1, :], rrow[0:1, 0, :]))

            @block.tensor
            def _(pe):
                pe.wait_ge(cs, 1)
                pe.wait_ge(cst, 6)
                pe.matmul(psb[:, :], ones[:, :], cnt[:, :], start=True, stop=True).then_inc(bs, 1)
                pe.wait_ge(its, 1)
                pe.wait_ge(pl, 2)
                for k in range(4):
                    last = pe.transpose(psi[:, k, :], it[:, k, :], ident[:, :])
                last.then_inc(itt, 1)


def scan_view(d):
    return d.rearrange("c e -> (c e)").rearrange("(p f) -> p f", f=CH)


def scan_buffers(env, ph):
    big = env["Hh"][:, :, :].rearrange("p t d -> p (t d)")
    b = dict(ident=env["ident"], n=0, stage=0, pe_stage=0)
    b["val"] = big[:, 0:H * CH].rearrange("p (c f) -> p c f", f=CH)
    b["run"] = big[:, H * CH:2 * H * CH].rearrange("p (c f) -> p c f", f=CH)
    for k in range(7):
        b[f"x{k}"] = big[:, (2 * H + k) * CH:(2 * H + k + 1) * CH]
    for n in ("st", "nst", "nen", "en"):
        b[n] = ph.sb(n, [P, CH])
    b["tot"] = ph.sb("tot", [P, 2 * H])
    b["totT"] = ph.sb("totT", [H, 2, P])
    b["car"] = ph.sb("car", [H, P + 1])
    b["carT"] = ph.sb("carT", [P, H])
    b["psT"] = ph.ps("psT", [H, 2, P])
    b["psC"] = ph.ps("psC", [P, H])
    for n in ("dve", "tot_ready", "totT_ready", "car_ready", "carT_ready", "shifted_in", "filled"):
        b[n] = ph.sem(n)
    return b


def scan_flags(env, b):
    nc = env["nc"]
    dst = env["dst_d"].rearrange("c e -> (c e)")
    cur, prv, nxt = b["x0"], b["x1"], b["x2"]
    ld, fl = b["shifted_in"], b["filled"]
    with nc.Block() as block:
        @block.sync
        def _(sp):
            sp.wait_ge(fl, 2)
            sp.dma_start(cur, dst.rearrange("(p f) -> p f", f=CH)).then_inc(ld, 16)
            sp.dma_start(prv[0:1, 1:CH], dst[0:CH - 1].rearrange("(a f) -> a f", a=1)).then_inc(ld, 16)
            sp.dma_start(prv[1:P, :], dst[CH - 1:EP - 1].rearrange("(p f) -> p f", f=CH)).then_inc(ld, 16)
            sp.dma_start(nxt[0:P - 1, :], dst[1:EP - CH + 1].rearrange("(p f) -> p f", f=CH)).then_inc(ld, 16)
            sp.dma_start(nxt[P - 1:P, 0:CH - 1], dst[EP - CH + 1:EP].rearrange("(a f) -> a f", a=1)).then_inc(ld, 16)
            sp.wait_ge(ld, 80)

        @block.vector
        def _(v):
            chain = Chain(v, b["dve"])
            v.memset(prv, -1.0).then_inc(fl, 1)
            v.memset(nxt, -1.0).then_inc(fl, 1)
            v.wait_ge(ld, 80)
            chain(v.tensor_tensor(b["nst"][:, :], cur, prv, ALU.is_equal))
            chain(v.tensor_tensor(b["nen"][:, :], cur, nxt, ALU.is_equal))
            chain(v.tensor_scalar(b["st"][:, :], b["nst"][:, :], BIG, -BIG, ALU.mult, ALU.add))
            chain(v.tensor_scalar(b["en"][:, :], b["nen"][:, :], -1.0, 1.0, ALU.mult, ALU.add))
            b["n"] = chain.n


def seg_weights(env):
    nc = env["nc"]
    with Phase(nc, "sw") as ph:
        b = scan_buffers(env, ph)
        tf, eq, wsum, sf = b["x3"], b["x4"], b["x5"], b["x6"]
        loaded, put, fin = ph.sem("loaded"), ph.sem("put"), ph.sem("weights")
        scan_flags(env, b)
        with nc.Block() as block:
            @block.vector
            def _(v):
                chain = Chain(v, b["dve"], b["n"])
                v.wait_ge(loaded, 32)
                chain(v.scalar_tensor_tensor(out=tf, in0=sf, scalar=-float(R), in1=tf, op0=ALU.mult, op1=ALU.add))
                chain(v.memset(wsum, 0.0))
                for half in range(R // H):
                    for r in range(H):
                        chain(v.tensor_scalar(b["val"][:, r, :], tf, float(H * half + r), None, ALU.is_equal))
                    seg_forward(v, chain, b, H, ALU.mult, b["nst"], ALU.add, 0.0)
                    seg_backward(v, chain, b, H)
                    for r in range(H):
                        chain(v.scalar_tensor_tensor(out=eq, in0=tf, scalar=float(H * half + r),
                                                     in1=b["val"][:, r, :], op0=ALU.is_equal, op1=ALU.mult))
                        chain(v.tensor_tensor(wsum, wsum, eq, ALU.add))
                chain(v.tensor_scalar(wsum, wsum, 1.0, None, ALU.max))
                v.reciprocal(eq, wsum).then_inc(fin, 1)

            @block.tensor
            def _(pe):
                for _ in range(2 * R // H):
                    seg_carry(pe, b, H)

            @block.sync
            def _(sp):
                sp.dma_start(tf, scan_view(env["rel_d"])).then_inc(loaded, 16)
                sp.dma_start(sf, scan_view(env["src_d"])).then_inc(loaded, 16)
                sp.wait_ge(fin, 1)
                sp.dma_start(scan_view(env["wgt_d"]), eq).then_inc(put, 16)
                sp.wait_ge(put, 16)


def seg_carry(pe, b, ch):
    k = b["pe_stage"] = b["pe_stage"] + 1
    pe.wait_ge(b["tot_ready"], k)
    pe.transpose(b["psT"][:, 0, :], b["tot"][:, 0:ch], b["ident"][:, :])
    pe.transpose(b["psT"][:, 1, :], b["tot"][:, ch:2 * ch], b["ident"][:, :]).then_inc(b["totT_ready"], 1)
    pe.wait_ge(b["car_ready"], k)
    lo = 0 if k % 2 else 1
    pe.transpose(b["psC"][:, :], b["car"][:, lo:lo + P], b["ident"][0:ch, 0:ch]).then_inc(b["carT_ready"], 1)


def seg_forward(v, chain, b, ch, op0, reset, op1, init):
    k = b["stage"] = b["stage"] + 1
    val, run, tot = b["val"], b["run"], b["tot"]
    for c in range(ch):
        chain(v.tensor_tensor_scan(run[:, c, :], reset[:, :], val[:, c, :], init, op0, op1))
    chain(v.tensor_copy(tot[:, 0:ch], run[:, :, CH - 1]))
    chain(v.tensor_reduce(tot[:, ch:ch + 1], reset[:, :], AX.X, ALU.min))
    for c in range(1, ch):
        chain(v.tensor_copy(tot[:, ch + c:ch + c + 1], tot[:, ch:ch + 1]))
    v.sem_inc(b["tot_ready"], 1)
    v.wait_ge(b["totT_ready"], k)
    chain(v.tensor_copy(b["totT"][:, :, :], b["psT"][:, :, :]))
    chain(v.memset(b["car"][:, :], init))
    chain(v.tensor_tensor_scan(b["car"][:, 1:P + 1], b["totT"][:, 1, :], b["totT"][:, 0, :], init, op0, op1))
    v.sem_inc(b["car_ready"], 1)
    v.wait_ge(b["carT_ready"], k)
    chain(v.tensor_copy(b["carT"][:, :], b["psC"][:, :]))
    for c in range(ch):
        chain(v.tensor_tensor_scan(run[:, c, :], reset[:, :], val[:, c, :], b["carT"][:, c:c + 1], op0, op1))


def seg_backward(v, chain, b, ch):
    k = b["stage"] = b["stage"] + 1
    val, run, tot = b["val"], b["run"], b["tot"]
    for c in range(ch):
        chain(v.tensor_tensor(run[:, c, :], run[:, c, :], b["en"][:, :], ALU.mult))
    for c in range(ch):
        chain(v.tensor_tensor_scan(val[:, c, ::-1], b["nen"][:, ::-1], run[:, c, ::-1], 0.0, ALU.mult, ALU.add))
    chain(v.tensor_copy(tot[:, 0:ch], val[:, :, 0]))
    chain(v.tensor_reduce(tot[:, ch:ch + 1], b["nen"][:, :], AX.X, ALU.min))
    for c in range(1, ch):
        chain(v.tensor_copy(tot[:, ch + c:ch + c + 1], tot[:, ch:ch + 1]))
    v.sem_inc(b["tot_ready"], 1)
    v.wait_ge(b["totT_ready"], k)
    chain(v.tensor_copy(b["totT"][:, :, :], b["psT"][:, :, :]))
    chain(v.memset(b["car"][:, :], 0.0))
    chain(v.tensor_tensor_scan(b["car"][:, P - 1::-1], b["totT"][:, 1, ::-1], b["totT"][:, 0, ::-1], 0.0,
                               ALU.mult, ALU.add))
    v.sem_inc(b["car_ready"], 1)
    v.wait_ge(b["carT_ready"], k)
    chain(v.tensor_copy(b["carT"][:, :], b["psC"][:, :]))
    for c in range(ch):
        chain(v.tensor_tensor_scan(val[:, c, ::-1], b["nen"][:, ::-1], run[:, c, ::-1], b["carT"][:, c:c + 1],
                                   ALU.mult, ALU.add))


def items(env):
    nc = env["nc"]
    with Phase(nc, "it") as ph:
        cf, tl, ci = ph.sb("cf", [P, IG]), ph.sb("tl", [P, IG]), env["item_chunk"]
        rows = ph.sb("rows", [P, IG, 4, P])
        ok, tmp = ph.sb("ok", [P, P]), ph.sb("tmp", [P, P])
        pt = ph.ps("pt", [P, 4, P])
        got, idx, gat, dv, tr, cp, rd = (ph.sem(n) for n in ("got", "idx", "gathered", "dve", "tr", "cp", "rd"))
        with nc.Block() as block:
            @block.sync
            def _(sp):
                sp.dma_start(cf[:, :], env["item_d"][0, :].rearrange("(g p) -> p g", p=P),
                             allow_slow_non_contiguous=True).then_inc(got, 16)
                sp.dma_start(tl[:, :], env["item_d"][1, :].rearrange("(g p) -> p g", p=P),
                             allow_slow_non_contiguous=True).then_inc(got, 16)
                sp.wait_ge(got, 32)

            @block.gpsimd
            def _(pool):
                pool.wait_ge(idx, 1)
                for g in range(IG):
                    for k, d in enumerate(("dst_d", "src_d", "rel_d", "wgt_d")):
                        pool.indirect_dma_start(out=rows[:, g, k, :], out_offset=None, in_=env[d][:, :],
                                                in_offset=bass.IndirectOffsetOnAxis(ap=ci[:, g:g + 1], axis=0))\
                            .then_inc(gat, 16)
                pool.wait_ge(gat, 16 * 4 * IG)

            @block.vector
            def _(v):
                chain = Chain(v, dv)
                v.wait_ge(got, 32)
                v.tensor_copy(ci[:, :], cf[:, :]).then_inc(idx, 1)
                chain(v.tensor_scalar(tl[:, :], tl[:, :], float(P), None, ALU.mult))
                v.wait_ge(gat, 16 * 4 * IG)
                for g in range(IG):
                    dl = rows[:, g, 0, :]
                    chain(v.tensor_scalar(dl, dl, tl[:, g:g + 1], None, ALU.subtract))
                    chain(v.tensor_scalar(tmp[:, :], dl, 0.0, None, ALU.is_ge))
                    chain(v.scalar_tensor_tensor(out=ok[:, :], in0=dl, scalar=float(P), in1=tmp[:, :],
                                                 op0=ALU.is_lt, op1=ALU.mult))
                    for k in (1, 2):
                        x = rows[:, g, k, :]
                        chain(v.scalar_tensor_tensor(out=x, in0=x, scalar=-OOB, in1=ok[:, :],
                                                     op0=ALU.add, op1=ALU.mult))
                        chain(v.tensor_scalar(x, x, OOB, None, ALU.add))
                    v.sem_inc(rd, 1)
                    v.wait_ge(tr, g + 1)
                    s = slice(g * P, (g + 1) * P)
                    chain(v.tensor_copy(env["item_dst"][:, s], pt[:, 0, :]))
                    chain(v.tensor_copy(env["item_src"][:, s], pt[:, 1, :]))
                    chain(v.tensor_copy(env["item_rel"][:, s], pt[:, 2, :]))
                    v.tensor_copy(env["item_wgt"][:, s], pt[:, 3, :]).then_inc(cp, 1)
                v.wait_ge(cp, IG)

            @block.tensor
            def _(pe):
                for g in range(IG):
                    pe.wait_ge(rd, g + 1)
                    wait(pe, cp, g)
                    for k in range(4):
                        last = pe.transpose(pt[:, k, :], rows[:, g, k, :], env["ident"][:, :])
                    last.then_inc(tr, 1)


def last_edges(env):
    nc, A = env["nc"], env["A"]
    with Phase(nc, "le") as ph:
        rw = ph.sb("rw", [P, LG, LC], I32)
        rf = ph.sb("rf", [P, LG, LC])
        ci = ph.sb("ci", [LC, LG * P], I32)
        chi, clo = ph.sb("chi", [LC, LG * P]), ph.sb("clo", [LC, LG * P])
        tmpi = ph.sb("tmpi", [LC, LG * P], I32)
        pw_i = ph.sb("pw_i", [LC, 1], I32)
        ohh = ph.sb("ohh", [LC, 2, LU, NHI], BF16)
        ohl = ph.sb("ohl", [LC, 2, LU, NLO], BF16)
        vi = ph.sb("vi", [NHI, 2, LU, NLO], I32)
        m1, key = ph.sb("m1", [NHI, LU, NLO]), ph.sb("key", [NHI, LU, NLO])
        cadd = ph.sb("cadd", [NHI, LU, NLO])
        red = ph.sb("red", [NHI, NLO])
        T, T1 = ph.sb("T", [NHI, NLO]), ph.sb("T1", [NHI, NLO])
        pt = ph.ps("pt", [LC, P])
        pp = [ph.ps(f"pp{i}", [NHI, LU, NLO]) for i in range(2)]
        ld, cst, tr, cp, dv, rd, oh, mm, sh, lp, fin, put, cv = (
            ph.sem(n) for n in ("ld", "const", "tr", "cp", "dve", "rd", "onehots", "sums", "shifted", "loop", "fin",
                                "put", "conv"))
        with nc.Block() as block:
            @block.gpsimd
            def _(pool):
                pool.iota(pw_i[:, :], pattern=[[0, 1]], base=3, channel_multiplier=2).then_inc(cst, 1)
                pool.iota(cadd[:, :, :], pattern=[[LC, LU], [0, NLO]], base=0, channel_multiplier=0,
                          allow_small_or_imprecise_dtypes=True).then_inc(cst, 1)
                pool.wait_ge(cst, 2)

            @block.sync
            def _(sp):
                sp.wait_ge(rd, 1)
                full = (LG - 1) * P
                sp.dma_start(rw[:, 0:LG - 1, :], A["src"][0:full * LC].rearrange("(g p f) -> p g f", p=P, f=LC))\
                    .then_inc(ld, 16)
                sp.dma_start(rw[0:LCH - full, LG - 1, :], A["src"][full * LC:E].rearrange("(p f) -> p f", f=LC))\
                    .then_inc(ld, 16)
                sp.wait_ge(fin, 1)
                sp.dma_start(env["last_d"].rearrange("(h l) -> h l", l=NLO), T[:, :]).then_inc(put, 16)
                sp.wait_ge(put, 16)

            @block.vector
            def _(v):
                chain = Chain(v, dv)
                v.memset(rw[:, LG - 1, :], 12287).then_inc(rd, 1)
                v.wait_ge(ld, 32)
                v.tensor_copy(rf[:, :, :], rw[:, :, :]).then_inc(cv, 1)
                for g in range(LG):
                    v.wait_ge(tr, g + 1)
                    v.tensor_copy(ci[:, g * P:(g + 1) * P], pt[:, :]).then_inc(cp, 1)
                v.wait_ge(cp, LG)
                chain(v.tensor_scalar(tmpi[:, :], ci[:, :], 6, None, ALU.arith_shift_right))
                chain(v.tensor_copy(chi[:, :], tmpi[:, :]))
                chain(v.tensor_scalar(tmpi[:, :], ci[:, :], NLO - 1, None, ALU.bitwise_and))
                chain(v.tensor_copy(clo[:, :], tmpi[:, :]))
                v.wait_ge(cst, 2)
                chain(v.tensor_scalar(pw_i[:, :], pw_i[:, :], 23, None, ALU.logical_shift_left))
                chain(v.memset(T[:, :], 0.0))
                pw = pw_i[:, 0:1].bitcast(FP32)

                def onehots(j, b, lag):
                    wait(v, mm, lag)
                    v.tensor_tensor(ohh[:, b, :, :], env["iota"][0:LC, 0:NHI].unsqueeze(1).to_broadcast([LC, LU, NHI]),
                                    chi[:, bass.ds(j * LU, LU)].unsqueeze(2).to_broadcast([LC, LU, NHI]),
                                    ALU.is_equal).then_inc(oh, 1)
                    for k in range(LU):
                        ins = v.tensor_scalar(ohl[:, b, k, :], env["iota"][0:LC, 0:NLO],
                                              clo[:, bass.ds(j * LU + k, 1)], pw, ALU.is_equal, ALU.mult)
                        ins.then_inc(oh, 1)

                def merge(j, b, c):
                    v.wait_ge(mm, j + 1)
                    c(v.tensor_scalar(vi[:, b, :, :], pp[b][:, :, :].bitcast(I32), 24, None,
                                      ALU.logical_shift_right))
                    c(v.scalar_tensor_tensor(out=m1[:, :, :].rearrange("h a b -> h (a b)"),
                                             in0=vi[:, b, :, :].rearrange("h a b -> h (a b)"), scalar=0.0,
                                             in1=cadd[:, :, :].rearrange("h a b -> h (a b)"),
                                             op0=ALU.is_gt, op1=ALU.mult))
                    c(v.tensor_tensor(key[:, :, :], m1[:, :, :], vi[:, b, :, :], ALU.add))
                    c(v.tensor_reduce(red[:, :], key[:, :, :].rearrange("h a b -> h b a"), AX.X, ALU.max))
                    c(v.tensor_scalar(T1[:, :], T[:, :], float(LC * LU), None, ALU.subtract))
                    c(v.tensor_scalar(m1[:, 0, :], red[:, :], 0.0, None, ALU.is_equal))
                    c(v.tensor_tensor(T1[:, :], T1[:, :], m1[:, 0, :], ALU.mult))
                    c(v.tensor_tensor(T[:, :], T1[:, :], red[:, :], ALU.add))

                NM = 8
                onehots(0, 0, 0)
                onehots(1, 1, 0)
                cc = Chain(v, lp)
                merge(0, 0, cc)
                assert cc.n == NM
                with v.Fori(1, (LB + 1) // 2) as i:
                    c = Chain(v, lp, NM * (2 * i - 1))
                    onehots(2 * i, 0, 2 * i - 1)
                    merge(2 * i - 1, 1, c)
                    onehots(2 * i + 1, 1, 2 * i)
                    merge(2 * i, 0, c)
                c = Chain(v, lp, NM * LB)
                merge(LB, 1, c)
                c(v.tensor_scalar(T[:, :], T[:, :], float(LC * LU * LB), 0.0, ALU.add, ALU.max))
                v.sem_inc(fin, 1)

            @block.tensor
            def _(pe):
                pe.wait_ge(cv, 1)
                for g in range(LG):
                    wait(pe, cp, g)
                    pe.transpose(pt[:, :], rf[:, g, :], env["ident"][:, :]).then_inc(tr, 1)

                def sums(j, b):
                    pe.wait_ge(oh, (LU + 1) * (j + 1))
                    wait(pe, lp, 8 * j - 15)
                    for k in range(LU):
                        last = pe.matmul(pp[b][:, k, :], ohh[:, b, k, :], ohl[:, b, k, :], start=True, stop=True)
                    last.then_inc(mm, 1)

                sums(0, 0)
                sums(1, 1)
                with pe.Fori(1, (LB + 1) // 2) as i:
                    sums(2 * i, 0)
                    sums(2 * i + 1, 1)


def load_rows(ph, nc, sp, sem, pairs):
    for t, a in pairs:
        sp.dma_start(t, a.rearrange("(a n) -> a n", a=1).partition_broadcast(P)).then_inc(sem, 16)


def norm_phase(env, name, to_dram=None):
    nc, X, Hh = env["nc"], env["X"], env["Hh"]
    with Phase(nc, name) as ph:
        stats = ph.sb("stats", [P, 2, 6])
        mv, mv1 = ph.sb("mv", [P, NT, 2]), ph.sb("mv1", [P, 2, 2])
        turn = ph.sem("turn")
        std, rstd, nmr = ph.sb("std", [P, NT]), ph.sb("rstd", [P, NT]), ph.sb("nmr", [P, NT])
        dv, sq, rs, hn, put, st = (ph.sem(n) for n in ("link", "roots", "scales", "rows_done", "put", "stats"))
        with nc.Block() as block:
            @block.vector
            def _(v):
                with v.Fori(0, NT // 2) as j:
                    for u in range(2):
                        t = 2 * j + u
                        c = Chain(v, dv, 3 * t)
                        v.sem_inc(turn, 1)
                        c(v.bn_stats(stats[:, u, :], tile_of(X, t)))
                        v.sem_inc(turn, 1)
                        c(v.bn_aggr(mv1[:, u, :], stats[:, u, :]))
                        c(v.tensor_copy(tile_of(mv, t), mv1[:, u, :]))
                v.sem_inc(st, 1)
                v.wait_ge(sq, 1)
                c = Chain(v, dv, 3 * NT)
                c(v.reciprocal(rstd[:, :], std[:, :]))
                c(v.tensor_tensor(nmr[:, :], mv[:, :, 0], rstd[:, :], ALU.mult))
                c(v.tensor_scalar(nmr[:, :], nmr[:, :], -1.0, None, ALU.mult))
                v.sem_inc(rs, 1)

            @block.scalar
            def _(act):
                act.wait_ge(st, 1)
                act.activation(std[:, :], mv[:, :, 1], ACT.Sqrt, bias=env["eps_c"][:, 0:1]).then_inc(sq, 1)
                act.wait_ge(rs, 1)
                with act.Fori(0, NT) as t:
                    act.activation(tile_of(Hh, t), tile_of(X, t), ACT.Relu,
                                   bias=nmr[:, bass.ds(t, 1)], scale=rstd[:, bass.ds(t, 1)]).then_inc(hn, 1)

            if to_dram is not None:
                @block.sync
                def _(sp):
                    for c in range(0, NT, 10):
                        sp.wait_ge(hn, c + 10)
                        sp.dma_start(to_dram[c * P:(c + 10) * P, :].rearrange("(t p) d -> p t d", p=P),
                                     Hh[:, c:c + 10, :]).then_inc(put, 16)
                    sp.wait_ge(put, 80)


def tile_of(a, t):
    return a[:, bass.ds(t, 1), :].rearrange("p a d -> p (a d)")


def flat(ap):
    return ap.rearrange("p k q -> p (k q)")


def load_rows(sp, sem, pairs):
    for t, a in pairs:
        sp.dma_start(t, a.rearrange("(a n) -> a n", a=1).partition_broadcast(P)).then_inc(sem, 16)


class Dense:

    def __init__(self, env, name, width, kt=2):
        self.env, self.nc, self.kt, self.width = env, env["nc"], kt, width
        self.ph = ph = Phase(env["nc"], name)
        self.rows = ph.sb("rows", [P, 2, kt, P])
        self.rowsT = ph.sb("rowsT", [P, 2, kt, P])
        self.psT = [ph.ps(f"psT{i}", [P, kt, P]) for i in range(2)]
        self.psO = [ph.ps(f"psO{i}", [P, width]) for i in range(2)]
        self.rows_ready, self.transposed, self.copied, self.products, self.taken, self.mid_done, self.link = (
            ph.sem(n) for n in ("rows_ready", "transposed", "copied", "products", "taken", "mid_done", "link"))

    def pe(self, pe, weights):
        ident = self.env["ident"]

        def body(j):
            for u in range(2):
                t = 2 * j + u
                pe.wait_ge(self.rows_ready, t + 1)
                wait(pe, self.copied, t - 1)
                for k in range(self.kt):
                    last = pe.transpose(self.psT[u][:, k, :], self.rows[:, u, k, :], ident[:, :])
                last.then_inc(self.transposed, 1)
                pe.wait_ge(self.copied, t + 1)
                wait(pe, self.taken, t - 1)
                for s in range(0, self.width, 512):
                    e = min(s + 512, self.width)
                    for k in range(self.kt):
                        last = pe.matmul(self.psO[u][:, s:e], self.rowsT[:, u, k, :], weights(k)[:, s:e],
                                         start=(k == 0), stop=(k == self.kt - 1))
                last.then_inc(self.products, 1)
        body(0)
        with pe.Fori(1, NT // 2) as j:
            body(j)

    def act(self, act, mid=None):
        def do_mid(t, u):
            act.wait_ge(self.taken, t + 1)
            mid(t, u).then_inc(self.mid_done, 1)

        def body(j):
            for u in range(2):
                t = 2 * j + u
                act.wait_ge(self.transposed, t + 1)
                wait(act, self.products, t - 1)
                act.copy(self.rowsT[:, u, :, :], self.psT[u][:, :, :]).then_inc(self.copied, 1)
                if mid and not (isinstance(t, int) and t == 0):
                    do_mid(t - 1, 1 - u)
        body(0)
        with act.Fori(1, NT // 2) as j:
            body(j)
        if mid:
            do_mid(NT - 1, 1)

    def dve(self, v, pre, post, npre, npost, end=None, nend=0):
        n = npre + npost + nend

        def do_pre(t, u, h, base):
            wait(v, self.transposed, t - 1)
            c = Chain(v, self.link, base)
            pre(t, u, h, c).then_inc(self.rows_ready, 1)
            assert c.n == npre, (c.n, npre)

        def do_post(t, u, h, base):
            v.wait_ge(self.products, t + 1)
            c = Chain(v, self.link, base)
            post(t, u, h, c).then_inc(self.taken, 1)
            assert c.n == npost, (c.n, npost)

        def do_end(t, u, h, base):
            v.wait_ge(self.mid_done, t + 1)
            c = Chain(v, self.link, base)
            end(t, u, h, c)
            assert c.n == nend, (c.n, nend)

        def step(t, u, h, h1, pre_too=True):
            base = npre + n * t - (nend if end else 0)
            if isinstance(t, int) and t == 0:
                base = npre
            if pre_too:
                do_pre(t + 1, 1 - u, h1, base)
                base = base + npre
            do_post(t, u, h, base)
            if end and not (isinstance(t, int) and t == 0):
                do_end(t - 1, 1 - u, h if u else h - 1, base + npost)

        do_pre(0, 0, 0, 0)

        def body(j):
            step(2 * j, 0, j, j)
            step(2 * j + 1, 1, j, j + 1)
        body(0)
        with v.Fori(1, NT // 2 - 1) as j:
            body(j)
        step(NT - 2, 0, NT // 2 - 1, NT // 2 - 1)
        step(NT - 1, 1, NT // 2 - 1, 0, pre_too=False)
        if end:
            do_end(NT - 1, 1, NT // 2 - 1, n * NT - nend)


def tile_loads(d, sp, slots, sems, source):
    def body(j):
        for u in range(2):
            t = 2 * j + u
            wait(sp, d.taken, t - 1)
            sp.dma_start(slots[:, u, :], source[bass.ds(t * P, P), :]).then_inc(sems[u], 16)
    body(0)
    with sp.Fori(1, NT // 2) as j:
        body(j)


def tile_stores(d, sp, parts):
    with sp.Fori(0, NT // 2) as j:
        for u in range(2):
            t = 2 * j + u
            sp.wait_ge(d.taken, t + 1)
            for slots, sems, target in parts:
                sp.dma_start(target(t), slots[:, u, :]).then_inc(sems[u], 16)
    for _, sems, _ in parts:
        for s in sems:
            sp.wait_ge(s, 16 * NT // 2)


def layer0(env):
    nc, A, X, Hh = env["nc"], env["A"], env["X"], env["Hh"]
    norm_phase(env, "n0", env["h_d"])
    d = Dense(env, "l0", D, kt=4)
    with d.ph as ph:
        wn = ph.sb("wn", [P, 2, 4, P])
        wT = ph.sb("wT", [P, 4, D])
        bias = ph.sb("bias", [P, D])
        lastn = ph.sb("lastn", [P, NT])
        tmp = ph.sb("tmp", [P, NT])
        eidx = ph.sb("eidx", [P, NT], I32)
        nidx = ph.sb("nidx", [P, NT], I32)
        nring = ph.sb("nring", [P, 2], I32)
        ag = ph.sb("ag", [P, 2, D])
        res = ph.sb("res", [P, 2, D])
        pw = ph.ps("pw", [P, 4, P])
        ld, dv, ei, ng, wt, wc, z, nr, go = (ph.sem(n) for n in (
            "loaded", "dve", "edge_index", "node_index", "w_transposed", "w_copied", "zeroed", "ring", "go"))
        gs = [ph.sem(f"gathered{i}") for i in range(2)]
        with nc.Block() as block:
            @block.sync
            def _(sp):
                for a in range(2):
                    sp.dma_start(wn[:, a, :, :], A["L0_gnn_W"][a * P:(a + 1) * P, :].rearrange("p (k q) -> p k q", q=P))\
                        .then_inc(ld, 16)
                load_rows(sp, ld, [(bias[:, :], A["L0_gnn_b"])])
                sp.wait_ge(z, 2)
                with nc.allow_non_contiguous_dma("one value per node"):
                    sp.dma_start(lastn[:, 0:RT], env["last_d"].rearrange("(t p) -> p t", p=P)).then_inc(ld, 16)
                sp.wait_ge(ld, 64)

            @block.vector
            def _(v):
                chain = Chain(v, dv)
                v.memset(lastn[:, :], 0.0).then_inc(z, 1)
                v.memset(nidx[:, :], int(OOB)).then_inc(z, 1)
                v.wait_ge(ld, 64)
                chain(v.tensor_scalar(tmp[:, :], lastn[:, :], 0.0, 200001.0, ALU.is_equal, ALU.mult))
                chain(v.scalar_tensor_tensor(out=lastn[:, :], in0=lastn[:, :], scalar=-1.0, in1=tmp[:, :],
                                             op0=ALU.add, op1=ALU.add))
                v.tensor_copy(eidx[:, :], lastn[:, :]).then_inc(ei, 1)
                for a in range(2):
                    v.wait_ge(wt, a + 1)
                    v.tensor_copy(wT[:, :, a * P:(a + 1) * P], pw[:, :, :]).then_inc(wc, 1)

                def pre(t, u, h, c):
                    c(v.tensor_copy(flat(d.rows[:, u, 0:2, :]), tile_of(Hh, t)))
                    v.wait_ge(gs[u], 16 * (h + 1))
                    return v.tensor_copy(flat(d.rows[:, u, 2:4, :]), ag[:, u, :])

                def post(t, u, h, c):
                    c(v.tensor_tensor(res[:, u, :], d.psO[u][:, :], bias[:, :], ALU.add))
                    return v.tensor_tensor(tile_of(X, t), tile_of(X, t), res[:, u, :], ALU.add)
                d.dve(v, pre, post, 1, 1)

            @block.tensor
            def _(pe):
                pe.wait_ge(ld, 64)
                for a in range(2):
                    wait(pe, wc, a)
                    for k in range(4):
                        last = pe.transpose(pw[:, k, :], wn[:, a, k, :], env["ident"][:, :])
                    last.then_inc(wt, 1)
                pe.wait_ge(wc, 2)
                d.pe(pe, lambda k: wT[:, k, :])

            @block.scalar
            def _(act):
                d.act(act)

            @block.gpsimd
            def _(pool):
                lim_e = pool.to_reg(E - 1)
                lim_n = pool.to_reg(N - 1)
                pool.wait_ge(z, 2)
                pool.wait_ge(ei, 1)
                for t in range(NT):
                    pool.indirect_dma_start(out=nidx[:, t:t + 1], out_offset=None,
                                            in_=A["dst"].rearrange("(e a) -> e a", a=1),
                                            in_offset=bass.IndirectOffsetOnAxis(ap=eidx[:, t:t + 1], axis=0),
                                            bounds_check=lim_e, oob_is_err=False).then_inc(ng, 16)
                pool.wait_ge(ng, 16 * NT)

                def body(j):
                    for u in range(2):
                        t = 2 * j + u
                        wait(pool, d.rows_ready, t - 1)
                        pool.sem_inc(go, 1)
                        pool.memset(ag[:, u, :], 0.0).then_inc(nr, 1)
                        pool.tensor_copy(nring[:, u:u + 1], nidx[:, bass.ds(t, 1)]).then_inc(nr, 1)
                        pool.wait_ge(nr, 2 * t + 2)
                        pool.sem_inc(go, 1)
                        pool.indirect_dma_start(out=ag[:, u, :], out_offset=None, in_=env["h_d"][:, :],
                                                in_offset=bass.IndirectOffsetOnAxis(ap=nring[:, u:u + 1], axis=0),
                                                bounds_check=lim_n, oob_is_err=False).then_inc(gs[u], 16)
                body(0)
                with pool.Fori(1, NT // 2) as j:
                    body(j)


def copy_rows(v, d, a):
    def pre(t, u, h, c):
        return v.tensor_copy(flat(d.rows[:, u, :, :]), tile_of(a, t))
    return pre


def layer1_tables(env):
    nc, A, X, Hh = env["nc"], env["A"], env["X"], env["Hh"]
    norm_phase(env, "n1")
    for half in range(2):
        q = R // 2
        d = Dense(env, f"t1{half}", q * D)
        with d.ph as ph:
            w = ph.sb("w", [P, 2, q * D])
            o = ph.sb("o", [P, 2, q * D])
            ld = ph.sem("loaded")
            st = [ph.sem(f"stored{i}") for i in range(2)]
            view = env["rel_t"].rearrange("(n r) d -> n (r d)", r=R)[:, half * q * D:(half + 1) * q * D]
            with nc.Block() as block:
                @block.sync
                def _(sp):
                    for r in range(q):
                        sp.dma_start(w[:, :, r * D:(r + 1) * D],
                                     A["L1_gnn_W_rel"][half * q + r, :, :].rearrange("(k p) o -> p k o", p=P)).then_inc(ld, 16)
                    sp.wait_ge(ld, 16 * q)
                    tile_stores(d, sp, [(o, st, lambda t: view[bass.ds(t * P, P), :])])

                @block.vector
                def _(v):
                    def post(t, u, h, c):
                        wait(v, st[u], 16 * h)
                        return v.tensor_copy(o[:, u, :], d.psO[u][:, :])
                    d.dve(v, copy_rows(v, d, Hh), post, 0, 0)

                @block.tensor
                def _(pe):
                    pe.wait_ge(ld, 16 * q)
                    d.pe(pe, lambda k: w[:, k, :])

                @block.scalar
                def _(act):
                    d.act(act)


def layer1_end(env):
    nc, A, X, Hh = env["nc"], env["A"], env["X"], env["Hh"]
    d = Dense(env, "e1", D)
    with d.ph as ph:
        w = ph.sb("w", [P, 2, D])
        bias, gam, bet = ph.sb("bias", [P, D]), ph.sb("gam", [P, D]), ph.sb("bet", [P, D])
        ag = ph.sb("ag", [P, 2, D])
        cv, gl, y = ph.sb("cv", [P, 2, D]), ph.sb("gl", [P, 2, D]), ph.sb("y", [P, 2, D])
        stats = ph.sb("stats", [P, 2, 6])
        mv, mv1 = ph.sb("mv", [P, NT, 2]), ph.sb("mv1", [P, 2, 2])
        turn = ph.sem("turn")
        std, rstd, nmr = ph.sb("std", [P, NT]), ph.sb("rstd", [P, NT]), ph.sb("nmr", [P, NT])
        ld, dv, st, sq = ph.sem("loaded"), ph.sem("dve"), ph.sem("stats"), ph.sem("roots")
        got = [ph.sem(f"got{i}") for i in range(2)]
        with nc.Block() as block:
            @block.sync
            def _(sp):
                sp.dma_start(w[:, :, :], A["L1_gnn_W_root"].rearrange("(k p) o -> p k o", p=P)).then_inc(ld, 16)
                load_rows(sp, ld, [(bias[:, :], A["L1_gnn_bias"]), (gam[:, :], A["L1_gnn_ln_gamma"]),
                                   (bet[:, :], A["L1_gnn_ln_beta"])])
                tile_loads(d, sp, ag, got, env["agg_d"][0])

            @block.vector
            def _(v):
                v.wait_ge(ld, 64)

                def post(t, u, h, c):
                    v.wait_ge(got[u], 16 * (h + 1))
                    c(v.tensor_tensor(y[:, u, :], ag[:, u, :], bias[:, :], ALU.add))
                    return v.tensor_tensor(cv[:, u, :], d.psO[u][:, :], y[:, u, :], ALU.add)

                def end(t, u, h, c):
                    c(v.tensor_tensor(tile_of(Hh, t), tile_of(Hh, t), gl[:, u, :], ALU.add))
                    v.sem_inc(turn, 1)
                    c(v.bn_stats(stats[:, u, :], tile_of(Hh, t)))
                    v.sem_inc(turn, 1)
                    c(v.bn_aggr(mv1[:, u, :], stats[:, u, :]))
                    c(v.tensor_copy(tile_of(mv, t), mv1[:, u, :]))
                d.dve(v, copy_rows(v, d, Hh), post, 0, 1, end, 4)
                v.sem_inc(st, 1)
                v.wait_ge(sq, 1)
                c = Chain(v, dv)
                c(v.reciprocal(rstd[:, :], std[:, :]))
                with v.Fori(0, NT // 2) as j:
                    for u in range(2):
                        t = 2 * j + u
                        c = Chain(v, dv, 1 + 4 * t)
                        c(v.tensor_scalar(y[:, u, :], tile_of(Hh, t), mv[:, bass.ds(t, 1), 0], rstd[:, bass.ds(t, 1)],
                                          ALU.subtract, ALU.mult))
                        c(v.tensor_tensor(y[:, u, :], y[:, u, :], gam[:, :], ALU.mult))
                        c(v.tensor_tensor(y[:, u, :], y[:, u, :], bet[:, :], ALU.add))
                        c(v.tensor_tensor(tile_of(X, t), tile_of(X, t), y[:, u, :], ALU.add))

            @block.tensor
            def _(pe):
                pe.wait_ge(ld, 64)
                d.pe(pe, lambda k: w[:, k, :])

            @block.scalar
            def _(act):
                d.act(act, lambda t, u: act.activation(gl[:, u, :], cv[:, u, :], ACT.Gelu))
                act.wait_ge(st, 1)
                act.activation(std[:, :], mv[:, :, 1], ACT.Sqrt, bias=env["eps_c"][:, 0:1]).then_inc(sq, 1)


def layer2_tables(env):
    nc, A, X, Hh = env["nc"], env["A"], env["X"], env["Hh"]
    norm_phase(env, "n2")
    d = Dense(env, "t2", D)
    with d.ph as ph:
        w = ph.sb("w", [P, 2, D])
        att = ph.sb("att", [P, H, 2 * F])
        o = ph.sb("o", [P, 2, H * (F + 1)])
        a = ph.sb("a", [P, 2, 2 * H])
        pr = ph.sb("pr", [P, 2, 2, D])
        ld, ones = ph.sem("loaded"), ph.sem("ones")
        st = [ph.sem(f"stored{i}") for i in range(2)]
        sa = [ph.sem(f"stored_att{i}") for i in range(2)]
        heads = lambda ap, n=F: ap.rearrange("p (h f) -> p h f", f=n)
        with nc.Block() as block:
            @block.sync
            def _(sp):
                for h in range(H):
                    sp.dma_start(w[:, :, h * F:(h + 1) * F], A["L2_gnn_W"][h, :, :].rearrange("(k p) f -> p k f", p=P))\
                        .then_inc(ld, 16)
                sp.dma_start(att[:, :, :].rearrange("p h f -> p (h f)"),
                             A["L2_gnn_att"].rearrange("h f -> (h f)").rearrange("(a n) -> a n", a=1)
                             .partition_broadcast(P)).then_inc(ld, 16)
                sp.wait_ge(ld, 80)
                tile_stores(d, sp, [(o, st, lambda t: env["z_t"][bass.ds(t * P, P), :]),
                                    (a, sa, lambda t: env["att_t"][bass.ds(t * P, P), :])])

            @block.vector
            def _(v):
                v.memset(o[:, :, :], 1.0).then_inc(ones, 1)
                v.wait_ge(ones, 1)
                v.wait_ge(ld, 80)

                def post(t, u, h, c):
                    wait(v, st[u], 16 * h)
                    wait(v, sa[u], 16 * h)
                    z = heads(d.psO[u][:, :])
                    c(v.tensor_copy(heads(o[:, u, :], F + 1)[:, :, 0:F], z))
                    for k in range(2):
                        c(v.tensor_tensor(heads(pr[:, u, k, :]), z, att[:, :, k * F:(k + 1) * F], ALU.mult))
                        ins = v.tensor_reduce(a[:, u, k * H:(k + 1) * H], heads(pr[:, u, k, :]), AX.X, ALU.add)
                        if k == 0:
                            c(ins)
                    return ins
                d.dve(v, copy_rows(v, d, Hh), post, 0, 4)

            @block.tensor
            def _(pe):
                pe.wait_ge(ld, 80)
                d.pe(pe, lambda k: w[:, k, :])

            @block.scalar
            def _(act):
                d.act(act)


SB = 8
SBL = -(-CH // SB)


def edge_scores(env):
    nc, A = env["nc"], env["A"]
    with Phase(nc, "es") as ph:
        rows = ph.sb("rows", [P, 2, CG, P])
        cols = ph.sb("cols", [P, 2, CG * P], I32)
        ring = ph.sb("ring", [P, 2, 2, SB], I32)
        g = ph.sb("g", [P, 2, 2, SB, 2 * H])
        x = ph.sb("x", [P, SB, H])
        y = ph.sb("y", [P, SB, H])
        z = ph.sb("z", [P, SB, H])
        e = ph.sb("e", [P, 2, H, SB])
        eT = ph.sb("eT", [H * SB, 2, P])
        pt = ph.ps("pt", [P, 2, P])
        pe_ = [ph.ps(f"pe{i}", [H * SB, P]) for i in range(2)]
        fl, ld, tr, cp, gz, go, staged, lk, sc, trn, cpy, cl = (ph.sem(n) for n in (
            "filled", "loaded", "cols_t", "cols_c", "zeroed", "go", "staged", "link", "scores", "transposed", "copied",
            "clamped"))
        gs = [ph.sem(f"gathered{i}") for i in range(2)]
        st = [ph.sem(f"stored{i}") for i in range(2)]
        with nc.Block() as block:
            @block.sync
            def _(sp):
                sp.wait_ge(fl, 1)
                full = (CG - 1) * P
                for k, dd in enumerate(("src_d", "dst_d")):
                    sp.dma_start(rows[:, k, 0:CG - 1, :], env[dd][0:full, :].rearrange("(g p) e -> p g e", p=P)).then_inc(ld, 16)
                    sp.dma_start(rows[0:CH - full, k, CG - 1, :], env[dd][full:CH, :]).then_inc(ld, 16)

                def body(i):
                    for b in range(2):
                        j = 2 * i + b
                        sp.wait_ge(cpy, j + 1)
                        for h in range(H):
                            sp.dma_start(env["sc_d"][h][bass.ds(j * SB, SB), :], eT[h * SB:(h + 1) * SB, b, :])\
                                .then_inc(st[b], 16)
                with sp.Fori(0, SBL // 2) as i:
                    body(i)
                for b in range(2):
                    sp.wait_ge(st[b], 16 * H * SBL // 2)

            @block.vector
            def _(v):
                v.memset(rows[:, :, CG - 1, :], 0.0).then_inc(fl, 1)
                v.wait_ge(ld, 64)
                v.tensor_scalar(rows[:, 1, :, :], rows[:, 1, :, :], float(N - 1), None, ALU.min).then_inc(cl, 1)
                for k in range(CG):
                    v.wait_ge(tr, k + 1)
                    v.tensor_copy(cols[:, :, k * P:(k + 1) * P], pt[:, :, :]).then_inc(cp, 1)

                def body(i):
                    for b in range(2):
                        j = 2 * i + b
                        v.wait_ge(gs[b], 16 * 2 * SB * (i + 1))
                        c = Chain(v, lk, 3 * j)
                        c(v.tensor_tensor(x[:, :, :], g[:, b, 0, :, 0:H], g[:, b, 1, :, H:2 * H], ALU.add))
                        xf, yf = flat(x[:, :, :]), flat(y[:, :, :])
                        c(v.scalar_tensor_tensor(out=yf, in0=xf, scalar=0.01, in1=xf, op0=ALU.mult, op1=ALU.max))
                        c(v.tensor_scalar(z[:, :, :], y[:, :, :], 0.0, -1000.0, ALU.is_equal, ALU.mult))
                        wait(v, trn, j - 1)
                        v.tensor_tensor(e[:, b, :, :].rearrange("p h s -> p s h"), y[:, :, :], z[:, :, :],
                                        ALU.add).then_inc(sc, 1)
                        v.wait_ge(sc, j + 1)
                body(0)
                with v.Fori(1, SBL // 2) as i:
                    body(i)

            @block.tensor
            def _(pe):
                pe.wait_ge(cl, 1)
                for k in range(CG):
                    wait(pe, cp, k)
                    for s in range(2):
                        last = pe.transpose(pt[:, s, :], rows[:, s, k, :], env["ident"][:, :])
                    last.then_inc(tr, 1)

                def body(i):
                    for b in range(2):
                        j = 2 * i + b
                        pe.wait_ge(sc, j + 1)
                        wait(pe, cpy, j - 1)
                        pe.transpose(pe_[b][:, :], e[:, b, :, :].rearrange("p h s -> p (h s)"), env["ident"][:, :])\
                            .then_inc(trn, 1)
                body(0)
                with pe.Fori(1, SBL // 2) as i:
                    body(i)

            @block.scalar
            def _(act):
                act.wait_ge(cp, CG)

                def stage(j, b, used):
                    wait(act, sc, used)
                    act.copy(ring[:, b, :, :], cols[:, :, bass.ds(j * SB, SB)]).then_inc(staged, 1)
                stage(0, 0, 0)
                stage(1, 1, 0)

                def body(i, more):
                    for b in range(2):
                        j = 2 * i + b
                        act.wait_ge(trn, j + 1)
                        wait(act, st[b], 16 * H * i)
                        act.copy(eT[:, b, :], pe_[b][:, :]).then_inc(cpy, 1)
                        if more:
                            stage(j + 2, b, j + 1)
                body(0, True)
                with act.Fori(1, SBL // 2 - 1) as i:
                    body(i, True)
                body(SBL // 2 - 1, False)

            @block.gpsimd
            def _(pool):
                with pool.Fori(0, SBL // 2) as i:
                    for b in range(2):
                        pool.wait_ge(staged, 2 * i + b + 1)
                        pool.sem_inc(go, 1)
                        for k in range(SB):
                            for s in range(2):
                                pool.indirect_dma_start(
                                    out=g[:, b, s, k, :], out_offset=None, in_=env["att_t"][:, :],
                                    in_offset=bass.IndirectOffsetOnAxis(ap=ring[:, b, s, k:k + 1], axis=0))\
                                    .then_inc(gs[b], 16)


def softmax(env):
    nc = env["nc"]
    with Phase(nc, "sm") as ph:
        b = scan_buffers(env, ph)
        loaded, again, tot, sub, ex, put = (ph.sem(n) for n in ("loaded", "again", "maxima", "shifted", "exps", "put"))
        scan_flags(env, b)
        view = lambda h: env["sc_d"][h][0:CH, :]
        with nc.Block() as block:
            @block.sync
            def _(sp):
                for h in range(H):
                    sp.dma_start(b["val"][:, h, :], scan_view(view(h))).then_inc(loaded, 16)
                sp.wait_ge(tot, 1)
                for h in range(H):
                    sp.dma_start(b["run"][:, h, :], scan_view(view(h))).then_inc(again, 16)
                for h in range(H):
                    sp.wait_ge(ex, h + 1)
                    sp.dma_start(scan_view(env["ex_d"][h]), b["run"][:, h, :]).then_inc(put, 16)
                sp.wait_ge(put, 64)

            @block.vector
            def _(v):
                chain = Chain(v, b["dve"], b["n"])
                v.wait_ge(loaded, 64)
                seg_forward(v, chain, b, H, ALU.add, b["st"], ALU.max, -BIG)
                seg_backward(v, chain, b, H)
                v.sem_inc(tot, 1)
                v.wait_ge(again, 64)
                for h in range(H):
                    v.tensor_tensor(b["run"][:, h, :], b["run"][:, h, :], b["val"][:, h, :], ALU.subtract).then_inc(sub, 1)

            @block.tensor
            def _(pe):
                for _ in range(2):
                    seg_carry(pe, b, H)

            @block.scalar
            def _(act):
                for h in range(H):
                    act.wait_ge(sub, h + 1)
                    act.activation(b["run"][:, h, :], b["run"][:, h, :], ACT.Exp).then_inc(ex, 1)


def ex_columns(env):
    return env["Hh"][:, :, :].rearrange("p t d -> p (t d)")[:, 0:H * IG * P].rearrange("p (h i) -> p h i", h=H)


def score_items(env):
    nc = env["nc"]
    with Phase(nc, "si") as ph:
        rows = ph.sb("rows", [P, IG, H, P])
        pt = ph.ps("pt", [P, H, P])
        gat, tr, cp = ph.sem("gathered"), ph.sem("transposed"), ph.sem("copied")
        with nc.Block() as block:
            @block.gpsimd
            def _(pool):
                for g in range(IG):
                    for h in range(H):
                        pool.indirect_dma_start(out=rows[:, g, h, :], out_offset=None, in_=env["ex_d"][h][:, :],
                                                in_offset=bass.IndirectOffsetOnAxis(
                                                    ap=env["item_chunk"][:, g:g + 1], axis=0)).then_inc(gat, 16)

            @block.tensor
            def _(pe):
                pe.wait_ge(gat, 16 * H * IG)
                for g in range(IG):
                    wait(pe, cp, g)
                    for h in range(H):
                        last = pe.transpose(pt[:, h, :], rows[:, g, h, :], env["ident"][:, :])
                    last.then_inc(tr, 1)

            @block.vector
            def _(v):
                for g in range(IG):
                    v.wait_ge(tr, g + 1)
                    v.tensor_copy(ex_columns(env)[:, :, g * P:(g + 1) * P], pt[:, :, :]).then_inc(cp, 1)
                v.wait_ge(cp, IG)


LAG = 4
NS = 8


def aggregate(env, name, layer, table, W, limit, idx, weight):
    nc = env["nc"]
    target = env["agg_d"][layer]
    per_head = weight == "ex"
    with Phase(nc, name) as ph:
        G = ph.sb("G", [P, U, W])
        S = ph.sb("S", [P, NS, P])
        acc = ph.sb("acc", [P, U, W])
        gw = ph.sb("gw", [P, NS, W]) if per_head else None
        r_idx = ph.sb("r_idx", [P, U], I32)
        r_dst, r_wgt, r_keep = (ph.sb(n, [P, U]) for n in ("r_dst", "r_wgt", "r_keep"))
        r_ex = ph.sb("r_ex", [P, H, U]) if per_head else None
        ps = [ph.ps(f"ps{i}", [P, W]) for i in range(NS)]
        staged, go, built, products, added, cleared = (ph.sem(n) for n in (
            "staged", "go", "selections", "products", "added", "cleared"))
        gs = [ph.sem(f"gathered{k}") for k in range(U)]
        st = [ph.sem(f"stored{k}") for k in range(U)]
        HU = U // 2
        with nc.Block() as block:
            @block.gpsimd
            def _(pool):
                lim = pool.to_reg(limit)
                pool.memset(G[:, :, :], 0.0).then_inc(cleared, 1)
                pool.wait_ge(cleared, 2)
                with pool.Fori(0, ITEMS // U) as j:
                    for half in range(2):
                        pool.wait_ge(staged, 2 * j + half + 1)
                        pool.sem_inc(go, 1)
                        for k in range(half * HU, (half + 1) * HU):
                            pool.indirect_dma_start(out=G[:, k, :], out_offset=None, in_=table[:, :],
                                                    in_offset=bass.IndirectOffsetOnAxis(ap=r_idx[:, k:k + 1], axis=0),
                                                    bounds_check=lim, oob_is_err=False).then_inc(gs[k], 16)

            @block.scalar
            def _(act):
                def body(j):
                    for half in range(2):
                        a, b = half * HU, (half + 1) * HU
                        wait(act, added, U * (j - 1) + b)
                        s = bass.ds(j * U + a, HU)
                        act.copy(r_dst[:, a:b], env["item_dst"][:, s])
                        act.copy(r_keep[:, a:b], env["item_keep"][:, s])
                        if weight == "wgt":
                            act.copy(r_wgt[:, a:b], env["item_wgt"][:, s])
                        if per_head:
                            act.copy(r_ex[:, :, a:b], ex_columns(env)[:, :, s])
                        act.copy(r_idx[:, a:b], idx[:, s]).then_inc(staged, 1)
                body(0)
                with act.Fori(1, ITEMS // U) as j:
                    body(j)

            @block.vector
            def _(v):
                v.memset(acc[:, U - 1, :], 0.0).then_inc(cleared, 1)
                v.wait_ge(cleared, 2)

                def select(i, k, j):
                    if k % HU == 0:
                        v.wait_ge(staged, 2 * j + k // HU + 1)
                    wait(v, products, i - NS + 1)
                    if per_head:
                        v.wait_ge(gs[k], 16 * (j + 1))
                        v.tensor_tensor(gw[:, k % NS, :].rearrange("p (h f) -> p h f", h=H),
                                        G[:, k, :].rearrange("p (h f) -> p h f", h=H),
                                        r_ex[:, :, k:k + 1].to_broadcast([P, H, F + 1]), ALU.mult).then_inc(built, 1)
                    if weight == "wgt":
                        v.tensor_scalar(S[:, k % NS, :], env["iota"][:, :], r_dst[:, k:k + 1], r_wgt[:, k:k + 1],
                                        ALU.is_equal, ALU.mult).then_inc(built, 1)
                    else:
                        v.tensor_scalar(S[:, k % NS, :], env["iota"][:, :], r_dst[:, k:k + 1], None,
                                        ALU.is_equal).then_inc(built, 1)

                def add(i, k, h):
                    v.wait_ge(products, i + 1)
                    wait(v, added, i)
                    wait(v, st[k], 16 * h)
                    v.scalar_tensor_tensor(out=acc[:, k, :], in0=acc[:, (k - 1) % U, :], scalar=r_keep[:, k:k + 1],
                                           in1=ps[k % NS][:, :], op0=ALU.mult, op1=ALU.add).then_inc(added, 1)

                def body(j):
                    for k in range(U):
                        select(U * j + k, k, j)
                        if k >= LAG:
                            add(U * j + k - LAG, k - LAG, j)
                        elif not isinstance(j, int):
                            add(U * j + k - LAG, U + k - LAG, j - 1)
                body(0)
                with v.Fori(1, ITEMS // U) as j:
                    body(j)
                for k in range(U - LAG, U):
                    add(ITEMS - U + k, k, ITEMS // U - 1)

            @block.tensor
            def _(pe):
                n = 2 if per_head else 1

                def body(j):
                    for k in range(U):
                        i = U * j + k
                        pe.wait_ge(built, n * (i + 1))
                        if not per_head:
                            pe.wait_ge(gs[k], 16 * (j + 1))
                        wait(pe, added, i - NS + 1)
                        pe.matmul(ps[k % NS][:, :], S[:, k % NS, :], gw[:, k % NS, :] if per_head else G[:, k, :],
                                  start=True, stop=True).then_inc(products, 1)
                body(0)
                with pe.Fori(1, ITEMS // U) as j:
                    body(j)

            @block.sync
            def _(sp):
                with sp.Fori(0, ITEMS // U) as j:
                    for k in range(U):
                        i = U * j + k
                        row = sp.value_load(env["item_row"][0:1, bass.ds(i, 1)], min_val=0, max_val=NT - 1)
                        sp.wait_ge(added, i + 1)
                        sp.dma_start(target[bass.ds(row * P, P), :], acc[:, k, :], cond=row < RT).then_inc(st[k], 16)
                for k in range(U):
                    sp.wait_ge(st[k], 16 * ITEMS // U)


def add_attention(env):
    nc, X = env["nc"], env["X"]
    W = agg_width(1)
    with Phase(nc, "aa") as ph:
        g = ph.sb("g", [P, 2, W])
        den, rec, o = ph.sb("den", [P, 2, H]), ph.sb("rec", [P, 2, H]), ph.sb("o", [P, 2, D])
        dv, done = ph.sem("link"), ph.sem("done")
        got = [ph.sem(f"got{i}") for i in range(2)]
        with nc.Block() as block:
            @block.sync
            def _(sp):
                def body(j):
                    for u in range(2):
                        t = 2 * j + u
                        wait(sp, done, t - 1)
                        sp.dma_start(g[:, u, :], env["agg_d"][1][bass.ds(t * P, P), :]).then_inc(got[u], 16)
                body(0)
                with sp.Fori(1, NT // 2) as j:
                    body(j)

            @block.vector
            def _(v):
                with v.Fori(0, NT // 2) as j:
                    for u in range(2):
                        t = 2 * j + u
                        v.wait_ge(got[u], 16 * (j + 1))
                        gh = g[:, u, :].rearrange("p (h f) -> p h f", h=H)
                        c = Chain(v, dv, 5 * t)
                        c(v.tensor_scalar(den[:, u, :], gh[:, :, F], 0.0, None, ALU.is_le))
                        c(v.tensor_tensor(den[:, u, :], den[:, u, :], gh[:, :, F], ALU.add))
                        c(v.reciprocal(rec[:, u, :], den[:, u, :]))
                        c(v.tensor_tensor(o[:, u, :].rearrange("p (h f) -> p h f", h=H), gh[:, :, 0:F],
                                          rec[:, u, :].unsqueeze(2).to_broadcast([P, H, F]), ALU.mult))
                        c(v.tensor_tensor(tile_of(X, t), tile_of(X, t), o[:, u, :], ALU.add))
                        v.sem_inc(done, 1)


def prelu(v, c, out, x, alpha, tmp):
    c(v.scalar_tensor_tensor(out=tmp, in0=x, scalar=0.0, in1=alpha, op0=ALU.min, op1=ALU.mult))
    return v.scalar_tensor_tensor(out=out, in0=x, scalar=0.0, in1=tmp, op0=ALU.max, op1=ALU.add)


def layer3_tables(env):
    nc, A, X, Hh = env["nc"], env["A"], env["X"], env["Hh"]
    norm_phase(env, "n3")
    d = Dense(env, "p3", D)
    with d.ph as ph:
        w = ph.sb("w", [P, 2, D])
        bias, alpha = ph.sb("bias", [P, D]), ph.sb("alpha", [P, D])
        x, tmp = ph.sb("x", [P, 2, D]), ph.sb("tmp", [P, 2, D])
        ld = ph.sem("loaded")
        with nc.Block() as block:
            @block.sync
            def _(sp):
                sp.dma_start(w[:, :, :], A["L3_gnn_W_pre"].rearrange("(k p) o -> p k o", p=P)).then_inc(ld, 16)
                load_rows(sp, ld, [(bias[:, :], A["L3_gnn_b_pre"]), (alpha[:, :], A["L3_gnn_alpha_pre"])])

            @block.vector
            def _(v):
                v.wait_ge(ld, 48)

                def post(t, u, h, c):
                    c(v.tensor_tensor(x[:, u, :], d.psO[u][:, :], bias[:, :], ALU.add))
                    return prelu(v, c, tile_of(Hh, t), x[:, u, :], alpha[:, :], tmp[:, u, :])
                d.dve(v, copy_rows(v, d, Hh), post, 0, 2)

            @block.tensor
            def _(pe):
                pe.wait_ge(ld, 48)
                d.pe(pe, lambda k: w[:, k, :])

            @block.scalar
            def _(act):
                d.act(act)
    d = Dense(env, "m3", D)
    with d.ph as ph:
        w = ph.sb("w", [P, 2, D])
        bias, o = ph.sb("bias", [P, D]), ph.sb("o", [P, 2, D])
        ld = ph.sem("loaded")
        st = [ph.sem(f"stored{i}") for i in range(2)]
        with nc.Block() as block:
            @block.sync
            def _(sp):
                sp.dma_start(w[:, :, :], A["L3_gnn_W_mp"].rearrange("(k p) o -> p k o", p=P)).then_inc(ld, 16)
                load_rows(sp, ld, [(bias[:, :], A["L3_gnn_b_mp"])])
                tile_stores(d, sp, [(o, st, lambda t: env["m_t"][bass.ds(t * P, P), :])])

            @block.vector
            def _(v):
                v.wait_ge(ld, 32)

                def post(t, u, h, c):
                    wait(v, st[u], 16 * h)
                    return v.tensor_tensor(o[:, u, :], d.psO[u][:, :], bias[:, :], ALU.add)
                d.dve(v, copy_rows(v, d, Hh), post, 0, 0)

            @block.tensor
            def _(pe):
                pe.wait_ge(ld, 32)
                d.pe(pe, lambda k: w[:, k, :])

            @block.scalar
            def _(act):
                d.act(act)


def layer3_end(env):
    nc, A, X, Hh = env["nc"], env["A"], env["X"], env["Hh"]
    d = Dense(env, "e3", D)
    with d.ph as ph:
        w = ph.sb("w", [P, 2, D])
        bias, alpha = ph.sb("bias", [P, D]), ph.sb("alpha", [P, D])
        ag = ph.sb("ag", [P, 2, D])
        tmp, r, x = ph.sb("tmp", [P, 2, D]), ph.sb("r", [P, 2, D]), ph.sb("x", [P, 2, D])
        ld, put = ph.sem("loaded"), ph.sem("put")
        got = [ph.sem(f"got{i}") for i in range(2)]
        with nc.Block() as block:
            @block.sync
            def _(sp):
                sp.dma_start(w[:, :, :], A["L3_gnn_W_post"].rearrange("(k p) o -> p k o", p=P)).then_inc(ld, 16)
                load_rows(sp, ld, [(bias[:, :], A["L3_gnn_b_post"]), (alpha[:, :], A["L3_gnn_alpha_mp"])])
                tile_loads(d, sp, ag, got, env["agg_d"][2])
                for t in range(0, RT - 1, 12):
                    sp.dma_start(env["out"][t * P:(t + 12) * P, :].rearrange("(t p) d -> p t d", p=P),
                                 X[:, t:t + 12, :]).then_inc(put, 16)
                sp.wait_ge(d.taken, NT)
                sp.dma_start(env["out"][(RT - 1) * P:N, :], X[0:LAST, RT - 1, :]).then_inc(put, 16)
                sp.wait_ge(put, 80)

            @block.vector
            def _(v):
                v.wait_ge(ld, 48)

                def pre(t, u, h, c):
                    v.wait_ge(got[u], 16 * (h + 1))
                    c(prelu(v, c, r[:, u, :], ag[:, u, :], alpha[:, :], tmp[:, u, :]))
                    return v.tensor_tensor(flat(d.rows[:, u, :, :]), tile_of(Hh, t), r[:, u, :], ALU.add)

                def post(t, u, h, c):
                    c(v.tensor_tensor(x[:, u, :], d.psO[u][:, :], bias[:, :], ALU.add))
                    return v.scalar_tensor_tensor(out=tile_of(X, t), in0=x[:, u, :], scalar=0.0, in1=tile_of(X, t),
                                                  op0=ALU.max, op1=ALU.add)
                d.dve(v, pre, post, 2, 1)

            @block.tensor
            def _(pe):
                pe.wait_ge(ld, 48)
                d.pe(pe, lambda k: w[:, k, :])

            @block.scalar
            def _(act):
                d.act(act)


_INS = ['x', 'src', 'dst', 'edge_type_8', 'L0_gnn_W', 'L0_gnn_b', 'L1_gnn_W_rel', 'L1_gnn_W_root', 'L1_gnn_bias',
        'L1_gnn_ln_gamma', 'L1_gnn_ln_beta', 'L2_gnn_W', 'L2_gnn_att', 'L3_gnn_W_pre', 'L3_gnn_b_pre',
        'L3_gnn_alpha_pre', 'L3_gnn_W_mp', 'L3_gnn_b_mp', 'L3_gnn_alpha_mp', 'L3_gnn_W_post', 'L3_gnn_b_post']


def kernel(**inputs):
    import numpy as _np
    import concourse.bacc as _bacc
    from concourse import mybir as _mybir
    from concourse.bass_utils import run_bass_kernel_spmd as _run

    nc = _bacc.Bacc("TRN2", target_bir_lowering=False, num_devices=1)
    arrays, args = {}, {}
    for name in _INS:
        a = _np.ascontiguousarray(inputs[name])
        arrays[f"in_{name}"] = a
        args[name] = nc.dram_tensor(f"in_{name}", a.shape, _mybir.dt.from_np(a.dtype), kind="ExternalInput").ap()
    out = nc.dram_tensor("out_x", (N, D), _mybir.dt.float32, kind="ExternalOutput").ap()
    build(nc, args, out)
    r = _run(nc, [arrays], core_ids=[0])
    return r.results[0]["out_x"]
```

```python
import concourse.bass as bass
from concourse import mybir
from contextlib import ExitStack

FP32 = mybir.dt.float32
BF16 = mybir.dt.bfloat16
I32 = mybir.dt.int32
ALU = mybir.AluOpType
ACT = mybir.ActivationFunctionType
AX = mybir.AxisListType

N, D, E = 6250, 256, 106250
R, H, F = 8, 4, 64
P = 128
NT = 50
NP = NT * P
RT = 49
LAST = N - (RT - 1) * P
CH = -(-E // P)
EP = CH * P
CG = -(-CH // P)
FULLP = E // CH
REST = E - FULLP * CH
U = 16
ITEMS = -(-(CH + RT - 1) // U) * U
IG = -(-ITEMS // P)
LC, LCH = 125, 850
LG = -(-LCH // P)
LU = 25
LP = 9
NHI, NLO = 98, 64
PADDST = 8191.0
OOB = 60000.0
BIG = 1.0e30
EPS = 1e-5


def wait(eng, sem, value):
    if isinstance(value, int) and value <= 0:
        return
    eng.wait_ge(sem, value)


class Chain:

    def __init__(self, eng, sem, base=0):
        self.eng, self.sem, self.base, self.n = eng, sem, base, 0

    def __call__(self, ins):
        self.n += 1
        ins.then_inc(self.sem, 1)
        self.eng.wait_ge(self.sem, self.base + self.n)


def build(nc, A, out):
    top = ExitStack()
    with top:
        def dram(name, shape, dt=FP32):
            return nc.dram_tensor(name, shape, dt).ap()

        dst_d = dram("dst_d", (CH, P))
        src_d = dram("src_d", (CH, P))
        rel_d = dram("rel_d", (CH, P))
        wgt_d = dram("wgt_d", (CH, P))
        item_gdst_d = dram("item_gdst_d", (ITEMS, P))
        item_ldst_d = dram("item_ldst_d", (ITEMS, P))
        sc_d = [dram(f"sc_d{h}", (ITEMS, P)) for h in range(H)]
        ex_d = [dram(f"ex_d{h}", (ITEMS, P)) for h in range(H)]
        last_d = dram("last_d", (NHI * NLO,))
        pack_d = dram("pack_d", (E,), I32)
        item_d = dram("item_d", (4, IG * P))
        h_d = dram("h_d", (NP, D))
        rel_t = dram("rel_t", (NP * R, D))
        z_t = dram("z_t", (NP, H * (F + 1)))
        es_t = dram("es_t", (NP, H))
        m_t = dram("m_t", (NP, D))
        agg_d = [dram(f"agg_d{l}", (NP, w)) for l, w in enumerate((D, H * (F + 1), D))]

        def sb(name, shape, dt=FP32, ctx=top):
            return ctx.enter_context(nc.sbuf_tensor(name, shape, dt))

        X = sb("X", [P, NT, D])
        Hh = sb("Hh", [P, NT, D])
        ident = sb("ident", [P, P])
        iota = sb("iota", [P, P])
        item_dst = sb("item_dst", [P, IG * P])
        item_rel = sb("item_rel", [P, IG * P], I32)
        item_src = sb("item_src", [P, IG * P], I32)
        item_wgt = sb("item_wgt", [P, IG * P])
        item_chunk = sb("item_chunk", [P, IG], I32)
        item_tile = sb("item_tile", [1, IG * P], I32)
        ed_sb = sb("ed_sb", [P, NT * (H + 1)])
        item_keep = sb("item_keep", [P, IG * P])
        item_row = sb("item_row", [1, IG * P], I32)
        eps_c = sb("eps_c", [P, 1])
        node = sb("node", [P, NT])
        last_dst = sb("last_dst", [P, NT], I32)

        stats = sb("stats", [P, NT, 6])
        rstd, nmr = sb("rstd", [P, NT]), sb("nmr", [P, NT])

        env = dict(locals())
        setup(env)
        seg_weights(env)
        items(env)
        last_edges(env)
        layer0(env)
        layer1_tables(env)
        aggregate(env, "a1", 0, rel_t, D, N * R - 1, item_rel, "wgt")
        layer1_end(env)
        layer2_tables(env)
        edge_scores(env)
        softmax(env)
        score_items(env)
        aggregate(env, "a2", 1, z_t, H * (F + 1), N - 1, item_src, "ex")
        add_attention(env)
        layer3_tables(env)
        aggregate(env, "a3", 2, m_t, D, N - 1, item_src, None)
        layer3_end(env)


def agg_width(l):
    return H * (F + 1) if l == 1 else D


class Phase:

    def __init__(self, nc, name):
        self.nc, self.name, self.ctx, self.sems = nc, name, ExitStack(), []

    def __enter__(self):
        return self

    def __exit__(self, *a):
        self.ctx.close()
        self.nc.clear_and_free_semaphores(self.sems)
        self.nc.all_engine_barrier()

    def sb(self, name, shape, dt=FP32):
        return self.ctx.enter_context(self.nc.sbuf_tensor(f"{self.name}_{name}", shape, dt))

    def ps(self, name, shape, dt=FP32):
        return self.ctx.enter_context(self.nc.psum_tensor(f"{self.name}_{name}", shape, dt))

    def sem(self, name):
        self.sems.append(self.nc.alloc_semaphore(f"{self.name}_{name}"))
        return self.sems[-1]


def setup(env):
    nc, A = env["nc"], env["A"]
    X, ident, iota = env["X"], env["ident"], env["iota"]
    with Phase(nc, "su") as ph:
        di = ph.sb("di", [P, CH], I32)
        si = ph.sb("si", [P, CH], I32)
        ti = ph.sb("ti", [P, CH], I32)
        df, sf, tf = (ph.sb(n, [P, CH]) for n in ("df", "sf", "tf"))
        rl = ph.sb("rl", [P, CH])
        ones = ph.sb("ones", [P, P])
        cnt = ph.sb("cnt", [P, NT])
        bnd = ph.sb("bnd", [P, NT])
        bi = ph.sb("bi", [P, NT], I32)
        flo = ph.sb("flo", [P, NT])
        cei = ph.sb("cei", [P, NT])
        num = ph.sb("num", [P, NT])
        pre = ph.sb("pre", [P, NT])
        dlt = ph.sb("dlt", [P, NT])
        dd = ph.sb("dd", [P, NT])
        ii = ph.sb("ii", [P, IG])
        i1 = ph.sb("i1", [P, IG])
        it = ph.sb("it", [P, 4, IG])
        itT = ph.sb("itT", [IG, 4, P])
        jk = ph.sb("jk", [P, CH])
        krow = ph.sb("krow", [P, IG * P])
        rrow = ph.sb("rrow", [1, 3, IG * P])
        psb = ph.ps("psb", [P, NT])
        psi = ph.ps("psi", [IG, 4, P])
        dls, xl, cst, fill = ph.sem("edges_in"), ph.sem("x_in"), ph.sem("const"), ph.sem("filled")
        dv, cs, bs, its, itt, itc = (ph.sem(n) for n in ("dve", "counts", "bounds", "items", "itemsT", "itemsTc"))
        fst, put, back, pl, rdy = (ph.sem(n) for n in ("floats", "put", "back", "pool", "item_put"))
        with nc.Block() as block:
            @block.gpsimd
            def _(pool):
                chain = Chain(pool, pl)
                chain(pool.memset(ident[:, :], 0.0))
                chain(pool.affine_select(out=ident[:, :], in_=ident[:, :], compare_op=ALU.not_equal, fill=1.0,
                                         base=0, pattern=[[-1, P]], channel_multiplier=1))
                pool.iota(iota[:, :], pattern=[[1, P]], base=0, channel_multiplier=0,
                          allow_small_or_imprecise_dtypes=True).then_inc(cst, 1)
                pool.iota(ii[:, :], pattern=[[P, IG]], base=0, channel_multiplier=1,
                          allow_small_or_imprecise_dtypes=True).then_inc(cst, 1)
                pool.iota(i1[:, :], pattern=[[P, IG]], base=1, channel_multiplier=1,
                          allow_small_or_imprecise_dtypes=True).then_inc(cst, 1)
                pool.memset(ones[:, :], 1.0).then_inc(cst, 1)
                pool.memset(env["eps_c"][:, :], EPS).then_inc(cst, 1)
                pool.memset(X[:, RT - 1:NT, :], 0.0).then_inc(cst, 1)
                pool.wait_ge(cst, 6)

            @block.sync
            def _(sp):
                sp.wait_ge(fill, 3)
                full = FULLP * CH
                for t, name in ((di, "dst"), (si, "src"), (ti, "edge_type_8")):
                    sp.dma_start(t[0:FULLP, :], A[name][0:full].rearrange("(p f) -> p f", f=CH)).then_inc(dls, 16)
                    sp.dma_start(t[FULLP:FULLP + 1, 0:REST], A[name][full:E].rearrange("(a f) -> a f", a=1))\
                        .then_inc(dls, 16)
                sp.wait_ge(cst, 6)
                for c in range(0, RT - 1, 12):
                    sp.dma_start(X[:, c:c + 12, :], A["x"][c * P:(c + 12) * P, :].rearrange("(t p) d -> p t d", p=P))\
                        .then_inc(xl, 16)
                sp.dma_start(X[0:LAST, RT - 1, :], A["x"][(RT - 1) * P:N, :]).then_inc(xl, 16)
                for l in range(3):
                    w = agg_width(l)
                    for c in range(0, w, D):
                        sp.dma_start(env["agg_d"][l][RT * P:NP, c:min(c + D, w)], X[:, RT, 0:min(D, w - c)])\
                            .then_inc(put, 16)
                sp.wait_ge(fst, 1)
                for n, (t, d) in enumerate(((df, "dst_d"), (sf, "src_d"), (rl, "rel_d"))):
                    sp.dma_start(env[d].rearrange("c e -> (c e)").rearrange("(p f) -> p f", f=CH), t[:, :])\
                        .then_inc(put, 16)
                sp.dma_start(env["pack_d"][0:FULLP * CH].rearrange("(p f) -> p f", f=CH), di[0:FULLP, :]).then_inc(put, 16)
                sp.dma_start(env["pack_d"][FULLP * CH:E].rearrange("(a f) -> a f", a=1), di[FULLP:FULLP + 1, 0:REST])\
                    .then_inc(put, 16)
                sp.wait_ge(itc, 1)
                for k in range(4):
                    sp.dma_start(env["item_d"][k, :].rearrange("(g p) -> g p", p=P), itT[:, k, :]).then_inc(rdy, 16)
                sp.wait_ge(rdy, 64)
                sp.dma_start(krow[:, :], env["item_d"][2:3, :].partition_broadcast(P)).then_inc(back, 16)
                sp.dma_start(rrow[0:1, 0, :], env["item_d"][1:2, :]).then_inc(back, 16)
                sp.dma_start(rrow[0:1, 1, :], env["item_d"][3:4, :]).then_inc(back, 16)
                sp.wait_ge(put, 48 + 64 + 32)
                sp.wait_ge(xl, 80)

            @block.vector
            def _(v):
                chain = Chain(v, dv)
                v.memset(di[:, :], int(PADDST)).then_inc(fill, 1)
                v.memset(si[:, :], 0).then_inc(fill, 1)
                v.memset(ti[:, :], 0).then_inc(fill, 1)
                v.wait_ge(fill, 3)
                v.wait_ge(dls, 16 * 6)
                chain(v.tensor_copy(df[:, :], di[:, :]))
                chain(v.tensor_copy(sf[:, :], si[:, :]))
                chain(v.tensor_copy(tf[:, :], ti[:, :]))
                chain(v.tensor_scalar(di[:, :], di[:, :], 13, None, ALU.logical_shift_left))
                chain(v.tensor_tensor(di[:, :], di[:, :], si[:, :], ALU.bitwise_or))
                v.scalar_tensor_tensor(out=rl[:, :], in0=sf[:, :], scalar=float(R), in1=tf[:, :],
                                       op0=ALU.mult, op1=ALU.add).then_inc(fst, 1)
                v.wait_ge(fst, 1)
                v.wait_ge(cst, 6)
                chain(v.memset(cnt[:, :], 0.0))
                for t in range(1, NT):
                    chain(v.tensor_scalar(jk[:, :], df[:, :], float(min(t * P, N)), 0.0, ALU.is_lt, ALU.add,
                                          accum_out=cnt[:, t:t + 1]))
                v.sem_inc(cs, 1)
                v.wait_ge(bs, 1)
                chain(v.tensor_copy(bnd[:, :], psb[:, :]))
                chain(v.tensor_copy(bi[:, :], bnd[:, :]))
                chain(v.tensor_scalar(bi[:, :], bi[:, :], 7, None, ALU.arith_shift_right))
                chain(v.tensor_copy(flo[:, :], bi[:, :]))
                chain(v.tensor_scalar(cei[:, :], bnd[:, :], float(P - 1), None, ALU.add))
                chain(v.tensor_copy(bi[:, :], cei[:, :]))
                chain(v.tensor_scalar(bi[:, :], bi[:, :], 7, None, ALU.arith_shift_right))
                chain(v.tensor_copy(cei[:, :], bi[:, :]))
                chain(v.memset(num[:, :], 0.0))
                chain(v.tensor_tensor(num[:, 1:NT], cei[:, 1:NT], flo[:, 0:NT - 1], ALU.subtract))
                chain(v.tensor_scalar(num[:, 1:NT], num[:, 1:NT], 1.0, None, ALU.max))
                chain(v.memset(dlt[:, :], 1.0))
                chain(v.tensor_tensor_scan(pre[:, :], dlt[:, :], num[:, :], 0.0, ALU.mult, ALU.add))
                chain(v.tensor_tensor(dlt[:, :], flo[:, :], pre[:, :], ALU.subtract))
                chain(v.tensor_copy(dd[:, 0:1], dlt[:, 0:1]))
                chain(v.tensor_tensor(dd[:, 1:NT], dlt[:, 1:NT], dlt[:, 0:NT - 1], ALU.subtract))
                for g in range(IG):
                    i = ii[:, g:g + 1]
                    chain(v.tensor_scalar(jk[:, 0:NT], pre[:, :], i, 0.0, ALU.is_le, ALU.add,
                                          accum_out=it[:, 1, g:g + 1]))
                    chain(v.scalar_tensor_tensor(out=jk[:, 0:NT], in0=pre[:, :], scalar=i, in1=dd[:, :],
                                                 op0=ALU.is_le, op1=ALU.mult, accum_out=it[:, 0, g:g + 1]))
                    chain(v.tensor_scalar(jk[:, 0:NT], pre[:, :], i, 0.0, ALU.is_equal, ALU.add,
                                          accum_out=it[:, 2, g:g + 1]))
                    chain(v.tensor_scalar(jk[:, 0:NT], pre[:, :], i1[:, g:g + 1], 0.0, ALU.is_equal, ALU.add,
                                          accum_out=it[:, 3, g:g + 1]))
                chain(v.tensor_tensor(it[:, 0, :], it[:, 0, :], ii[:, :], ALU.add))
                chain(v.tensor_scalar(it[:, 0, :], it[:, 0, :], float(CH - 1), None, ALU.min))
                chain(v.tensor_scalar(it[:, 1, :], it[:, 1, :], 1.0, None, ALU.subtract))
                v.sem_inc(its, 1)
                v.wait_ge(itt, 1)
                v.tensor_copy(itT[:, :, :], psi[:, :, :]).then_inc(itc, 1)
                v.wait_ge(back, 48)
                chain(v.tensor_scalar(env["item_keep"][:, :], krow[:, :], -1.0, 1.0, ALU.mult, ALU.add))
                chain(v.tensor_copy(env["item_tile"][0:1, :], rrow[0:1, 0, :]))
                chain(v.tensor_scalar(rrow[0:1, 0, :], rrow[0:1, 0, :], float(RT), None, ALU.subtract))
                chain(v.tensor_tensor(rrow[0:1, 0, :], rrow[0:1, 0, :], rrow[0:1, 1, :], ALU.mult))
                chain(v.tensor_scalar(rrow[0:1, 0, :], rrow[0:1, 0, :], float(RT), None, ALU.add))
                chain(v.tensor_copy(env["item_row"][0:1, :], rrow[0:1, 0, :]))

            @block.tensor
            def _(pe):
                pe.wait_ge(cs, 1)
                pe.wait_ge(cst, 6)
                pe.matmul(psb[:, :], ones[:, :], cnt[:, :], start=True, stop=True).then_inc(bs, 1)
                pe.wait_ge(its, 1)
                pe.wait_ge(pl, 2)
                for k in range(4):
                    last = pe.transpose(psi[:, k, :], it[:, k, :], ident[:, :])
                last.then_inc(itt, 1)


def scan_view(d):
    return d.rearrange("c e -> (c e)").rearrange("(p f) -> p f", p=P)


def scan_buffers(env, ph, width, extra):
    big = env["Hh"][:, :, :].rearrange("p t d -> p (t d)")
    b = dict(ident=env["ident"], n=0, stage=0, pe_stage=0, width=width)
    b["val"] = big[:, 0:H * width].rearrange("p (c f) -> p c f", f=width)
    b["run"] = big[:, H * width:2 * H * width].rearrange("p (c f) -> p c f", f=width)
    for k in range(extra):
        b[f"x{k}"] = big[:, (2 * H + k) * width:(2 * H + k + 1) * width]
    for n in ("st", "nst", "nen", "en"):
        b[n] = ph.sb(n, [P, width])
    b["tot"] = ph.sb("tot", [P, 2 * H])
    b["totT"] = ph.sb("totT", [H, 2, P])
    b["car"] = ph.sb("car", [H, P + 1])
    b["carT"] = ph.sb("carT", [P, H])
    b["psT"] = ph.ps("psT", [H, 2, P])
    b["psC"] = ph.ps("psC", [P, H])
    for n in ("dve", "tot_ready", "totT_ready", "car_ready", "carT_ready", "shifted_in", "filled"):
        b[n] = ph.sem(n)
    return b


def scan_flags(env, b, source):
    nc = env["nc"]
    dst = source.rearrange("c e -> (c e)")
    w, n = b["width"], b["width"] * P
    cur, prv, nxt = b["x0"], b["x1"], b["x2"]
    ld, fl = b["shifted_in"], b["filled"]
    with nc.Block() as block:
        @block.sync
        def _(sp):
            sp.wait_ge(fl, 2)
            row = lambda a: a.rearrange("(a f) -> a f", a=1)
            sp.dma_start(cur, dst.rearrange("(p f) -> p f", f=w)).then_inc(ld, 16)
            sp.dma_start(prv[0:1, 1:w], row(dst[0:w - 1])).then_inc(ld, 16)
            sp.dma_start(prv[1:P, :], dst[w - 1:n - 1].rearrange("(p f) -> p f", f=w)).then_inc(ld, 16)
            sp.dma_start(nxt[0:P - 1, :], dst[1:n - w + 1].rearrange("(p f) -> p f", f=w)).then_inc(ld, 16)
            sp.dma_start(nxt[P - 1:P, 0:w - 1], row(dst[n - w + 1:n])).then_inc(ld, 16)
            sp.wait_ge(ld, 80)

        @block.vector
        def _(v):
            chain = Chain(v, b["dve"])
            v.memset(prv, -1.0).then_inc(fl, 1)
            v.memset(nxt, -1.0).then_inc(fl, 1)
            v.wait_ge(ld, 80)
            chain(v.tensor_tensor(b["nst"][:, :], cur, prv, ALU.is_equal))
            chain(v.tensor_tensor(b["nen"][:, :], cur, nxt, ALU.is_equal))
            chain(v.tensor_scalar(b["st"][:, :], b["nst"][:, :], BIG, -BIG, ALU.mult, ALU.add))
            chain(v.tensor_scalar(b["en"][:, :], b["nen"][:, :], -1.0, 1.0, ALU.mult, ALU.add))
            b["n"] = chain.n


def seg_weights(env):
    nc = env["nc"]
    with Phase(nc, "sw") as ph:
        b = scan_buffers(env, ph, CH, 7)
        tf, eq, wsum, sf = b["x3"], b["x4"], b["x5"], b["x6"]
        loaded, put, fin = ph.sem("loaded"), ph.sem("put"), ph.sem("weights")
        scan_flags(env, b, env["dst_d"])
        with nc.Block() as block:
            @block.vector
            def _(v):
                chain = Chain(v, b["dve"], b["n"])
                v.wait_ge(loaded, 32)
                chain(v.scalar_tensor_tensor(out=tf, in0=sf, scalar=-float(R), in1=tf, op0=ALU.mult, op1=ALU.add))
                chain(v.memset(wsum, 0.0))
                for half in range(R // H):
                    for r in range(H):
                        chain(v.tensor_scalar(b["val"][:, r, :], tf, float(H * half + r), None, ALU.is_equal))
                    seg_forward(v, chain, b, H, ALU.mult, b["nst"], ALU.add, 0.0)
                    seg_backward(v, chain, b, H)
                    for r in range(H):
                        chain(v.scalar_tensor_tensor(out=eq, in0=tf, scalar=float(H * half + r),
                                                     in1=b["val"][:, r, :], op0=ALU.is_equal, op1=ALU.mult))
                        chain(v.tensor_tensor(wsum, wsum, eq, ALU.add))
                chain(v.tensor_scalar(wsum, wsum, 1.0, None, ALU.max))
                v.reciprocal(eq, wsum).then_inc(fin, 1)

            @block.tensor
            def _(pe):
                for _ in range(2 * R // H):
                    seg_carry(pe, b, H)

            @block.sync
            def _(sp):
                sp.dma_start(tf, scan_view(env["rel_d"])).then_inc(loaded, 16)
                sp.dma_start(sf, scan_view(env["src_d"])).then_inc(loaded, 16)
                sp.wait_ge(fin, 1)
                sp.dma_start(scan_view(env["wgt_d"]), eq).then_inc(put, 16)
                sp.wait_ge(put, 16)


def seg_carry(pe, b, ch):
    k = b["pe_stage"] = b["pe_stage"] + 1
    pe.wait_ge(b["tot_ready"], k)
    pe.transpose(b["psT"][:, 0, :], b["tot"][:, 0:ch], b["ident"][:, :])
    pe.transpose(b["psT"][:, 1, :], b["tot"][:, ch:2 * ch], b["ident"][:, :]).then_inc(b["totT_ready"], 1)
    pe.wait_ge(b["car_ready"], k)
    lo = 0 if k % 2 else 1
    pe.transpose(b["psC"][:, :], b["car"][:, lo:lo + P], b["ident"][0:ch, 0:ch]).then_inc(b["carT_ready"], 1)


def seg_forward(v, chain, b, ch, op0, reset, op1, init):
    k = b["stage"] = b["stage"] + 1
    val, run, tot = b["val"], b["run"], b["tot"]
    for c in range(ch):
        chain(v.tensor_tensor_scan(run[:, c, :], reset[:, :], val[:, c, :], init, op0, op1))
    chain(v.tensor_copy(tot[:, 0:ch], run[:, :, b["width"] - 1]))
    chain(v.tensor_reduce(tot[:, ch:ch + 1], reset[:, :], AX.X, ALU.min))
    for c in range(1, ch):
        chain(v.tensor_copy(tot[:, ch + c:ch + c + 1], tot[:, ch:ch + 1]))
    v.sem_inc(b["tot_ready"], 1)
    v.wait_ge(b["totT_ready"], k)
    chain(v.tensor_copy(b["totT"][:, :, :], b["psT"][:, :, :]))
    chain(v.memset(b["car"][:, :], init))
    chain(v.tensor_tensor_scan(b["car"][:, 1:P + 1], b["totT"][:, 1, :], b["totT"][:, 0, :], init, op0, op1))
    v.sem_inc(b["car_ready"], 1)
    v.wait_ge(b["carT_ready"], k)
    chain(v.tensor_copy(b["carT"][:, :], b["psC"][:, :]))
    for c in range(ch):
        chain(v.tensor_tensor_scan(run[:, c, :], reset[:, :], val[:, c, :], b["carT"][:, c:c + 1], op0, op1))


def seg_backward(v, chain, b, ch):
    k = b["stage"] = b["stage"] + 1
    val, run, tot = b["val"], b["run"], b["tot"]
    for c in range(ch):
        chain(v.tensor_tensor(run[:, c, :], run[:, c, :], b["en"][:, :], ALU.mult))
    for c in range(ch):
        chain(v.tensor_tensor_scan(val[:, c, ::-1], b["nen"][:, ::-1], run[:, c, ::-1], 0.0, ALU.mult, ALU.add))
    chain(v.tensor_copy(tot[:, 0:ch], val[:, :, 0]))
    chain(v.tensor_reduce(tot[:, ch:ch + 1], b["nen"][:, :], AX.X, ALU.min))
    for c in range(1, ch):
        chain(v.tensor_copy(tot[:, ch + c:ch + c + 1], tot[:, ch:ch + 1]))
    v.sem_inc(b["tot_ready"], 1)
    v.wait_ge(b["totT_ready"], k)
    chain(v.tensor_copy(b["totT"][:, :, :], b["psT"][:, :, :]))
    chain(v.memset(b["car"][:, :], 0.0))
    chain(v.tensor_tensor_scan(b["car"][:, P - 1::-1], b["totT"][:, 1, ::-1], b["totT"][:, 0, ::-1], 0.0,
                               ALU.mult, ALU.add))
    v.sem_inc(b["car_ready"], 1)
    v.wait_ge(b["carT_ready"], k)
    chain(v.tensor_copy(b["carT"][:, :], b["psC"][:, :]))
    for c in range(ch):
        chain(v.tensor_tensor_scan(val[:, c, ::-1], b["nen"][:, ::-1], run[:, c, ::-1], b["carT"][:, c:c + 1],
                                   ALU.mult, ALU.add))


def items(env):
    nc = env["nc"]
    with Phase(nc, "it") as ph:
        cf, tl, ci = ph.sb("cf", [P, IG]), ph.sb("tl", [P, IG]), env["item_chunk"]
        rows = ph.sb("rows", [P, IG, 4, P])
        ok, tmp = ph.sb("ok", [P, P]), ph.sb("tmp", [P, P])
        pt = ph.ps("pt", [P, 4, P])
        got, idx, gat, dv, tr, cp, rd, put, put2 = (ph.sem(n) for n in (
            "got", "idx", "gathered", "dve", "tr", "cp", "rd", "put_global", "put_local"))
        with nc.Block() as block:
            @block.sync
            def _(sp):
                sp.dma_start(cf[:, :], env["item_d"][0, :].rearrange("(g p) -> p g", p=P),
                             allow_slow_non_contiguous=True).then_inc(got, 16)
                sp.dma_start(tl[:, :], env["item_d"][1, :].rearrange("(g p) -> p g", p=P),
                             allow_slow_non_contiguous=True).then_inc(got, 16)
                sp.wait_ge(gat, 16 * 4 * IG)
                for k, (sem, target) in enumerate(((put, "item_gdst_d"), (put2, "item_ldst_d"))):
                    if k:
                        sp.wait_ge(rd, IG)
                    full = (IG - 1) * P
                    sp.dma_start(env[target][0:full, :].rearrange("(g p) e -> p g e", p=P), rows[:, 0:IG - 1, 0, :])\
                        .then_inc(sem, 16)
                    sp.dma_start(env[target][full:ITEMS, :], rows[0:ITEMS - full, IG - 1, 0, :]).then_inc(sem, 16)
                sp.wait_ge(put2, 32)

            @block.gpsimd
            def _(pool):
                pool.wait_ge(idx, 1)
                for g in range(IG):
                    for k, d in enumerate(("dst_d", "src_d", "rel_d", "wgt_d")):
                        pool.indirect_dma_start(out=rows[:, g, k, :], out_offset=None, in_=env[d][:, :],
                                                in_offset=bass.IndirectOffsetOnAxis(ap=ci[:, g:g + 1], axis=0))\
                            .then_inc(gat, 16)
                pool.wait_ge(gat, 16 * 4 * IG)

            @block.vector
            def _(v):
                chain = Chain(v, dv)
                v.wait_ge(got, 32)
                v.tensor_copy(ci[:, :], cf[:, :]).then_inc(idx, 1)
                chain(v.tensor_scalar(tl[:, :], tl[:, :], float(P), None, ALU.mult))
                v.wait_ge(gat, 16 * 4 * IG)
                v.wait_ge(put, 32)
                for g in range(IG):
                    dl = rows[:, g, 0, :]
                    chain(v.tensor_scalar(dl, dl, tl[:, g:g + 1], None, ALU.subtract))
                    chain(v.tensor_scalar(tmp[:, :], dl, 0.0, None, ALU.is_ge))
                    chain(v.scalar_tensor_tensor(out=ok[:, :], in0=dl, scalar=float(P), in1=tmp[:, :],
                                                 op0=ALU.is_lt, op1=ALU.mult))
                    for k in (1, 2):
                        x = rows[:, g, k, :]
                        chain(v.scalar_tensor_tensor(out=x, in0=x, scalar=-OOB, in1=ok[:, :],
                                                     op0=ALU.add, op1=ALU.mult))
                        chain(v.tensor_scalar(x, x, OOB, None, ALU.add))
                    v.sem_inc(rd, 1)
                    v.wait_ge(tr, g + 1)
                    s = slice(g * P, (g + 1) * P)
                    chain(v.tensor_copy(env["item_dst"][:, s], pt[:, 0, :]))
                    chain(v.tensor_copy(env["item_src"][:, s], pt[:, 1, :]))
                    chain(v.tensor_copy(env["item_rel"][:, s], pt[:, 2, :]))
                    v.tensor_copy(env["item_wgt"][:, s], pt[:, 3, :]).then_inc(cp, 1)
                v.wait_ge(cp, IG)

            @block.tensor
            def _(pe):
                for g in range(IG):
                    pe.wait_ge(rd, g + 1)
                    wait(pe, cp, g)
                    for k in range(4):
                        last = pe.transpose(pt[:, k, :], rows[:, g, k, :], env["ident"][:, :])
                    last.then_inc(tr, 1)


def last_edges(env):
    nc, A = env["nc"], env["A"]
    with Phase(nc, "le") as ph:
        rw = ph.sb("rw", [P, LG, LC], I32)
        rf = ph.sb("rf", [P, LG, LC])
        ci = ph.sb("ci", [LC, LG * P], I32)
        chi, clo = ph.sb("chi", [LC, LG * P]), ph.sb("clo", [LC, LG * P])
        tmpi = ph.sb("tmpi", [LC, LG * P], I32)
        ohh = ph.sb("ohh", [LC, 2, LU, NHI], BF16)
        ohl = ph.sb("ohl", [LC, 2, LU, NLO], BF16)
        rlo = ph.sb("rlo", [LC, 2, LP])
        vi = ph.sb("vi", [NHI, NLO], I32)
        T, T1, nf = (ph.sb(n, [NHI, NLO]) for n in ("T", "T1", "nf"))
        pt = ph.ps("pt", [LC, P])
        pp = [ph.ps(f"pp{i}", [NHI, 512]) for i in range(2)]
        ld, tr, cp, dv, rd, hi_s, lo_s, mm, lp, fin, put, cv, cols = (
            ph.sem(n) for n in ("ld", "tr", "cp", "dve", "rd", "hi_ready", "lo_ready", "sums", "loop", "fin", "put",
                                "conv", "columns"))
        chunk, ci2, num, m = (ph.sb("chunk", [P, NT]), ph.sb("ci2", [P, NT], I32), ph.sb("num", [P, NT]),
                              ph.sb("m", [P, NT]))
        big = env["Hh"][:, :, :].rearrange("p t d -> p (t d)")
        pk = big[:, 0:RT * LC].rearrange("p (t e) -> p t e", e=LC)
        pk2 = big[:, RT * LC:2 * RT * LC].rearrange("p (t e) -> p t e", e=LC)
        z, back, gat, ready, io, staged, go = (ph.sem(n) for n in (
            "zeroed", "back", "gathered", "chunks", "iota", "staged", "go"))
        groups = LCH // LU

        with nc.Block() as block:
            @block.sync
            def _(sp):
                sp.wait_ge(rd, 1)
                full = (LG - 1) * P
                sp.dma_start(rw[:, 0:LG - 1, :], A["src"][0:full * LC].rearrange("(g p f) -> p g f", p=P, f=LC))\
                    .then_inc(ld, 16)
                sp.dma_start(rw[0:LCH - full, LG - 1, :], A["src"][full * LC:E].rearrange("(p f) -> p f", f=LC))\
                    .then_inc(ld, 16)
                sp.wait_ge(fin, 1)
                sp.dma_start(env["last_d"].rearrange("(h l) -> h l", l=NLO), T[:, :]).then_inc(put, 16)
                sp.wait_ge(put, 16)
                with nc.allow_non_contiguous_dma("one value per node"):
                    sp.dma_start(chunk[:, 0:RT], env["last_d"].rearrange("(t p) -> p t", p=P)).then_inc(back, 16)
                sp.wait_ge(back, 16)

            @block.vector
            def _(v):
                chain = Chain(v, dv)
                v.memset(rw[:, LG - 1, :], 12287).then_inc(rd, 1)
                v.memset(pk, 0.0).then_inc(z, 1)
                v.memset(chunk[:, :], 0.0).then_inc(z, 1)
                v.wait_ge(ld, 32)
                v.tensor_copy(rf[:, :, :], rw[:, :, :]).then_inc(cv, 1)
                for g in range(LG):
                    v.wait_ge(tr, g + 1)
                    v.tensor_copy(ci[:, g * P:(g + 1) * P], pt[:, :]).then_inc(cp, 1)
                v.wait_ge(cp, LG)
                chain(v.tensor_scalar(tmpi[:, :], ci[:, :], 6, None, ALU.arith_shift_right))
                chain(v.tensor_copy(chi[:, :], tmpi[:, :]))
                chain(v.tensor_scalar(tmpi[:, :], ci[:, :], NLO - 1, None, ALU.bitwise_and))
                chain(v.tensor_copy(clo[:, :], tmpi[:, :]))
                v.sem_inc(cols, 1)
                chain(v.memset(T[:, :], 0.0))

                def build(j, b):
                    wait(v, mm, j - 1)
                    for k in range(LU):
                        v.tensor_scalar(ohh[:, b, k, :], env["iota"][0:LC, 0:NHI], chi[:, bass.ds(j * LU + k, 1)],
                                        2.0 ** (8 * (k + 1) - 127), ALU.is_equal, ALU.mult).then_inc(hi_s, 1)

                    v.tensor_tensor(ohl[:, b, LP:LU, :],
                                    env["iota"][0:LC, 0:NLO].unsqueeze(1).to_broadcast([LC, LU - LP, NLO]),
                                    clo[:, bass.ds(j * LU + LP, LU - LP)].unsqueeze(2).to_broadcast([LC, LU - LP, NLO]),
                                    ALU.is_equal).then_inc(hi_s, 1)

                def merge(j, b):
                    c = Chain(v, lp, 5 * j)
                    v.wait_ge(mm, j + 1)
                    c(v.tensor_scalar(vi[:, :], pp[b][:, 0:NLO].bitcast(I32), 26, None, ALU.logical_shift_right))
                    c(v.tensor_scalar(nf[:, :], vi[:, :], 0.0, None, ALU.is_equal))
                    c(v.tensor_scalar(T1[:, :], T[:, :], float(LU), None, ALU.subtract))
                    c(v.tensor_tensor(T1[:, :], T1[:, :], nf[:, :], ALU.mult))
                    c(v.tensor_tensor(T[:, :], T1[:, :], vi[:, :], ALU.add))

                build(0, 0)
                with v.Fori(0, groups // 2 - 1) as i:
                    build(2 * i + 1, 1)
                    merge(2 * i, 0)
                    build(2 * i + 2, 0)
                    merge(2 * i + 1, 1)
                build(groups - 1, 1)
                merge(groups - 2, 0)
                merge(groups - 1, 1)
                chain(v.tensor_scalar(T[:, :], T[:, :], float(LU * (groups - 1)), 0.0, ALU.add, ALU.max))
                v.sem_inc(fin, 1)
                v.wait_ge(back, 16)
                chain(v.tensor_scalar(m[:, :], chunk[:, :], 0.0, OOB, ALU.is_equal, ALU.mult))
                chain(v.scalar_tensor_tensor(out=num[:, :], in0=chunk[:, :], scalar=-1.0, in1=m[:, :],
                                             op0=ALU.add, op1=ALU.add))
                v.tensor_copy(ci2[:, :], num[:, :]).then_inc(ready, 1)
                v.wait_ge(io, 1)
                v.wait_ge(gat, 16 * RT)
                pki, pk2i = pk.bitcast(I32), pk2.bitcast(I32)
                chain(v.tensor_scalar(pk2i, pki, 8191, None, ALU.bitwise_and))
                chain(v.tensor_scalar(pki, pki, 13, None, ALU.logical_shift_right))
                for t in range(RT):
                    ins = v.scalar_tensor_tensor(out=pk2[:, t, :], in0=pk2i[:, t, :], scalar=env["node"][:, t:t + 1],
                                                 in1=pki[:, t, :], op0=ALU.is_equal, op1=ALU.mult)
                    ins.then_inc(cp, 1)
                v.wait_ge(cp, LG + RT)
                chain(v.memset(num[:, :], OOB))
                chain(v.tensor_reduce(num[:, 0:RT], pk2, AX.X, ALU.max))
                chain(v.tensor_tensor(num[:, :], num[:, :], m[:, :], ALU.add))
                chain(v.tensor_copy(env["last_dst"][:, :], num[:, :]))

            @block.gpsimd
            def _(pool):
                pool.iota(env["node"][:, :], pattern=[[P, NT]], base=0, channel_multiplier=1,
                          allow_small_or_imprecise_dtypes=True).then_inc(io, 1)
                pool.wait_ge(cols, 1)

                def build(j, b):
                    wait(pool, mm, j - 1)
                    pool.sem_inc(go, 1)
                    pool.tensor_copy(rlo[:, b, :], clo[:, bass.ds(j * LU, LP)]).then_inc(staged, 1)
                    pool.wait_ge(staged, j + 1)
                    pool.sem_inc(go, 1)
                    for k in range(LP):
                        pool.tensor_scalar(ohl[:, b, k, :], env["iota"][0:LC, 0:NLO], rlo[:, b, k:k + 1], None,
                                           ALU.is_equal).then_inc(lo_s, 1)
                build(0, 0)
                build(1, 1)
                with pool.Fori(1, groups // 2) as i:
                    build(2 * i, 0)
                    build(2 * i + 1, 1)
                lim = pool.to_reg(LCH - 1)
                pool.wait_ge(z, 2)
                pool.wait_ge(ready, 1)
                for t in range(RT):
                    pool.indirect_dma_start(out=pk.bitcast(I32)[:, t, :], out_offset=None,
                                            in_=env["pack_d"].rearrange("(c e) -> c e", e=LC),
                                            in_offset=bass.IndirectOffsetOnAxis(ap=ci2[:, t:t + 1], axis=0),
                                            bounds_check=lim, oob_is_err=False).then_inc(gat, 16)
                pool.wait_ge(gat, 16 * RT)

            @block.tensor
            def _(pe):
                pe.wait_ge(cv, 1)
                for g in range(LG):
                    wait(pe, cp, g)
                    pe.transpose(pt[:, :], rf[:, g, :], env["ident"][:, :]).then_inc(tr, 1)

                def sums(j, b):
                    pe.wait_ge(hi_s, (LU + 1) * (j + 1))
                    pe.wait_ge(lo_s, LP * (j + 1))
                    wait(pe, lp, 5 * j - 9)
                    for k in range(LU):
                        last = pe.matmul(pp[b][:, 0:NLO], ohh[:, b, k, :], ohl[:, b, k, :], start=(k == 0),
                                         stop=(k == LU - 1))
                    last.then_inc(mm, 1)

                sums(0, 0)
                sums(1, 1)
                with pe.Fori(1, groups // 2) as i:
                    sums(2 * i, 0)
                    sums(2 * i + 1, 1)


class Scales:

    def __init__(self, env, ph):
        self.env = env
        self.var, self.mean, self.dif, self.std = (ph.sb(n, [P, NT]) for n in ("var", "mean", "dif", "std"))
        self.summed, self.rooted, self.link, self.ready = (
            ph.sem(n) for n in ("var_ready", "root_ready", "scales_link", "scales_ready"))

    def dve(self, v):
        s, c = self.env["stats"], Chain(v, self.link)
        rstd, nmr = self.env["rstd"], self.env["nmr"]
        c(v.tensor_tensor(self.mean[:, :], s[:, :, 1], s[:, :, 4], ALU.add))
        c(v.tensor_tensor(self.dif[:, :], s[:, :, 1], s[:, :, 4], ALU.subtract))
        c(v.tensor_tensor(self.var[:, :], s[:, :, 2], s[:, :, 5], ALU.add))
        c(v.scalar_tensor_tensor(out=self.dif[:, :], in0=self.dif[:, :], scalar=0.25, in1=self.dif[:, :],
                                 op0=ALU.mult, op1=ALU.mult))
        v.scalar_tensor_tensor(out=self.var[:, :], in0=self.var[:, :], scalar=1.0 / D, in1=self.dif[:, :],
                               op0=ALU.mult, op1=ALU.add).then_inc(self.summed, 1)
        v.wait_ge(self.rooted, 1)
        c(v.reciprocal(rstd[:, :], self.std[:, :]))
        c(v.scalar_tensor_tensor(out=nmr[:, :], in0=self.mean[:, :], scalar=-0.5, in1=rstd[:, :],
                                 op0=ALU.mult, op1=ALU.mult))
        v.sem_inc(self.ready, 1)

    def act(self, act):
        act.wait_ge(self.summed, 1)
        act.activation(self.std[:, :], self.var[:, :], ACT.Sqrt, bias=self.env["eps_c"][:, 0:1])\
            .then_inc(self.rooted, 1)
        act.wait_ge(self.ready, 1)


def normed(env, act, out, t):
    return act.activation(out, tile_of(env["X"], t), ACT.Relu, bias=env["nmr"][:, bass.ds(t, 1)],
                          scale=env["rstd"][:, bass.ds(t, 1)])


def first_norm(env):
    nc, X, Hh = env["nc"], env["X"], env["Hh"]
    with Phase(nc, "n0") as ph:
        sc = Scales(env, ph)
        hn, put, st = ph.sem("rows_done"), ph.sem("put"), ph.sem("stats")
        with nc.Block() as block:
            @block.vector
            def _(v):
                with v.Fori(0, NT // 10) as j:
                    for u in range(10):
                        v.bn_stats(tile_of(env["stats"], 10 * j + u), tile_of(X, 10 * j + u)).then_inc(st, 1)
                v.wait_ge(st, NT)
                sc.dve(v)

            @block.scalar
            def _(act):
                sc.act(act)
                with act.Fori(0, NT // 10) as j:
                    for u in range(10):
                        normed(env, act, tile_of(Hh, 10 * j + u), 10 * j + u).then_inc(hn, 1)

            @block.sync
            def _(sp):
                for c in range(0, NT, 10):
                    sp.wait_ge(hn, c + 10)
                    sp.dma_start(env["h_d"][c * P:(c + 10) * P, :].rearrange("(t p) d -> p t d", p=P),
                                 Hh[:, c:c + 10, :]).then_inc(put, 16)
                sp.wait_ge(put, 80)


def tile_of(a, t):
    return a[:, bass.ds(t, 1), :].rearrange("p a d -> p (a d)")


def flat(ap):
    return ap.rearrange("p k q -> p (k q)")


def load_rows(sp, sem, pairs):
    for t, a in pairs:
        sp.dma_start(t, a.rearrange("(a n) -> a n", a=1).partition_broadcast(P)).then_inc(sem, 16)


class Tile:

    def __init__(self, un, j, k):
        if k < 0:
            j, k = j - 1, k + un
        if k >= un:
            j, k = j + 1, k - un
        self.j, self.k, self.u, self.t, self.h = j, k, k % 2, un * j + k, (un // 2) * j + k // 2
        self.first = isinstance(j, int) and j == 0 and k == 0


class Dense:

    def __init__(self, env, name, width, kt=2, un=2):
        self.env, self.nc, self.kt, self.width, self.un = env, env["nc"], kt, width, un
        self.ph = ph = Phase(env["nc"], name)
        self.rows = ph.sb("rows", [P, 2, kt, P])
        self.rowsT = ph.sb("rowsT", [P, 2, kt, P])
        self.psT = [ph.ps(f"psT{i}", [P, kt, P]) for i in range(2)]
        self.psO = [ph.ps(f"psO{i}", [P, width]) for i in range(2)]
        self.rows_ready, self.transposed, self.copied, self.products, self.taken, self.mid_done, self.link = (
            ph.sem(n) for n in ("rows_ready", "transposed", "copied", "products", "taken", "mid_done", "link"))

    def turns(self, engine, step):
        un, n = self.un, NT // self.un

        def body(j, last=False):
            for k in range(un):
                step(Tile(un, j, k), min(2, un - 1 - k) if last else 2)
        body(0)
        with engine.Fori(1, n - 1) as j:
            body(j)
        body(n - 1, last=True)

    def pe(self, pe, weights):
        ident = self.env["ident"]

        def transpose(a):
            pe.wait_ge(self.rows_ready, a.t + 1)
            wait(pe, self.copied, a.t - 1)
            for k in range(self.kt):
                last = pe.transpose(self.psT[a.u][:, k, :], self.rows[:, a.u, k, :], ident[:, :])
            last.then_inc(self.transposed, 1)

        def product(a):
            pe.wait_ge(self.copied, a.t + 1)
            wait(pe, self.taken, a.t - 1)
            for k in range(self.kt):
                last = pe.matmul(self.psO[a.u][:, :], self.rowsT[:, a.u, k, :], weights(k), start=(k == 0),
                                 stop=(k == self.kt - 1))
            last.then_inc(self.products, 1)

        def step(a, left):
            if left:
                transpose(Tile(self.un, a.j, a.k + 1))
            product(a)
        transpose(Tile(self.un, 0, 0))
        self.turns(pe, step)

    def act(self, act, mid=None, pre=None):
        def do_pre(a):
            wait(act, self.transposed, a.t - 1)
            pre(a).then_inc(self.rows_ready, 1)

        def do_mid(a):
            act.wait_ge(self.taken, a.t + 1)
            mid(a).then_inc(self.mid_done, 1)

        def step(a, left):
            if pre and left == 2:
                do_pre(Tile(self.un, a.j, a.k + 2))
            act.wait_ge(self.transposed, a.t + 1)
            wait(act, self.products, a.t - 1)
            act.copy(self.rowsT[:, a.u, :, :], self.psT[a.u][:, :, :]).then_inc(self.copied, 1)
            if mid and not a.first:
                do_mid(Tile(self.un, a.j, a.k - 1))
            if mid and not left:
                do_mid(a)
        if pre:
            do_pre(Tile(self.un, 0, 0))
            do_pre(Tile(self.un, 0, 1))
        self.turns(act, step)

    def dve(self, v, pre, post, npre, npost, end=None, nend=0):
        n = npre + npost + nend

        def do_pre(a, base):
            if pre is None:
                return
            wait(v, self.transposed, a.t - 1)
            c = Chain(v, self.link, base)
            pre(a, c).then_inc(self.rows_ready, 1)
            assert c.n == npre, (c.n, npre)

        def do_end(a, base):
            v.wait_ge(self.mid_done, a.t + 1)
            c = Chain(v, self.link, base)
            end(a, c)
            assert c.n == nend, (c.n, nend)

        def step(a, left):
            base = 2 * npre if a.first else n * a.t + 2 * npre - nend
            if left == 2:
                do_pre(Tile(self.un, a.j, a.k + 2), base)
                base = base + npre
            if not left:
                base = base - npre
            v.wait_ge(self.products, a.t + 1)
            c = Chain(v, self.link, base)
            post(a, c).then_inc(self.taken, 1)
            assert c.n == npost, (c.n, npost)
            if end and not a.first:
                do_end(Tile(self.un, a.j, a.k - 1), base + npost)
            if end and not left:
                do_end(a, base + npost + nend)

        do_pre(Tile(self.un, 0, 0), 0)
        do_pre(Tile(self.un, 0, 1), npre)
        self.turns(v, step)


GL = 5


def group_loads(d, sp, ring, sems, source):
    def body(j):
        for half in range(2):
            wait(sp, d.taken, 2 * GL * j - (2 - half - 1) * GL)
            sp.dma_start(ring[:, half * GL:(half + 1) * GL, :],
                         source[bass.ds((2 * GL * j + half * GL) * P, GL * P), :].rearrange("(t p) d -> p t d", p=P))\
                .then_inc(sems[half], 16)
    body(0)
    with sp.Fori(1, NT // (2 * GL)) as j:
        body(j)


def tile_loads(d, sp, slots, sems, source):
    def body(j):
        for u in range(2):
            t = 2 * j + u
            wait(sp, d.taken, t - 1)
            sp.dma_start(slots[:, u, :], source[bass.ds(t * P, P), :]).then_inc(sems[u], 16)
    body(0)
    with sp.Fori(1, NT // 2) as j:
        body(j)


def tile_stores(d, sp, parts):
    with sp.Fori(0, NT // 2) as j:
        for u in range(2):
            t = 2 * j + u
            sp.wait_ge(d.taken, t + 1)
            for slots, sems, target in parts:
                sp.dma_start(target(t), slots[:, u, :]).then_inc(sems[u], 16)
    for _, sems, _ in parts:
        for s in sems:
            sp.wait_ge(s, 16 * NT // 2)


def layer0(env):
    nc, A, X, Hh = env["nc"], env["A"], env["X"], env["Hh"]
    first_norm(env)
    d = Dense(env, "l0", D, kt=4, un=2 * GL)
    with d.ph as ph:
        wn = ph.sb("wn", [P, 2, 4, P])
        wT = ph.sb("wT", [P, 4, D])
        bias = ph.sb("bias", [P, D])
        nring = ph.sb("nring", [P, 2 * GL], I32)
        ag = ph.sb("ag", [P, 2 * GL, D])
        res = ph.sb("res", [P, 2, D])
        pw = ph.ps("pw", [P, 4, P])
        ld, wt, wc, nr, go = (ph.sem(n) for n in ("loaded", "w_transposed", "w_copied", "ring", "go"))
        turn = ph.sem("turn")
        sc = Scales(env, ph)
        gs = [ph.sem(f"gathered{i}") for i in range(2 * GL)]
        with nc.Block() as block:
            @block.sync
            def _(sp):
                for a in range(2):
                    sp.dma_start(wn[:, a, :, :], A["L0_gnn_W"][a * P:(a + 1) * P, :].rearrange("p (k q) -> p k q", q=P))\
                        .then_inc(ld, 16)
                load_rows(sp, ld, [(bias[:, :], A["L0_gnn_b"])])

            @block.vector
            def _(v):
                v.wait_ge(ld, 48)
                for a in range(2):
                    v.wait_ge(wt, a + 1)
                    v.tensor_copy(wT[:, :, a * P:(a + 1) * P], pw[:, :, :]).then_inc(wc, 1)

                def pre(a, c):
                    t, u = a.t, a.u
                    c(v.tensor_copy(flat(d.rows[:, u, 0:2, :]), tile_of(Hh, t)))
                    v.wait_ge(gs[a.k], 16 * (a.j + 1))
                    return v.tensor_copy(flat(d.rows[:, u, 2:4, :]), ag[:, a.k, :])

                def post(a, c):
                    t, u, h = a.t, a.u, a.h
                    c(v.tensor_tensor(res[:, u, :], d.psO[u][:, :], bias[:, :], ALU.add))
                    c(v.tensor_tensor(tile_of(X, t), tile_of(X, t), res[:, u, :], ALU.add))
                    v.sem_inc(turn, 1)
                    return v.bn_stats(tile_of(env["stats"], t), tile_of(X, t))
                d.dve(v, pre, post, 1, 2)
                v.wait_ge(d.taken, NT)
                sc.dve(v)

            @block.tensor
            def _(pe):
                pe.wait_ge(ld, 48)
                for a in range(2):
                    wait(pe, wc, a)
                    for k in range(4):
                        last = pe.transpose(pw[:, k, :], wn[:, a, k, :], env["ident"][:, :])
                    last.then_inc(wt, 1)
                pe.wait_ge(wc, 2)
                d.pe(pe, lambda k: wT[:, k, :])

            @block.scalar
            def _(act):
                d.act(act)
                sc.act(act)

            @block.gpsimd
            def _(pool):
                lim_n = pool.to_reg(N - 1)

                def body(j):
                    for half in range(2):
                        a, b = half * GL, (half + 1) * GL
                        wait(pool, d.rows_ready, 2 * GL * (j - 1) + b)
                        pool.sem_inc(go, 1)
                        pool.memset(ag[:, a:b, :], 0.0).then_inc(nr, 1)
                        pool.tensor_copy(nring[:, a:b], env["last_dst"][:, bass.ds(2 * GL * j + a, GL)])\
                            .then_inc(nr, 1)
                        pool.wait_ge(nr, 4 * j + 2 * half + 2)
                        pool.sem_inc(go, 1)
                        for k in range(a, b):
                            pool.indirect_dma_start(out=ag[:, k, :], out_offset=None, in_=env["h_d"][:, :],
                                                    in_offset=bass.IndirectOffsetOnAxis(ap=nring[:, k:k + 1], axis=0),
                                                    bounds_check=lim_n, oob_is_err=False).then_inc(gs[k], 16)
                body(0)
                with pool.Fori(1, NT // (2 * GL)) as j:
                    body(j)


def layer1_tables(env):
    nc, A = env["nc"], env["A"]
    q = R // 2
    with Phase(nc, "t1") as ph:
        w = ph.sb("w", [P, 2, R * D])
        rows, rowsT = ph.sb("rows", [P, 2, 2, P]), ph.sb("rowsT", [P, 2, 2, P])
        o = ph.sb("o", [P, 2, q * D])
        psT = [ph.ps(f"psT{i}", [P, 512]) for i in range(2)]
        psO = [ph.ps(f"psO{i}", [P, q * D]) for i in range(2)]
        ld, ready, trn, cpy = ph.sem("loaded"), ph.sem("rows_ready"), ph.sem("transposed"), ph.sem("copied")
        mm = [ph.sem(f"products{i}") for i in range(2)]
        out = [ph.sem(f"out{i}") for i in range(2)]
        st = [ph.sem(f"stored{i}") for i in range(2)]
        view = env["rel_t"].rearrange("(n r) d -> n (r d)", r=R)
        with nc.Block() as block:
            @block.sync
            def _(sp):
                for r in range(R):
                    sp.dma_start(w[:, :, r * D:(r + 1) * D],
                                 A["L1_gnn_W_rel"][r, :, :].rearrange("(k p) o -> p k o", p=P)).then_inc(ld, 16)
                with sp.Fori(0, NT) as t:
                    for s in range(2):
                        sp.wait_ge(out[s], t + 1)
                        sp.dma_start(view[bass.ds(t * P, P), s * q * D:(s + 1) * q * D], o[:, s, :]).then_inc(st[s], 16)
                for s in range(2):
                    sp.wait_ge(st[s], 16 * NT)

            @block.vector
            def _(v):
                def body(t):
                    v.wait_ge(mm[0], t + 1)
                    wait(v, st[0], 16 * t)
                    v.tensor_copy(o[:, 0, :], psO[0][:, :]).then_inc(out[0], 1)
                body(0)
                with v.Fori(1, NT) as t:
                    body(t)

            @block.tensor
            def _(pe):
                pe.wait_ge(ld, 16 * R)

                def transpose(t, u):
                    pe.wait_ge(ready, t + 1)
                    wait(pe, cpy, t - 1)
                    for k in range(2):
                        last = pe.transpose(psT[u][:, k * P:(k + 1) * P], rows[:, u, k, :], env["ident"][:, :])
                    last.then_inc(trn, 1)

                def product(t, u):
                    pe.wait_ge(cpy, t + 1)
                    for s in range(2):
                        wait(pe, out[s], t)
                        for a in range(s * q * D, (s + 1) * q * D, 512):
                            for k in range(2):
                                last = pe.matmul(psO[s][:, a - s * q * D:a - s * q * D + 512], rowsT[:, u, k, :],
                                                 w[:, k, a:a + 512], start=(k == 0), stop=(k == 1))
                        last.then_inc(mm[s], 1)

                def body(j):
                    transpose(2 * j + 1, 1)
                    product(2 * j, 0)
                    transpose(2 * j + 2, 0)
                    product(2 * j + 1, 1)
                transpose(0, 0)
                body(0)
                with pe.Fori(1, NT // 2 - 1) as j:
                    body(j)
                transpose(NT - 1, 1)
                product(NT - 2, 0)
                product(NT - 1, 1)

            @block.scalar
            def _(act):
                def norm(t, u):
                    wait(act, trn, t - 1)
                    normed(env, act, flat(rows[:, u, :, :]), t).then_inc(ready, 1)

                def copy(t, u):
                    act.wait_ge(trn, t + 1)
                    wait(act, mm[1], t - 1)
                    act.copy(flat(rowsT[:, u, :, :]), psT[u][:, 0:2 * P]).then_inc(cpy, 1)

                def half(t):
                    act.wait_ge(mm[1], t + 1)
                    wait(act, st[1], 16 * t)
                    act.copy(o[:, 1, :], psO[1][:, :]).then_inc(out[1], 1)

                def body(j):
                    for u in range(2):
                        t = 2 * j + u
                        norm(t + 2, u)
                        copy(t + 1, 1 - u)
                        half(t)
                norm(0, 0)
                norm(1, 1)
                copy(0, 0)
                body(0)
                with act.Fori(1, NT // 2 - 1) as j:
                    body(j)
                copy(NT - 1, 1)
                half(NT - 2)
                half(NT - 1)


def layer1_end(env):
    nc, A, X, Hh = env["nc"], env["A"], env["X"], env["Hh"]
    stats = env["stats"]
    d = Dense(env, "e1", D)
    with d.ph as ph:
        w = ph.sb("w", [P, 2, D])
        bias, gam, bet = ph.sb("bias", [P, D]), ph.sb("gam", [P, D]), ph.sb("bet", [P, D])
        ag = ph.sb("ag", [P, 2, D])
        cv, gl, y = ph.sb("cv", [P, 2, D]), ph.sb("gl", [P, 2, D]), ph.sb("y", [P, 2 * GL, D])
        ld, fin, turn, yr, yu, xa = (ph.sem(n) for n in ("loaded", "stats_in", "turn", "y_ready", "y_used", "x_beta"))
        lk2 = ph.sem("link2")
        got = [ph.sem(f"got{i}") for i in range(2)]
        sc = Scales(env, ph)
        with nc.Block() as block:
            @block.sync
            def _(sp):
                sp.dma_start(w[:, :, :], A["L1_gnn_W_root"].rearrange("(k p) o -> p k o", p=P)).then_inc(ld, 16)
                load_rows(sp, ld, [(bias[:, :], A["L1_gnn_bias"]), (gam[:, :], A["L1_gnn_ln_gamma"]),
                                   (bet[:, :], A["L1_gnn_ln_beta"])])
                tile_loads(d, sp, ag, got, env["agg_d"][0])

            @block.vector
            def _(v):
                v.wait_ge(ld, 64)

                def post(a, c):
                    t, u, h = a.t, a.u, a.h
                    v.wait_ge(got[u], 16 * (h + 1))
                    c(v.tensor_tensor(y[:, u, :], ag[:, u, :], bias[:, :], ALU.add))
                    return v.tensor_tensor(cv[:, u, :], d.psO[u][:, :], y[:, u, :], ALU.add)

                def end(a, c):
                    t, u = a.t, a.u
                    c(v.tensor_tensor(tile_of(Hh, t), tile_of(Hh, t), gl[:, u, :], ALU.add))
                    v.sem_inc(turn, 1)
                    v.bn_stats(tile_of(stats, t), tile_of(Hh, t)).then_inc(fin, 1)
                d.dve(v, None, post, 0, 1, end, 1)
                v.wait_ge(fin, NT)
                sc.dve(v)
                v.wait_ge(xa, NT)

                def update(g, half):
                    c = Chain(v, lk2, 2 * g)
                    yg = y[:, half * GL:(half + 1) * GL, :]
                    xg = X[:, bass.ds(GL * g, GL), :]
                    v.wait_ge(yr, g + 1)
                    c(v.tensor_tensor(yg, yg, gam[:, :].unsqueeze(1).to_broadcast([P, GL, D]), ALU.mult))
                    c(v.tensor_tensor(xg, xg, yg, ALU.add))
                    v.sem_inc(turn, 1)
                    for k in range(GL):
                        v.bn_stats(tile_of(stats, GL * g + k), tile_of(X, GL * g + k)).then_inc(fin, 1)
                with v.Fori(0, NT // (2 * GL)) as j:
                    for half in range(2):
                        update(2 * j + half, half)
                v.wait_ge(fin, 2 * NT)

            @block.tensor
            def _(pe):
                pe.wait_ge(ld, 64)
                d.pe(pe, lambda k: w[:, k, :])

            @block.gpsimd
            def _(pool):
                pool.wait_ge(ld, 64)

                def body(t):
                    pool.wait_ge(d.rows_ready, t + 1)
                    pool.tensor_tensor(tile_of(X, t), tile_of(X, t), bet[:, :], ALU.add).then_inc(xa, 1)
                with pool.Fori(0, NT) as t:
                    body(t)

            @block.scalar
            def _(act):
                def pre(a):
                    normed(env, act, tile_of(Hh, a.t), a.t)
                    return normed(env, act, flat(d.rows[:, a.u, :, :]), a.t)
                d.act(act, lambda a: act.activation(gl[:, a.u, :], cv[:, a.u, :], ACT.Gelu), pre)
                sc.act(act)

                def rows(g, half):
                    wait(act, lk2, 2 * g - 2)
                    for k in range(GL):
                        t = GL * g + k
                        last = act.activation(y[:, half * GL + k, :], tile_of(Hh, t), ACT.Identity,
                                              bias=env["nmr"][:, bass.ds(t, 1)], scale=env["rstd"][:, bass.ds(t, 1)])
                    last.then_inc(yr, 1)
                rows(0, 0)
                rows(1, 1)
                with act.Fori(1, NT // (2 * GL)) as j:
                    for half in range(2):
                        rows(2 * j + half, half)
    next_scales(env, "s2")


def next_scales(env, name):
    nc = env["nc"]
    with Phase(nc, name) as ph:
        sc = Scales(env, ph)
        with nc.Block() as block:
            @block.vector
            def _(v):
                sc.dve(v)

            @block.scalar
            def _(act):
                sc.act(act)


def layer2_tables(env):
    nc, A, X, Hh = env["nc"], env["A"], env["X"], env["Hh"]
    d = Dense(env, "t2", D)
    with d.ph as ph:
        w = ph.sb("w", [P, 2, D])
        att = ph.sb("att", [P, H, 2 * F])
        o = ph.sb("o", [P, 2, H * (F + 1)])
        es = ph.sb("es", [P, 2, H])
        pr = ph.sb("pr", [P, 2, 2, D])
        ld, ones = ph.sem("loaded"), ph.sem("ones")
        st = [ph.sem(f"stored{i}") for i in range(2)]
        sa = [ph.sem(f"stored_att{i}") for i in range(2)]
        heads = lambda ap, n=F: ap.rearrange("p (h f) -> p h f", f=n)
        with nc.Block() as block:
            @block.sync
            def _(sp):
                for h in range(H):
                    sp.dma_start(w[:, :, h * F:(h + 1) * F], A["L2_gnn_W"][h, :, :].rearrange("(k p) f -> p k f", p=P))\
                        .then_inc(ld, 16)
                sp.dma_start(att[:, :, :].rearrange("p h f -> p (h f)"),
                             A["L2_gnn_att"].rearrange("h f -> (h f)").rearrange("(a n) -> a n", a=1)
                             .partition_broadcast(P)).then_inc(ld, 16)
                sp.wait_ge(ld, 80)
                tile_stores(d, sp, [(o, st, lambda t: env["z_t"][bass.ds(t * P, P), :]),
                                    (es, sa, lambda t: env["es_t"][bass.ds(t * P, P), :])])

            @block.vector
            def _(v):
                v.memset(o[:, :, :], 1.0).then_inc(ones, 1)
                v.memset(env["ed_sb"][:, :], 1.0).then_inc(ones, 1)
                v.wait_ge(ones, 2)
                v.wait_ge(ld, 80)

                def post(a, c):
                    t, u, h = a.t, a.u, a.h
                    wait(v, st[u], 16 * h)
                    wait(v, sa[u], 16 * h)
                    z = heads(d.psO[u][:, :])
                    c(v.tensor_copy(heads(o[:, u, :], F + 1)[:, :, 0:F], z))
                    for k in range(2):
                        c(v.tensor_tensor(heads(pr[:, u, k, :]), z, att[:, :, k * F:(k + 1) * F], ALU.mult))
                    c(v.tensor_reduce(env["ed_sb"][:, bass.ds(t * (H + 1), H)], heads(pr[:, u, 1, :]), AX.X, ALU.add))
                    return v.tensor_reduce(es[:, u, :], heads(pr[:, u, 0, :]), AX.X, ALU.add)
                d.dve(v, None, post, 0, 4)

            @block.tensor
            def _(pe):
                pe.wait_ge(ld, 80)
                d.pe(pe, lambda k: w[:, k, :])

            @block.scalar
            def _(act):
                d.act(act, pre=lambda a: normed(env, act, flat(d.rows[:, a.u, :, :]), a.t))


SB = 8
SBL = ITEMS // SB


def edge_scores(env):
    nc = env["nc"]
    W = H + 1
    with Phase(nc, "es") as ph:
        drow = ph.sb("drow", [P, 2, SB * P])
        sel = ph.sb("sel", [P, 2, SB * P])
        pidx = ph.sb("pidx", [P, 1])
        ring = ph.sb("ring", [P, 2, SB], I32)
        g = ph.sb("g", [P, 2, SB, H])
        x, y, z = ph.sb("x", [P, SB, H]), ph.sb("y", [P, SB, H]), ph.sb("z", [P, SB, H])
        pen = ph.sb("pen", [P, SB])
        e = ph.sb("e", [P, 2, H, SB])
        eT = ph.sb("eT", [H * SB, 2, P])
        pd = [ph.ps(f"pd{i}", [P, SB, W]) for i in range(2)]
        pt = [ph.ps(f"pt{i}", [H * SB, P]) for i in range(2)]
        cst, go, staged, lk, sc, trn, cpy, sl, lu = (ph.sem(n) for n in (
            "const", "go", "staged", "link", "scores", "transposed", "copied", "selections", "looked_up"))
        gs = [ph.sem(f"gathered{i}") for i in range(2)]
        st = [ph.sem(f"stored{i}") for i in range(2)]
        rl = [ph.sem(f"rows_loaded{i}") for i in range(2)]
        with nc.Block() as block:
            @block.sync
            def _(sp):
                flat_dst = env["item_ldst_d"].rearrange("c e -> (c e)").rearrange("(a n) -> a n", a=1)

                def load(j, b):
                    wait(sp, sl, j - 1)
                    sp.dma_start(drow[:, b, :], flat_dst[:, bass.ds(j * SB * P, SB * P)].partition_broadcast(P))\
                        .then_inc(rl[b], 16)

                def store(j, b):
                    sp.wait_ge(cpy, j + 1)
                    for h in range(H):
                        sp.dma_start(env["sc_d"][h][bass.ds(j * SB, SB), :], eT[h * SB:(h + 1) * SB, b, :])\
                            .then_inc(st[b], 16)
                load(0, 0)
                load(1, 1)
                with sp.Fori(0, SBL // 2 - 1) as i:
                    for b in range(2):
                        load(2 * i + b + 2, b)
                        store(2 * i + b, b)
                for b in range(2):
                    store(SBL - 2 + b, b)
                for b in range(2):
                    sp.wait_ge(st[b], 16 * H * SBL // 2)

            @block.vector
            def _(v):
                v.memset(g[:, :, :, :], 0.0).then_inc(cst, 1)
                v.wait_ge(cst, 2)

                def select(j, b, i):
                    v.wait_ge(rl[b], 16 * (i + 1))
                    wait(v, lu, j - 1)
                    v.tensor_scalar(sel[:, b, :], drow[:, b, :], pidx[:, 0:1], None, ALU.is_equal).then_inc(sl, 1)

                def score(j, b, i):
                    v.wait_ge(gs[b], 16 * SB * (i + 1))
                    v.wait_ge(lu, j + 1)
                    c = Chain(v, lk, 5 * j)
                    c(v.tensor_tensor(x[:, :, :], pd[b][:, :, 0:H], g[:, b, :, :], ALU.add))
                    c(v.tensor_scalar(pen[:, :], pd[b][:, :, H], BIG, -BIG, ALU.mult, ALU.add))
                    xf = flat(x[:, :, :])
                    c(v.scalar_tensor_tensor(out=flat(y[:, :, :]), in0=xf, scalar=0.01, in1=xf, op0=ALU.mult,
                                             op1=ALU.max))
                    c(v.tensor_scalar(z[:, :, :], y[:, :, :], 0.0, -1000.0, ALU.is_equal, ALU.mult))
                    c(v.tensor_tensor(z[:, :, :], z[:, :, :], pen[:, :].unsqueeze(2).to_broadcast([P, SB, H]), ALU.add))
                    wait(v, trn, j - 1)
                    v.tensor_tensor(e[:, b, :, :].rearrange("p h s -> p s h"), y[:, :, :], z[:, :, :],
                                    ALU.add).then_inc(sc, 1)
                    v.wait_ge(sc, j + 1)
                select(0, 0, 0)

                def body(i):
                    select(2 * i + 1, 1, i)
                    score(2 * i, 0, i)
                    select(2 * i + 2, 0, i + 1)
                    score(2 * i + 1, 1, i)
                body(0)
                with v.Fori(1, SBL // 2 - 1) as i:
                    body(i)
                i = SBL // 2 - 1
                select(2 * i + 1, 1, i)
                score(2 * i, 0, i)
                score(2 * i + 1, 1, i)

            @block.tensor
            def _(pe):
                def look(j, b):
                    pe.wait_ge(sl, j + 1)
                    wait(pe, sc, j - 1)
                    for k in range(SB):
                        t = pe.value_load(env["item_tile"][0:1, bass.ds(j * SB + k, 1)], min_val=0, max_val=NT - 1)
                        last = pe.matmul(pd[b][:, k, :], sel[:, b, k * P:(k + 1) * P],
                                         env["ed_sb"][:, bass.ds(t * W, W)], start=True, stop=True)
                    last.then_inc(lu, 1)

                def turn(j, b):
                    pe.wait_ge(sc, j + 1)
                    wait(pe, cpy, j - 1)
                    pe.transpose(pt[b][:, :], e[:, b, :, :].rearrange("p h s -> p (h s)"), env["ident"][:, :])\
                        .then_inc(trn, 1)
                look(0, 0)

                def body(i):
                    look(2 * i + 1, 1)
                    turn(2 * i, 0)
                    look(2 * i + 2, 0)
                    turn(2 * i + 1, 1)
                body(0)
                with pe.Fori(1, SBL // 2 - 1) as i:
                    body(i)
                i = SBL // 2 - 1
                look(2 * i + 1, 1)
                turn(2 * i, 0)
                turn(2 * i + 1, 1)

            @block.scalar
            def _(act):
                def stage(j, b):
                    wait(act, sc, j - 1)
                    act.copy(ring[:, b, :], env["item_src"][:, bass.ds(j * SB, SB)]).then_inc(staged, 1)

                def copy(j, b, i):
                    act.wait_ge(trn, j + 1)
                    wait(act, st[b], 16 * H * i)
                    act.copy(eT[:, b, :], pt[b][:, :]).then_inc(cpy, 1)
                stage(0, 0)
                stage(1, 1)

                def body(i):
                    for b in range(2):
                        stage(2 * i + b + 2, b)
                        copy(2 * i + b, b, i)
                body(0)
                with act.Fori(1, SBL // 2 - 1) as i:
                    body(i)
                for b in range(2):
                    copy(SBL - 2 + b, b, SBL // 2 - 1)

            @block.gpsimd
            def _(pool):
                lim = pool.to_reg(N - 1)
                pool.iota(pidx[:, :], pattern=[[0, 1]], base=0, channel_multiplier=1,
                          allow_small_or_imprecise_dtypes=True).then_inc(cst, 1)
                pool.wait_ge(cst, 2)
                with pool.Fori(0, SBL // 2) as i:
                    for b in range(2):
                        pool.wait_ge(staged, 2 * i + b + 1)
                        pool.sem_inc(go, 1)
                        for k in range(SB):
                            pool.indirect_dma_start(
                                out=g[:, b, k, :], out_offset=None, in_=env["es_t"][:, :],
                                in_offset=bass.IndirectOffsetOnAxis(ap=ring[:, b, k:k + 1], axis=0),
                                bounds_check=lim, oob_is_err=False).then_inc(gs[b], 16)


def softmax(env):
    nc = env["nc"]
    with Phase(nc, "sm") as ph:
        b = scan_buffers(env, ph, ITEMS, 3)
        loaded, again, tot, sub, ex, put = (ph.sem(n) for n in ("loaded", "again", "maxima", "shifted", "exps", "put"))
        scan_flags(env, b, env["item_gdst_d"])
        view = lambda h: env["sc_d"][h]
        with nc.Block() as block:
            @block.sync
            def _(sp):
                for h in range(H):
                    sp.dma_start(b["val"][:, h, :], scan_view(view(h))).then_inc(loaded, 16)
                sp.wait_ge(tot, 1)
                for h in range(H):
                    sp.dma_start(b["run"][:, h, :], scan_view(view(h))).then_inc(again, 16)
                for h in range(H):
                    sp.wait_ge(ex, h + 1)
                    sp.dma_start(scan_view(env["ex_d"][h]), b["run"][:, h, :]).then_inc(put, 16)
                sp.wait_ge(put, 64)

            @block.vector
            def _(v):
                chain = Chain(v, b["dve"], b["n"])
                v.wait_ge(loaded, 64)
                seg_forward(v, chain, b, H, ALU.add, b["st"], ALU.max, -BIG)
                seg_backward(v, chain, b, H)
                v.sem_inc(tot, 1)
                v.wait_ge(again, 64)
                for h in range(H):
                    v.tensor_tensor(b["run"][:, h, :], b["run"][:, h, :], b["val"][:, h, :], ALU.subtract).then_inc(sub, 1)

            @block.tensor
            def _(pe):
                for _ in range(2):
                    seg_carry(pe, b, H)

            @block.scalar
            def _(act):
                for h in range(H):
                    act.wait_ge(sub, h + 1)
                    act.activation(b["run"][:, h, :], b["run"][:, h, :], ACT.Exp).then_inc(ex, 1)


def ex_columns(env):
    return env["Hh"][:, :, :].rearrange("p t d -> p (t d)")[:, 0:H * IG * P].rearrange("p (h i) -> p h i", h=H)


def score_items(env):
    nc = env["nc"]
    with Phase(nc, "si") as ph:
        rows = ph.sb("rows", [P, IG, H, P])
        pt = ph.ps("pt", [P, H, P])
        gat, tr, cp, z = ph.sem("loaded"), ph.sem("transposed"), ph.sem("copied"), ph.sem("zeroed")
        with nc.Block() as block:
            @block.sync
            def _(sp):
                full = (IG - 1) * P
                sp.wait_ge(z, 1)
                for h in range(H):
                    sp.dma_start(rows[:, 0:IG - 1, h, :], env["ex_d"][h][0:full, :].rearrange("(g p) e -> p g e", p=P))\
                        .then_inc(gat, 16)
                    sp.dma_start(rows[0:ITEMS - full, IG - 1, h, :], env["ex_d"][h][full:ITEMS, :]).then_inc(gat, 16)

            @block.tensor
            def _(pe):
                pe.wait_ge(gat, 32 * H)
                for g in range(IG):
                    wait(pe, cp, g)
                    for h in range(H):
                        last = pe.transpose(pt[:, h, :], rows[:, g, h, :], env["ident"][:, :])
                    last.then_inc(tr, 1)

            @block.vector
            def _(v):
                v.memset(rows[:, IG - 1, :, :], 0.0).then_inc(z, 1)
                for g in range(IG):
                    v.wait_ge(tr, g + 1)
                    v.tensor_copy(ex_columns(env)[:, :, g * P:(g + 1) * P], pt[:, :, :]).then_inc(cp, 1)
                v.wait_ge(cp, IG)


LAG = 4
NS = 8


def aggregate(env, name, layer, table, W, limit, idx, weight):
    nc = env["nc"]
    target = env["agg_d"][layer]
    per_head = weight == "ex"
    with Phase(nc, name) as ph:
        G = ph.sb("G", [P, U, W])
        S = ph.sb("S", [P, NS, P])
        acc = ph.sb("acc", [P, U, W])
        gw = ph.sb("gw", [P, NS, W]) if per_head else None
        r_idx = ph.sb("r_idx", [P, U], I32)
        r_dst, r_wgt, r_keep = (ph.sb(n, [P, U]) for n in ("r_dst", "r_wgt", "r_keep"))
        r_ex = ph.sb("r_ex", [P, H, U]) if per_head else None
        ps = [ph.ps(f"ps{i}", [P, W]) for i in range(NS)]
        staged, go, built, products, added, cleared = (ph.sem(n) for n in (
            "staged", "go", "selections", "products", "added", "cleared"))
        gs = [ph.sem(f"gathered{k}") for k in range(U)]
        st = [ph.sem(f"stored{k}") for k in range(U)]
        HU = U // 2
        with nc.Block() as block:
            @block.gpsimd
            def _(pool):
                lim = pool.to_reg(limit)
                pool.memset(G[:, :, :], 0.0).then_inc(cleared, 1)
                pool.wait_ge(cleared, 2)
                with pool.Fori(0, ITEMS // U) as j:
                    for half in range(2):
                        pool.wait_ge(staged, 2 * j + half + 1)
                        pool.sem_inc(go, 1)
                        for k in range(half * HU, (half + 1) * HU):
                            pool.indirect_dma_start(out=G[:, k, :], out_offset=None, in_=table[:, :],
                                                    in_offset=bass.IndirectOffsetOnAxis(ap=r_idx[:, k:k + 1], axis=0),
                                                    bounds_check=lim, oob_is_err=False).then_inc(gs[k], 16)

            @block.scalar
            def _(act):
                def body(j):
                    for half in range(2):
                        a, b = half * HU, (half + 1) * HU
                        wait(act, added, U * (j - 1) + b)
                        s = bass.ds(j * U + a, HU)
                        act.copy(r_dst[:, a:b], env["item_dst"][:, s])
                        act.copy(r_keep[:, a:b], env["item_keep"][:, s])
                        if weight == "wgt":
                            act.copy(r_wgt[:, a:b], env["item_wgt"][:, s])
                        if per_head:
                            act.copy(r_ex[:, :, a:b], ex_columns(env)[:, :, s])
                        act.copy(r_idx[:, a:b], idx[:, s]).then_inc(staged, 1)
                body(0)
                with act.Fori(1, ITEMS // U) as j:
                    body(j)

            @block.vector
            def _(v):
                v.memset(acc[:, U - 1, :], 0.0).then_inc(cleared, 1)
                v.wait_ge(cleared, 2)

                def select(i, k, j):
                    if k % HU == 0:
                        v.wait_ge(staged, 2 * j + k // HU + 1)
                    wait(v, products, i - NS + 1)
                    if per_head:
                        v.wait_ge(gs[k], 16 * (j + 1))
                        v.tensor_tensor(gw[:, k % NS, :].rearrange("p (h f) -> p h f", h=H),
                                        G[:, k, :].rearrange("p (h f) -> p h f", h=H),
                                        r_ex[:, :, k:k + 1].to_broadcast([P, H, F + 1]), ALU.mult).then_inc(built, 1)
                    if weight == "wgt":
                        v.tensor_scalar(S[:, k % NS, :], env["iota"][:, :], r_dst[:, k:k + 1], r_wgt[:, k:k + 1],
                                        ALU.is_equal, ALU.mult).then_inc(built, 1)
                    else:
                        v.tensor_scalar(S[:, k % NS, :], env["iota"][:, :], r_dst[:, k:k + 1], None,
                                        ALU.is_equal).then_inc(built, 1)

                def add(i, k, h):
                    v.wait_ge(products, i + 1)
                    wait(v, added, i)
                    wait(v, st[k], 16 * h)
                    v.scalar_tensor_tensor(out=acc[:, k, :], in0=acc[:, (k - 1) % U, :], scalar=r_keep[:, k:k + 1],
                                           in1=ps[k % NS][:, :], op0=ALU.mult, op1=ALU.add).then_inc(added, 1)

                def body(j):
                    for k in range(U):
                        select(U * j + k, k, j)
                        if k >= LAG:
                            add(U * j + k - LAG, k - LAG, j)
                        elif not isinstance(j, int):
                            add(U * j + k - LAG, U + k - LAG, j - 1)
                body(0)
                with v.Fori(1, ITEMS // U) as j:
                    body(j)
                for k in range(U - LAG, U):
                    add(ITEMS - U + k, k, ITEMS // U - 1)

            @block.tensor
            def _(pe):
                n = 2 if per_head else 1

                def body(j):
                    for k in range(U):
                        i = U * j + k
                        pe.wait_ge(built, n * (i + 1))
                        if not per_head:
                            pe.wait_ge(gs[k], 16 * (j + 1))
                        wait(pe, added, i - NS + 1)
                        pe.matmul(ps[k % NS][:, :], S[:, k % NS, :], gw[:, k % NS, :] if per_head else G[:, k, :],
                                  start=True, stop=True).then_inc(products, 1)
                body(0)
                with pe.Fori(1, ITEMS // U) as j:
                    body(j)

            @block.sync
            def _(sp):
                with sp.Fori(0, ITEMS // U) as j:
                    for k in range(U):
                        i = U * j + k
                        row = sp.value_load(env["item_row"][0:1, bass.ds(i, 1)], min_val=0, max_val=NT - 1)
                        sp.wait_ge(added, i + 1)
                        sp.dma_start(target[bass.ds(row * P, P), :], acc[:, k, :], cond=row < RT).then_inc(st[k], 16)
                for k in range(U):
                    sp.wait_ge(st[k], 16 * ITEMS // U)


def add_attention(env):
    nc, X = env["nc"], env["X"]
    W = H * (F + 1)
    with Phase(nc, "aa") as ph:
        g = ph.sb("g", [P, 2, GL, W])
        den, rec, o = ph.sb("den", [P, GL, H]), ph.sb("rec", [P, GL, H]), ph.sb("o", [P, GL, D])
        link, turn, fin = ph.sem("link"), ph.sem("turn"), ph.sem("stats_in")
        sc = Scales(env, ph)
        got = [ph.sem(f"got{i}") for i in range(2)]
        with nc.Block() as block:
            @block.sync
            def _(sp):
                def load(n, b):
                    wait(sp, link, 8 * (n - 2) + 7)
                    sp.dma_start(g[:, b, :, :], env["agg_d"][1][bass.ds(n * GL * P, GL * P), :]
                                 .rearrange("(t p) d -> p t d", p=P)).then_inc(got[b], 16)
                load(0, 0)
                load(1, 1)
                with sp.Fori(1, NT // (2 * GL)) as j:
                    for b in range(2):
                        load(2 * j + b, b)

            @block.vector
            def _(v):
                with v.Fori(0, NT // (2 * GL)) as j:
                    for b in range(2):
                        n = 2 * j + b
                        v.wait_ge(got[b], 16 * (j + 1))
                        gh = g[:, b, :, :].rearrange("p t (h f) -> p t h f", h=H)
                        c = Chain(v, link, 8 * n)
                        c(v.tensor_scalar(den[:, :, :], gh[:, :, :, F], 0.0, None, ALU.is_le))
                        c(v.tensor_tensor(den[:, :, :], den[:, :, :], gh[:, :, :, F], ALU.add))
                        c(v.reciprocal(rec[:, :, :], den[:, :, :]))
                        for h in range(H):
                            v.tensor_tensor(o[:, :, h * F:(h + 1) * F], gh[:, :, h, 0:F],
                                            rec[:, :, h:h + 1].to_broadcast([P, GL, F]), ALU.mult).then_inc(link, 1)
                        v.wait_ge(link, 8 * n + 7)
                        xg = X[:, bass.ds(GL * n, GL), :]
                        v.tensor_tensor(xg, xg, o[:, :, :], ALU.add).then_inc(link, 1)
                        v.wait_ge(link, 8 * n + 8)
                        v.sem_inc(turn, 1)
                        for k in range(GL):
                            v.bn_stats(tile_of(env["stats"], GL * n + k), tile_of(X, GL * n + k)).then_inc(fin, 1)
                v.wait_ge(fin, NT)
                sc.dve(v)

            @block.scalar
            def _(act):
                sc.act(act)


def prelu(v, c, out, x, alpha, tmp):
    c(v.scalar_tensor_tensor(out=tmp, in0=x, scalar=0.0, in1=alpha, op0=ALU.min, op1=ALU.mult))
    return v.scalar_tensor_tensor(out=out, in0=x, scalar=0.0, in1=tmp, op0=ALU.max, op1=ALU.add)


def layer3_tables(env):
    nc, A, X, Hh = env["nc"], env["A"], env["X"], env["Hh"]
    d = Dense(env, "p3", D)
    with d.ph as ph:
        w = ph.sb("w", [P, 2, D])
        bias, alpha = ph.sb("bias", [P, D]), ph.sb("alpha", [P, D])
        x, tmp = ph.sb("x", [P, 2, D]), ph.sb("tmp", [P, 2, D])
        ld = ph.sem("loaded")
        with nc.Block() as block:
            @block.sync
            def _(sp):
                sp.dma_start(w[:, :, :], A["L3_gnn_W_pre"].rearrange("(k p) o -> p k o", p=P)).then_inc(ld, 16)
                load_rows(sp, ld, [(bias[:, :], A["L3_gnn_b_pre"]), (alpha[:, :], A["L3_gnn_alpha_pre"])])

            @block.vector
            def _(v):
                v.wait_ge(ld, 48)

                def post(a, c):
                    t, u, h = a.t, a.u, a.h
                    c(v.tensor_tensor(x[:, u, :], d.psO[u][:, :], bias[:, :], ALU.add))
                    return prelu(v, c, tile_of(Hh, t), x[:, u, :], alpha[:, :], tmp[:, u, :])
                d.dve(v, None, post, 0, 2)

            @block.tensor
            def _(pe):
                pe.wait_ge(ld, 48)
                d.pe(pe, lambda k: w[:, k, :])

            @block.scalar
            def _(act):
                d.act(act, pre=lambda a: normed(env, act, flat(d.rows[:, a.u, :, :]), a.t))
    d = Dense(env, "m3", D)
    with d.ph as ph:
        w = ph.sb("w", [P, 2, D])
        bias, o = ph.sb("bias", [P, D]), ph.sb("o", [P, 2, D])
        ld = ph.sem("loaded")
        st = [ph.sem(f"stored{i}") for i in range(2)]
        with nc.Block() as block:
            @block.sync
            def _(sp):
                sp.dma_start(w[:, :, :], A["L3_gnn_W_mp"].rearrange("(k p) o -> p k o", p=P)).then_inc(ld, 16)
                load_rows(sp, ld, [(bias[:, :], A["L3_gnn_b_mp"])])
                tile_stores(d, sp, [(o, st, lambda t: env["m_t"][bass.ds(t * P, P), :])])

            @block.vector
            def _(v):
                v.wait_ge(ld, 32)

                def post(a, c):
                    t, u, h = a.t, a.u, a.h
                    wait(v, st[u], 16 * h)
                    return v.tensor_tensor(o[:, u, :], d.psO[u][:, :], bias[:, :], ALU.add)
                d.dve(v, None, post, 0, 0)

            @block.tensor
            def _(pe):
                pe.wait_ge(ld, 32)
                d.pe(pe, lambda k: w[:, k, :])

            @block.scalar
            def _(act):
                d.act(act, pre=lambda a: act.copy(flat(d.rows[:, a.u, :, :]), tile_of(Hh, a.t)))


def layer3_end(env):
    nc, A, X, Hh = env["nc"], env["A"], env["X"], env["Hh"]
    d = Dense(env, "e3", D, un=2 * GL)
    with d.ph as ph:
        w = ph.sb("w", [P, 2, D])
        bias, alpha = ph.sb("bias", [P, D]), ph.sb("alpha", [P, D])
        ag = ph.sb("ag", [P, 2 * GL, D])
        tmp, r, x = ph.sb("tmp", [P, 2, D]), ph.sb("r", [P, 2, D]), ph.sb("x", [P, 2, D])
        ld, put = ph.sem("loaded"), ph.sem("put")
        got = [ph.sem(f"got{i}") for i in range(2)]
        with nc.Block() as block:
            @block.sync
            def _(sp):
                sp.dma_start(w[:, :, :], A["L3_gnn_W_post"].rearrange("(k p) o -> p k o", p=P)).then_inc(ld, 16)
                load_rows(sp, ld, [(bias[:, :], A["L3_gnn_b_post"]), (alpha[:, :], A["L3_gnn_alpha_mp"])])
                group_loads(d, sp, ag, got, env["agg_d"][2])

            @block.gpsimd
            def _(pool):
                for t in range(0, RT - 1, 12):
                    pool.wait_ge(d.taken, t + 12)
                    pool.dma_start(env["out"][t * P:(t + 12) * P, :].rearrange("(t p) d -> p t d", p=P),
                                 X[:, t:t + 12, :]).then_inc(put, 16)
                pool.wait_ge(d.taken, NT)
                pool.dma_start(env["out"][(RT - 1) * P:N, :], X[0:LAST, RT - 1, :]).then_inc(put, 16)
                pool.wait_ge(put, 80)

            @block.vector
            def _(v):
                v.wait_ge(ld, 48)

                def pre(a, c):
                    t, u = a.t, a.u
                    if a.k % GL == 0:
                        v.wait_ge(got[a.k // GL], 16 * (a.j + 1))
                    c(prelu(v, c, r[:, u, :], ag[:, a.k, :], alpha[:, :], tmp[:, u, :]))
                    return v.tensor_tensor(flat(d.rows[:, u, :, :]), tile_of(Hh, t), r[:, u, :], ALU.add)

                def post(a, c):
                    t, u, h = a.t, a.u, a.h
                    c(v.tensor_tensor(x[:, u, :], d.psO[u][:, :], bias[:, :], ALU.add))
                    return v.scalar_tensor_tensor(out=tile_of(X, t), in0=x[:, u, :], scalar=0.0, in1=tile_of(X, t),
                                                  op0=ALU.max, op1=ALU.add)
                d.dve(v, pre, post, 2, 1)

            @block.tensor
            def _(pe):
                pe.wait_ge(ld, 48)
                d.pe(pe, lambda k: w[:, k, :])

            @block.scalar
            def _(act):
                d.act(act)


_INS = ['x', 'src', 'dst', 'edge_type_8', 'L0_gnn_W', 'L0_gnn_b', 'L1_gnn_W_rel', 'L1_gnn_W_root', 'L1_gnn_bias',
        'L1_gnn_ln_gamma', 'L1_gnn_ln_beta', 'L2_gnn_W', 'L2_gnn_att', 'L3_gnn_W_pre', 'L3_gnn_b_pre',
        'L3_gnn_alpha_pre', 'L3_gnn_W_mp', 'L3_gnn_b_mp', 'L3_gnn_alpha_mp', 'L3_gnn_W_post', 'L3_gnn_b_post']


def kernel(**inputs):
    import numpy as _np
    import concourse.bacc as _bacc
    from concourse import mybir as _mybir
    from concourse.bass_utils import run_bass_kernel_spmd as _run

    nc = _bacc.Bacc("TRN2", target_bir_lowering=False, num_devices=1)
    arrays, args = {}, {}
    for name in _INS:
        a = _np.ascontiguousarray(inputs[name])
        arrays[f"in_{name}"] = a
        args[name] = nc.dram_tensor(f"in_{name}", a.shape, _mybir.dt.from_np(a.dtype), kind="ExternalInput").ap()
    out = nc.dram_tensor("out_x", (N, D), _mybir.dt.float32, kind="ExternalOutput").ap()
    build(nc, args, out)
    r = _run(nc, [arrays], core_ids=[0])
    return r.results[0]["out_x"]
```

```python
import concourse.bass as bass
from concourse import mybir
from contextlib import ExitStack

FP32 = mybir.dt.float32
BF16 = mybir.dt.bfloat16
I32 = mybir.dt.int32
ALU = mybir.AluOpType
ACT = mybir.ActivationFunctionType
AX = mybir.AxisListType

N, D, E = 6250, 256, 106250
R, H, F = 8, 4, 64
P = 128
NT = 50
NP = NT * P
RT = 49
LAST = N - (RT - 1) * P
CH = -(-E // P)
EP = CH * P
CG = -(-CH // P)
FULLP = E // CH
REST = E - FULLP * CH
U = 16
ITEMS = -(-(CH + RT - 1) // U) * U
IG = -(-ITEMS // P)
LC, LCH = 125, 850
LG = -(-LCH // P)
LU = 25
LP = 9
NHI, NLO = 98, 64
PADDST = 8191.0
OOB = 60000.0
BIG = 1.0e30
EPS = 1e-5


def wait(eng, sem, value):
    if isinstance(value, int) and value <= 0:
        return
    eng.wait_ge(sem, value)


class Chain:

    def __init__(self, eng, sem, base=0):
        self.eng, self.sem, self.base, self.n = eng, sem, base, 0

    def __call__(self, ins):
        self.n += 1
        ins.then_inc(self.sem, 1)
        self.eng.wait_ge(self.sem, self.base + self.n)


def build(nc, A, out):
    top = ExitStack()
    with top:
        def dram(name, shape, dt=FP32):
            return nc.dram_tensor(name, shape, dt).ap()

        dst_d = dram("dst_d", (CH, P))
        src_d = dram("src_d", (CH, P))
        rel_d = dram("rel_d", (CH, P))
        wgt_d = dram("wgt_d", (CH, P))
        item_gdst_d = dram("item_gdst_d", (ITEMS, P))
        item_ldst_d = dram("item_ldst_d", (ITEMS, P))
        link_d = dram("link_d", (ITEMS, P + 3))
        last_d = dram("last_d", (NHI * NLO,))
        pack_d = dram("pack_d", (E,), I32)
        item_d = dram("item_d", (4, IG * P))
        h_d = dram("h_d", (NP, D))
        rel_t = dram("rel_t", (NP * R, D))
        z_t = dram("z_t", (NP, H * (F + 1) + H))
        m_t = dram("m_t", (NP, D))
        agg_d = [dram(f"agg_d{l}", (NP, w)) for l, w in enumerate((D, H * (F + 1), D))]

        def sb(name, shape, dt=FP32, ctx=top):
            return ctx.enter_context(nc.sbuf_tensor(name, shape, dt))

        X = sb("X", [P, NT, D])
        Hh = sb("Hh", [P, NT, D])
        ident = sb("ident", [P, P])
        iota = sb("iota", [P, P])
        item_dst = sb("item_dst", [P, IG * P])
        item_rel = sb("item_rel", [P, IG * P], I32)
        item_src = sb("item_src", [P, IG * P], I32)
        item_wgt = sb("item_wgt", [P, IG * P])
        item_chunk = sb("item_chunk", [P, IG], I32)
        ed_sb = sb("ed_sb", [P, NT * (H + 1)])
        item_keep = sb("item_keep", [P, IG * P])
        item_row = sb("item_row", [1, IG * P], I32)
        eps_c = sb("eps_c", [P, 1])
        one_c = sb("one_c", [P, 1])
        node = sb("node", [P, NT])
        last_dst = sb("last_dst", [P, NT], I32)

        stats = sb("stats", [P, NT, 6])
        rstd, nmr = sb("rstd", [P, NT]), sb("nmr", [P, NT])

        env = dict(locals())
        setup(env)
        seg_weights(env)
        items(env)
        last_edges(env)
        layer0(env)
        layer1_tables(env)
        aggregate(env, "a1", 0, rel_t, D, N * R - 1, item_rel, "wgt")
        layer1_end(env)
        layer2_tables(env)
        item_links(env)
        attention(env)
        add_attention(env)
        layer3_tables(env)
        aggregate(env, "a3", 2, m_t, D, N - 1, item_src, None)
        layer3_end(env)


def agg_width(l):
    return H * (F + 1) if l == 1 else D


class Phase:

    def __init__(self, nc, name):
        self.nc, self.name, self.ctx, self.sems = nc, name, ExitStack(), []

    def __enter__(self):
        return self

    def __exit__(self, *a):
        self.ctx.close()
        self.nc.clear_and_free_semaphores(self.sems)
        self.nc.all_engine_barrier()

    def sb(self, name, shape, dt=FP32):
        return self.ctx.enter_context(self.nc.sbuf_tensor(f"{self.name}_{name}", shape, dt))

    def ps(self, name, shape, dt=FP32):
        return self.ctx.enter_context(self.nc.psum_tensor(f"{self.name}_{name}", shape, dt))

    def sem(self, name):
        self.sems.append(self.nc.alloc_semaphore(f"{self.name}_{name}"))
        return self.sems[-1]


def setup(env):
    nc, A = env["nc"], env["A"]
    X, ident, iota = env["X"], env["ident"], env["iota"]
    with Phase(nc, "su") as ph:
        di = ph.sb("di", [P, CH], I32)
        si = ph.sb("si", [P, CH], I32)
        ti = ph.sb("ti", [P, CH], I32)
        df, sf, tf = (ph.sb(n, [P, CH]) for n in ("df", "sf", "tf"))
        rl = ph.sb("rl", [P, CH])
        ones = ph.sb("ones", [P, P])
        cnt = ph.sb("cnt", [P, NT])
        bnd = ph.sb("bnd", [P, NT])
        bi = ph.sb("bi", [P, NT], I32)
        flo = ph.sb("flo", [P, NT])
        cei = ph.sb("cei", [P, NT])
        num = ph.sb("num", [P, NT])
        pre = ph.sb("pre", [P, NT])
        dlt = ph.sb("dlt", [P, NT])
        dd = ph.sb("dd", [P, NT])
        ii = ph.sb("ii", [P, IG])
        i1 = ph.sb("i1", [P, IG])
        it = ph.sb("it", [P, 4, IG])
        itT = ph.sb("itT", [IG, 4, P])
        hits = ph.sb("hits", [P, CH])
        krow = ph.sb("krow", [P, IG * P])
        rrow = ph.sb("rrow", [1, 3, IG * P])
        psb = ph.ps("psb", [P, NT])
        psi = ph.ps("psi", [IG, 4, P])
        dls, xl, cst, fill = ph.sem("edges_in"), ph.sem("x_in"), ph.sem("const"), ph.sem("filled")
        dv, cs, bs, its, itt, itc = (ph.sem(n) for n in ("dve", "counts", "bounds", "items", "itemsT", "itemsTc"))
        fst, put, back, pl, rdy = (ph.sem(n) for n in ("floats", "put", "back", "pool", "item_put"))
        with nc.Block() as block:
            @block.gpsimd
            def _(pool):
                chain = Chain(pool, pl)
                chain(pool.memset(ident[:, :], 0.0))
                chain(pool.affine_select(out=ident[:, :], in_=ident[:, :], compare_op=ALU.not_equal, fill=1.0,
                                         base=0, pattern=[[-1, P]], channel_multiplier=1))
                pool.iota(iota[:, :], pattern=[[1, P]], base=0, channel_multiplier=0,
                          allow_small_or_imprecise_dtypes=True).then_inc(cst, 1)
                pool.iota(ii[:, :], pattern=[[P, IG]], base=0, channel_multiplier=1,
                          allow_small_or_imprecise_dtypes=True).then_inc(cst, 1)
                pool.iota(i1[:, :], pattern=[[P, IG]], base=1, channel_multiplier=1,
                          allow_small_or_imprecise_dtypes=True).then_inc(cst, 1)
                pool.memset(ones[:, :], 1.0).then_inc(cst, 1)
                pool.memset(env["eps_c"][:, :], EPS).then_inc(cst, 1)
                pool.memset(X[:, RT - 1:NT, :], 0.0).then_inc(cst, 1)
                pool.wait_ge(cst, 6)

            @block.sync
            def _(sp):
                sp.wait_ge(fill, 3)
                full = FULLP * CH
                for t, name in ((di, "dst"), (si, "src"), (ti, "edge_type_8")):
                    sp.dma_start(t[0:FULLP, :], A[name][0:full].rearrange("(p f) -> p f", f=CH)).then_inc(dls, 16)
                    sp.dma_start(t[FULLP:FULLP + 1, 0:REST], A[name][full:E].rearrange("(a f) -> a f", a=1))\
                        .then_inc(dls, 16)
                sp.wait_ge(cst, 6)
                for c in range(0, RT - 1, 12):
                    sp.dma_start(X[:, c:c + 12, :], A["x"][c * P:(c + 12) * P, :].rearrange("(t p) d -> p t d", p=P))\
                        .then_inc(xl, 16)
                sp.dma_start(X[0:LAST, RT - 1, :], A["x"][(RT - 1) * P:N, :]).then_inc(xl, 16)
                for l in range(3):
                    w = agg_width(l)
                    for c in range(0, w, D):
                        sp.dma_start(env["agg_d"][l][RT * P:NP, c:min(c + D, w)], X[:, RT, 0:min(D, w - c)])\
                            .then_inc(put, 16)
                sp.wait_ge(fst, 1)
                for n, (t, d) in enumerate(((df, "dst_d"), (sf, "src_d"), (rl, "rel_d"))):
                    sp.dma_start(env[d].rearrange("c e -> (c e)").rearrange("(p f) -> p f", f=CH), t[:, :])\
                        .then_inc(put, 16)
                sp.dma_start(env["pack_d"][0:FULLP * CH].rearrange("(p f) -> p f", f=CH), di[0:FULLP, :]).then_inc(put, 16)
                sp.dma_start(env["pack_d"][FULLP * CH:E].rearrange("(a f) -> a f", a=1), di[FULLP:FULLP + 1, 0:REST])\
                    .then_inc(put, 16)
                sp.wait_ge(itc, 1)
                for k in range(4):
                    sp.dma_start(env["item_d"][k, :].rearrange("(g p) -> g p", p=P), itT[:, k, :]).then_inc(rdy, 16)
                sp.wait_ge(rdy, 64)
                sp.dma_start(krow[:, :], env["item_d"][2:3, :].partition_broadcast(P)).then_inc(back, 16)
                sp.dma_start(rrow[0:1, 0, :], env["item_d"][1:2, :]).then_inc(back, 16)
                sp.dma_start(rrow[0:1, 1, :], env["item_d"][3:4, :]).then_inc(back, 16)
                sp.wait_ge(put, 48 + 64 + 32)
                sp.wait_ge(xl, 80)

            @block.vector
            def _(v):
                chain = Chain(v, dv)
                v.memset(di[:, :], int(PADDST)).then_inc(fill, 1)
                v.memset(si[:, :], 0).then_inc(fill, 1)
                v.memset(ti[:, :], 0).then_inc(fill, 1)
                v.wait_ge(fill, 3)
                v.wait_ge(dls, 16 * 6)
                chain(v.tensor_copy(df[:, :], di[:, :]))
                chain(v.tensor_copy(sf[:, :], si[:, :]))
                chain(v.tensor_copy(tf[:, :], ti[:, :]))
                chain(v.tensor_scalar(di[:, :], di[:, :], 13, None, ALU.logical_shift_left))
                chain(v.tensor_tensor(di[:, :], di[:, :], si[:, :], ALU.bitwise_or))
                v.scalar_tensor_tensor(out=rl[:, :], in0=sf[:, :], scalar=float(R), in1=tf[:, :],
                                       op0=ALU.mult, op1=ALU.add).then_inc(fst, 1)
                v.wait_ge(fst, 1)
                v.wait_ge(cst, 6)
                chain(v.memset(cnt[:, :], 0.0))
                for t in range(1, NT):
                    chain(v.tensor_scalar(hits[:, :], df[:, :], float(min(t * P, N)), 0.0, ALU.is_lt, ALU.add,
                                          accum_out=cnt[:, t:t + 1]))
                v.sem_inc(cs, 1)
                v.wait_ge(bs, 1)
                chain(v.tensor_copy(bnd[:, :], psb[:, :]))
                chain(v.tensor_copy(bi[:, :], bnd[:, :]))
                chain(v.tensor_scalar(bi[:, :], bi[:, :], 7, None, ALU.arith_shift_right))
                chain(v.tensor_copy(flo[:, :], bi[:, :]))
                chain(v.tensor_scalar(cei[:, :], bnd[:, :], float(P - 1), None, ALU.add))
                chain(v.tensor_copy(bi[:, :], cei[:, :]))
                chain(v.tensor_scalar(bi[:, :], bi[:, :], 7, None, ALU.arith_shift_right))
                chain(v.tensor_copy(cei[:, :], bi[:, :]))
                chain(v.memset(num[:, :], 0.0))
                chain(v.tensor_tensor(num[:, 1:NT], cei[:, 1:NT], flo[:, 0:NT - 1], ALU.subtract))
                chain(v.tensor_scalar(num[:, 1:NT], num[:, 1:NT], 1.0, None, ALU.max))
                chain(v.memset(dlt[:, :], 1.0))
                chain(v.tensor_tensor_scan(pre[:, :], dlt[:, :], num[:, :], 0.0, ALU.mult, ALU.add))
                chain(v.tensor_tensor(dlt[:, :], flo[:, :], pre[:, :], ALU.subtract))
                chain(v.tensor_copy(dd[:, 0:1], dlt[:, 0:1]))
                chain(v.tensor_tensor(dd[:, 1:NT], dlt[:, 1:NT], dlt[:, 0:NT - 1], ALU.subtract))
                for g in range(IG):
                    i = ii[:, g:g + 1]
                    chain(v.tensor_scalar(hits[:, 0:NT], pre[:, :], i, 0.0, ALU.is_le, ALU.add,
                                          accum_out=it[:, 1, g:g + 1]))
                    chain(v.scalar_tensor_tensor(out=hits[:, 0:NT], in0=pre[:, :], scalar=i, in1=dd[:, :],
                                                 op0=ALU.is_le, op1=ALU.mult, accum_out=it[:, 0, g:g + 1]))
                    chain(v.tensor_scalar(hits[:, 0:NT], pre[:, :], i, 0.0, ALU.is_equal, ALU.add,
                                          accum_out=it[:, 2, g:g + 1]))
                    chain(v.tensor_scalar(hits[:, 0:NT], pre[:, :], i1[:, g:g + 1], 0.0, ALU.is_equal, ALU.add,
                                          accum_out=it[:, 3, g:g + 1]))
                chain(v.tensor_tensor(it[:, 0, :], it[:, 0, :], ii[:, :], ALU.add))
                chain(v.tensor_scalar(it[:, 0, :], it[:, 0, :], float(CH - 1), None, ALU.min))
                chain(v.tensor_scalar(it[:, 1, :], it[:, 1, :], 1.0, None, ALU.subtract))
                v.sem_inc(its, 1)
                v.wait_ge(itt, 1)
                v.tensor_copy(itT[:, :, :], psi[:, :, :]).then_inc(itc, 1)
                v.wait_ge(back, 48)
                chain(v.tensor_scalar(env["item_keep"][:, :], krow[:, :], -1.0, 1.0, ALU.mult, ALU.add))
                chain(v.tensor_scalar(rrow[0:1, 0, :], rrow[0:1, 0, :], float(RT), None, ALU.subtract))
                chain(v.tensor_tensor(rrow[0:1, 0, :], rrow[0:1, 0, :], rrow[0:1, 1, :], ALU.mult))
                chain(v.tensor_scalar(rrow[0:1, 0, :], rrow[0:1, 0, :], float(RT), None, ALU.add))
                chain(v.tensor_copy(env["item_row"][0:1, :], rrow[0:1, 0, :]))

            @block.tensor
            def _(pe):
                pe.wait_ge(cs, 1)
                pe.wait_ge(cst, 6)
                pe.matmul(psb[:, :], ones[:, :], cnt[:, :], start=True, stop=True).then_inc(bs, 1)
                pe.wait_ge(its, 1)
                pe.wait_ge(pl, 2)
                for k in range(4):
                    last = pe.transpose(psi[:, k, :], it[:, k, :], ident[:, :])
                last.then_inc(itt, 1)


def scan_view(d):
    return d.rearrange("c e -> (c e)").rearrange("(p f) -> p f", p=P)


def scan_buffers(env, ph, width, extra):
    big = env["Hh"][:, :, :].rearrange("p t d -> p (t d)")
    b = dict(ident=env["ident"], n=0, stage=0, pe_stage=0, width=width)
    b["val"] = big[:, 0:H * width].rearrange("p (c f) -> p c f", f=width)
    b["run"] = big[:, H * width:2 * H * width].rearrange("p (c f) -> p c f", f=width)
    for k in range(extra):
        b[f"x{k}"] = big[:, (2 * H + k) * width:(2 * H + k + 1) * width]
    for n in ("nst", "nen", "en"):
        b[n] = ph.sb(n, [P, width])
    b["tot"] = ph.sb("tot", [P, 2 * H])
    b["totT"] = ph.sb("totT", [H, 2, P])
    b["car"] = ph.sb("car", [H, P + 1])
    b["carT"] = ph.sb("carT", [P, H])
    b["psT"] = ph.ps("psT", [H, 2, P])
    b["psC"] = ph.ps("psC", [P, H])
    for n in ("dve", "tot_ready", "totT_ready", "car_ready", "carT_ready", "shifted_in", "filled"):
        b[n] = ph.sem(n)
    return b


def scan_flags(env, b, source):
    nc = env["nc"]
    dst = source.rearrange("c e -> (c e)")
    w, n = b["width"], b["width"] * P
    cur, prv, nxt = b["x0"], b["x1"], b["x2"]
    ld, fl = b["shifted_in"], b["filled"]
    with nc.Block() as block:
        @block.sync
        def _(sp):
            sp.wait_ge(fl, 2)
            row = lambda a: a.rearrange("(a f) -> a f", a=1)
            sp.dma_start(cur, dst.rearrange("(p f) -> p f", f=w)).then_inc(ld, 16)
            sp.dma_start(prv[0:1, 1:w], row(dst[0:w - 1])).then_inc(ld, 16)
            sp.dma_start(prv[1:P, :], dst[w - 1:n - 1].rearrange("(p f) -> p f", f=w)).then_inc(ld, 16)
            sp.dma_start(nxt[0:P - 1, :], dst[1:n - w + 1].rearrange("(p f) -> p f", f=w)).then_inc(ld, 16)
            sp.dma_start(nxt[P - 1:P, 0:w - 1], row(dst[n - w + 1:n])).then_inc(ld, 16)
            sp.wait_ge(ld, 80)

        @block.vector
        def _(v):
            chain = Chain(v, b["dve"])
            v.memset(prv, -1.0).then_inc(fl, 1)
            v.memset(nxt, -1.0).then_inc(fl, 1)
            v.wait_ge(ld, 80)
            chain(v.tensor_tensor(b["nst"][:, :], cur, prv, ALU.is_equal))
            chain(v.tensor_tensor(b["nen"][:, :], cur, nxt, ALU.is_equal))
            chain(v.tensor_scalar(b["en"][:, :], b["nen"][:, :], -1.0, 1.0, ALU.mult, ALU.add))
            b["n"] = chain.n


def seg_weights(env):
    nc = env["nc"]
    with Phase(nc, "sw") as ph:
        b = scan_buffers(env, ph, CH, 7)
        tf, eq, wsum, sf = b["x3"], b["x4"], b["x5"], b["x6"]
        loaded, put, fin = ph.sem("loaded"), ph.sem("put"), ph.sem("weights")
        scan_flags(env, b, env["dst_d"])
        with nc.Block() as block:
            @block.vector
            def _(v):
                chain = Chain(v, b["dve"], b["n"])
                v.wait_ge(loaded, 32)
                chain(v.scalar_tensor_tensor(out=tf, in0=sf, scalar=-float(R), in1=tf, op0=ALU.mult, op1=ALU.add))
                chain(v.memset(wsum, 0.0))
                for half in range(R // H):
                    for r in range(H):
                        chain(v.tensor_scalar(b["val"][:, r, :], tf, float(H * half + r), None, ALU.is_equal))
                    seg_forward(v, chain, b, H, ALU.mult, b["nst"], ALU.add, 0.0)
                    seg_backward(v, chain, b, H)
                    for r in range(H):
                        chain(v.scalar_tensor_tensor(out=eq, in0=tf, scalar=float(H * half + r),
                                                     in1=b["val"][:, r, :], op0=ALU.is_equal, op1=ALU.mult))
                        chain(v.tensor_tensor(wsum, wsum, eq, ALU.add))
                chain(v.tensor_scalar(wsum, wsum, 1.0, None, ALU.max))
                v.reciprocal(eq, wsum).then_inc(fin, 1)

            @block.tensor
            def _(pe):
                for _ in range(2 * R // H):
                    seg_carry(pe, b, H)

            @block.sync
            def _(sp):
                sp.dma_start(tf, scan_view(env["rel_d"])).then_inc(loaded, 16)
                sp.dma_start(sf, scan_view(env["src_d"])).then_inc(loaded, 16)
                sp.wait_ge(fin, 1)
                sp.dma_start(scan_view(env["wgt_d"]), eq).then_inc(put, 16)
                sp.wait_ge(put, 16)


def seg_carry(pe, b, ch):
    k = b["pe_stage"] = b["pe_stage"] + 1
    pe.wait_ge(b["tot_ready"], k)
    pe.transpose(b["psT"][:, 0, :], b["tot"][:, 0:ch], b["ident"][:, :])
    pe.transpose(b["psT"][:, 1, :], b["tot"][:, ch:2 * ch], b["ident"][:, :]).then_inc(b["totT_ready"], 1)
    pe.wait_ge(b["car_ready"], k)
    lo = 0 if k % 2 else 1
    pe.transpose(b["psC"][:, :], b["car"][:, lo:lo + P], b["ident"][0:ch, 0:ch]).then_inc(b["carT_ready"], 1)


def seg_forward(v, chain, b, ch, op0, reset, op1, init):
    k = b["stage"] = b["stage"] + 1
    val, run, tot = b["val"], b["run"], b["tot"]
    for c in range(ch):
        chain(v.tensor_tensor_scan(run[:, c, :], reset[:, :], val[:, c, :], init, op0, op1))
    chain(v.tensor_copy(tot[:, 0:ch], run[:, :, b["width"] - 1]))
    chain(v.tensor_reduce(tot[:, ch:ch + 1], reset[:, :], AX.X, ALU.min))
    for c in range(1, ch):
        chain(v.tensor_copy(tot[:, ch + c:ch + c + 1], tot[:, ch:ch + 1]))
    v.sem_inc(b["tot_ready"], 1)
    v.wait_ge(b["totT_ready"], k)
    chain(v.tensor_copy(b["totT"][:, :, :], b["psT"][:, :, :]))
    chain(v.memset(b["car"][:, :], init))
    chain(v.tensor_tensor_scan(b["car"][:, 1:P + 1], b["totT"][:, 1, :], b["totT"][:, 0, :], init, op0, op1))
    v.sem_inc(b["car_ready"], 1)
    v.wait_ge(b["carT_ready"], k)
    chain(v.tensor_copy(b["carT"][:, :], b["psC"][:, :]))
    for c in range(ch):
        chain(v.tensor_tensor_scan(run[:, c, :], reset[:, :], val[:, c, :], b["carT"][:, c:c + 1], op0, op1))


def seg_backward(v, chain, b, ch):
    k = b["stage"] = b["stage"] + 1
    val, run, tot = b["val"], b["run"], b["tot"]
    for c in range(ch):
        chain(v.tensor_tensor(run[:, c, :], run[:, c, :], b["en"][:, :], ALU.mult))
    for c in range(ch):
        chain(v.tensor_tensor_scan(val[:, c, ::-1], b["nen"][:, ::-1], run[:, c, ::-1], 0.0, ALU.mult, ALU.add))
    chain(v.tensor_copy(tot[:, 0:ch], val[:, :, 0]))
    chain(v.tensor_reduce(tot[:, ch:ch + 1], b["nen"][:, :], AX.X, ALU.min))
    for c in range(1, ch):
        chain(v.tensor_copy(tot[:, ch + c:ch + c + 1], tot[:, ch:ch + 1]))
    v.sem_inc(b["tot_ready"], 1)
    v.wait_ge(b["totT_ready"], k)
    chain(v.tensor_copy(b["totT"][:, :, :], b["psT"][:, :, :]))
    chain(v.memset(b["car"][:, :], 0.0))
    chain(v.tensor_tensor_scan(b["car"][:, P - 1::-1], b["totT"][:, 1, ::-1], b["totT"][:, 0, ::-1], 0.0,
                               ALU.mult, ALU.add))
    v.sem_inc(b["car_ready"], 1)
    v.wait_ge(b["carT_ready"], k)
    chain(v.tensor_copy(b["carT"][:, :], b["psC"][:, :]))
    for c in range(ch):
        chain(v.tensor_tensor_scan(val[:, c, ::-1], b["nen"][:, ::-1], run[:, c, ::-1], b["carT"][:, c:c + 1],
                                   ALU.mult, ALU.add))


def items(env):
    nc = env["nc"]
    with Phase(nc, "it") as ph:
        cf, tl, ci = ph.sb("cf", [P, IG]), ph.sb("tl", [P, IG]), env["item_chunk"]
        rows = ph.sb("rows", [P, IG, 4, P])
        ok, tmp = ph.sb("ok", [P, P]), ph.sb("tmp", [P, P])
        pt = ph.ps("pt", [P, 4, P])
        got, idx, gat, dv, tr, cp, rd, put, put2 = (ph.sem(n) for n in (
            "got", "idx", "gathered", "dve", "tr", "cp", "rd", "put_global", "put_local"))
        with nc.Block() as block:
            @block.sync
            def _(sp):
                sp.dma_start(cf[:, :], env["item_d"][0, :].rearrange("(g p) -> p g", p=P),
                             allow_slow_non_contiguous=True).then_inc(got, 16)
                sp.dma_start(tl[:, :], env["item_d"][1, :].rearrange("(g p) -> p g", p=P),
                             allow_slow_non_contiguous=True).then_inc(got, 16)
                sp.wait_ge(gat, 16 * 4 * IG)
                for k, (sem, target) in enumerate(((put, "item_gdst_d"), (put2, "item_ldst_d"))):
                    if k:
                        sp.wait_ge(rd, IG)
                    full = (IG - 1) * P
                    sp.dma_start(env[target][0:full, :].rearrange("(g p) e -> p g e", p=P), rows[:, 0:IG - 1, 0, :])\
                        .then_inc(sem, 16)
                    sp.dma_start(env[target][full:ITEMS, :], rows[0:ITEMS - full, IG - 1, 0, :]).then_inc(sem, 16)
                sp.wait_ge(put2, 32)

            @block.gpsimd
            def _(pool):
                pool.wait_ge(idx, 1)
                for g in range(IG):
                    for k, d in enumerate(("dst_d", "src_d", "rel_d", "wgt_d")):
                        pool.indirect_dma_start(out=rows[:, g, k, :], out_offset=None, in_=env[d][:, :],
                                                in_offset=bass.IndirectOffsetOnAxis(ap=ci[:, g:g + 1], axis=0))\
                            .then_inc(gat, 16)
                pool.wait_ge(gat, 16 * 4 * IG)

            @block.vector
            def _(v):
                chain = Chain(v, dv)
                v.wait_ge(got, 32)
                v.tensor_copy(ci[:, :], cf[:, :]).then_inc(idx, 1)
                chain(v.tensor_scalar(tl[:, :], tl[:, :], float(P), None, ALU.mult))
                v.wait_ge(gat, 16 * 4 * IG)
                v.wait_ge(put, 32)
                for g in range(IG):
                    dl = rows[:, g, 0, :]
                    chain(v.tensor_scalar(dl, dl, tl[:, g:g + 1], None, ALU.subtract))
                    chain(v.tensor_scalar(tmp[:, :], dl, 0.0, None, ALU.is_ge))
                    chain(v.scalar_tensor_tensor(out=ok[:, :], in0=dl, scalar=float(P), in1=tmp[:, :],
                                                 op0=ALU.is_lt, op1=ALU.mult))
                    for k in (1, 2):
                        x = rows[:, g, k, :]
                        chain(v.scalar_tensor_tensor(out=x, in0=x, scalar=-OOB, in1=ok[:, :],
                                                     op0=ALU.add, op1=ALU.mult))
                        chain(v.tensor_scalar(x, x, OOB, None, ALU.add))
                    v.sem_inc(rd, 1)
                    v.wait_ge(tr, g + 1)
                    s = slice(g * P, (g + 1) * P)
                    chain(v.tensor_copy(env["item_dst"][:, s], pt[:, 0, :]))
                    chain(v.tensor_copy(env["item_src"][:, s], pt[:, 1, :]))
                    chain(v.tensor_copy(env["item_rel"][:, s], pt[:, 2, :]))
                    v.tensor_copy(env["item_wgt"][:, s], pt[:, 3, :]).then_inc(cp, 1)
                v.wait_ge(cp, IG)

            @block.tensor
            def _(pe):
                for g in range(IG):
                    pe.wait_ge(rd, g + 1)
                    wait(pe, cp, g)
                    for k in range(4):
                        last = pe.transpose(pt[:, k, :], rows[:, g, k, :], env["ident"][:, :])
                    last.then_inc(tr, 1)


def last_edges(env):
    nc, A = env["nc"], env["A"]
    with Phase(nc, "le") as ph:
        rw = ph.sb("rw", [P, LG, LC], I32)
        rf = ph.sb("rf", [P, LG, LC])
        ci = ph.sb("ci", [LC, LG * P], I32)
        chi, clo = ph.sb("chi", [LC, LG * P]), ph.sb("clo", [LC, LG * P])
        tmpi = ph.sb("tmpi", [LC, LG * P], I32)
        ohh = ph.sb("ohh", [LC, 2, LU, NHI], BF16)
        ohl = ph.sb("ohl", [LC, 2, LU, NLO], BF16)
        rlo = ph.sb("rlo", [LC, 2, LP])
        vi = ph.sb("vi", [NHI, NLO], I32)
        T, T1, nf = (ph.sb(n, [NHI, NLO]) for n in ("T", "T1", "nf"))
        pt = ph.ps("pt", [LC, P])
        pp = [ph.ps(f"pp{i}", [NHI, 512]) for i in range(2)]
        ld, tr, cp, dv, rd, hi_s, lo_s, mm, lp, fin, put, cv, cols = (
            ph.sem(n) for n in ("ld", "tr", "cp", "dve", "rd", "hi_ready", "lo_ready", "sums", "loop", "fin", "put",
                                "conv", "columns"))
        chunk, ci2, num, m = (ph.sb("chunk", [P, NT]), ph.sb("ci2", [P, NT], I32), ph.sb("num", [P, NT]),
                              ph.sb("m", [P, NT]))
        big = env["Hh"][:, :, :].rearrange("p t d -> p (t d)")
        pk = big[:, 0:RT * LC].rearrange("p (t e) -> p t e", e=LC)
        pk2 = big[:, RT * LC:2 * RT * LC].rearrange("p (t e) -> p t e", e=LC)
        z, back, gat, ready, io, staged, go = (ph.sem(n) for n in (
            "zeroed", "back", "gathered", "chunks", "iota", "staged", "go"))
        groups = LCH // LU

        with nc.Block() as block:
            @block.sync
            def _(sp):
                sp.wait_ge(rd, 1)
                full = (LG - 1) * P
                sp.dma_start(rw[:, 0:LG - 1, :], A["src"][0:full * LC].rearrange("(g p f) -> p g f", p=P, f=LC))\
                    .then_inc(ld, 16)
                sp.dma_start(rw[0:LCH - full, LG - 1, :], A["src"][full * LC:E].rearrange("(p f) -> p f", f=LC))\
                    .then_inc(ld, 16)
                sp.wait_ge(fin, 1)
                sp.dma_start(env["last_d"].rearrange("(h l) -> h l", l=NLO), T[:, :]).then_inc(put, 16)
                sp.wait_ge(put, 16)
                with nc.allow_non_contiguous_dma("one value per node"):
                    sp.dma_start(chunk[:, 0:RT], env["last_d"].rearrange("(t p) -> p t", p=P)).then_inc(back, 16)
                sp.wait_ge(back, 16)

            @block.vector
            def _(v):
                chain = Chain(v, dv)
                v.memset(rw[:, LG - 1, :], 12287).then_inc(rd, 1)
                v.memset(pk, 0.0).then_inc(z, 1)
                v.memset(chunk[:, :], 0.0).then_inc(z, 1)
                v.wait_ge(ld, 32)
                v.tensor_copy(rf[:, :, :], rw[:, :, :]).then_inc(cv, 1)
                for g in range(LG):
                    v.wait_ge(tr, g + 1)
                    v.tensor_copy(ci[:, g * P:(g + 1) * P], pt[:, :]).then_inc(cp, 1)
                v.wait_ge(cp, LG)
                chain(v.tensor_scalar(tmpi[:, :], ci[:, :], 6, None, ALU.arith_shift_right))
                chain(v.tensor_copy(chi[:, :], tmpi[:, :]))
                chain(v.tensor_scalar(tmpi[:, :], ci[:, :], NLO - 1, None, ALU.bitwise_and))
                chain(v.tensor_copy(clo[:, :], tmpi[:, :]))
                v.sem_inc(cols, 1)
                chain(v.memset(T[:, :], 0.0))

                def build(j, b):
                    wait(v, mm, j - 1)
                    for k in range(LU):
                        v.tensor_scalar(ohh[:, b, k, :], env["iota"][0:LC, 0:NHI], chi[:, bass.ds(j * LU + k, 1)],
                                        2.0 ** (8 * (k + 1) - 127), ALU.is_equal, ALU.mult).then_inc(hi_s, 1)

                    v.tensor_tensor(ohl[:, b, LP:LU, :],
                                    env["iota"][0:LC, 0:NLO].unsqueeze(1).to_broadcast([LC, LU - LP, NLO]),
                                    clo[:, bass.ds(j * LU + LP, LU - LP)].unsqueeze(2).to_broadcast([LC, LU - LP, NLO]),
                                    ALU.is_equal).then_inc(hi_s, 1)

                def merge(j, b):
                    c = Chain(v, lp, 5 * j)
                    v.wait_ge(mm, j + 1)
                    c(v.tensor_scalar(vi[:, :], pp[b][:, 0:NLO].bitcast(I32), 26, None, ALU.logical_shift_right))
                    c(v.tensor_scalar(nf[:, :], vi[:, :], 0.0, None, ALU.is_equal))
                    c(v.tensor_scalar(T1[:, :], T[:, :], float(LU), None, ALU.subtract))
                    c(v.tensor_tensor(T1[:, :], T1[:, :], nf[:, :], ALU.mult))
                    c(v.tensor_tensor(T[:, :], T1[:, :], vi[:, :], ALU.add))

                build(0, 0)
                with v.Fori(0, groups // 2 - 1) as i:
                    build(2 * i + 1, 1)
                    merge(2 * i, 0)
                    build(2 * i + 2, 0)
                    merge(2 * i + 1, 1)
                build(groups - 1, 1)
                merge(groups - 2, 0)
                merge(groups - 1, 1)
                chain(v.tensor_scalar(T[:, :], T[:, :], float(LU * (groups - 1)), 0.0, ALU.add, ALU.max))
                v.sem_inc(fin, 1)
                v.wait_ge(back, 16)
                chain(v.tensor_scalar(m[:, :], chunk[:, :], 0.0, OOB, ALU.is_equal, ALU.mult))
                chain(v.scalar_tensor_tensor(out=num[:, :], in0=chunk[:, :], scalar=-1.0, in1=m[:, :],
                                             op0=ALU.add, op1=ALU.add))
                v.tensor_copy(ci2[:, :], num[:, :]).then_inc(ready, 1)
                v.wait_ge(io, 1)
                v.wait_ge(gat, 16 * RT)
                pki, pk2i = pk.bitcast(I32), pk2.bitcast(I32)
                chain(v.tensor_scalar(pk2i, pki, 8191, None, ALU.bitwise_and))
                chain(v.tensor_scalar(pki, pki, 13, None, ALU.logical_shift_right))
                for t in range(RT):
                    ins = v.scalar_tensor_tensor(out=pk2[:, t, :], in0=pk2i[:, t, :], scalar=env["node"][:, t:t + 1],
                                                 in1=pki[:, t, :], op0=ALU.is_equal, op1=ALU.mult)
                    ins.then_inc(cp, 1)
                v.wait_ge(cp, LG + RT)
                chain(v.memset(num[:, :], OOB))
                chain(v.tensor_reduce(num[:, 0:RT], pk2, AX.X, ALU.max))
                chain(v.tensor_tensor(num[:, :], num[:, :], m[:, :], ALU.add))
                chain(v.tensor_copy(env["last_dst"][:, :], num[:, :]))

            @block.gpsimd
            def _(pool):
                pool.iota(env["node"][:, :], pattern=[[P, NT]], base=0, channel_multiplier=1,
                          allow_small_or_imprecise_dtypes=True).then_inc(io, 1)
                pool.wait_ge(cols, 1)

                def build(j, b):
                    wait(pool, mm, j - 1)
                    pool.sem_inc(go, 1)
                    pool.tensor_copy(rlo[:, b, :], clo[:, bass.ds(j * LU, LP)]).then_inc(staged, 1)
                    pool.wait_ge(staged, j + 1)
                    pool.sem_inc(go, 1)
                    for k in range(LP):
                        pool.tensor_scalar(ohl[:, b, k, :], env["iota"][0:LC, 0:NLO], rlo[:, b, k:k + 1], None,
                                           ALU.is_equal).then_inc(lo_s, 1)
                build(0, 0)
                build(1, 1)
                with pool.Fori(1, groups // 2) as i:
                    build(2 * i, 0)
                    build(2 * i + 1, 1)
                lim = pool.to_reg(LCH - 1)
                pool.wait_ge(z, 2)
                pool.wait_ge(ready, 1)
                for t in range(RT):
                    pool.indirect_dma_start(out=pk.bitcast(I32)[:, t, :], out_offset=None,
                                            in_=env["pack_d"].rearrange("(c e) -> c e", e=LC),
                                            in_offset=bass.IndirectOffsetOnAxis(ap=ci2[:, t:t + 1], axis=0),
                                            bounds_check=lim, oob_is_err=False).then_inc(gat, 16)
                pool.wait_ge(gat, 16 * RT)

            @block.tensor
            def _(pe):
                pe.wait_ge(cv, 1)
                for g in range(LG):
                    wait(pe, cp, g)
                    pe.transpose(pt[:, :], rf[:, g, :], env["ident"][:, :]).then_inc(tr, 1)

                def sums(j, b):
                    pe.wait_ge(hi_s, (LU + 1) * (j + 1))
                    pe.wait_ge(lo_s, LP * (j + 1))
                    wait(pe, lp, 5 * j - 9)
                    for k in range(LU):
                        last = pe.matmul(pp[b][:, 0:NLO], ohh[:, b, k, :], ohl[:, b, k, :], start=(k == 0),
                                         stop=(k == LU - 1))
                    last.then_inc(mm, 1)

                sums(0, 0)
                sums(1, 1)
                with pe.Fori(1, groups // 2) as i:
                    sums(2 * i, 0)
                    sums(2 * i + 1, 1)


class Scales:

    def __init__(self, env, ph):
        self.env = env
        self.var, self.mean, self.dif, self.std = (ph.sb(n, [P, NT]) for n in ("var", "mean", "dif", "std"))
        self.summed, self.rooted, self.link, self.ready = (
            ph.sem(n) for n in ("var_ready", "root_ready", "scales_link", "scales_ready"))

    def dve(self, v):
        s, c = self.env["stats"], Chain(v, self.link)
        rstd, nmr = self.env["rstd"], self.env["nmr"]
        c(v.tensor_tensor(self.mean[:, :], s[:, :, 1], s[:, :, 4], ALU.add))
        c(v.tensor_tensor(self.dif[:, :], s[:, :, 1], s[:, :, 4], ALU.subtract))
        c(v.tensor_tensor(self.var[:, :], s[:, :, 2], s[:, :, 5], ALU.add))
        c(v.scalar_tensor_tensor(out=self.dif[:, :], in0=self.dif[:, :], scalar=0.25, in1=self.dif[:, :],
                                 op0=ALU.mult, op1=ALU.mult))
        v.scalar_tensor_tensor(out=self.var[:, :], in0=self.var[:, :], scalar=1.0 / D, in1=self.dif[:, :],
                               op0=ALU.mult, op1=ALU.add).then_inc(self.summed, 1)
        v.wait_ge(self.rooted, 1)
        c(v.reciprocal(rstd[:, :], self.std[:, :]))
        c(v.scalar_tensor_tensor(out=nmr[:, :], in0=self.mean[:, :], scalar=-0.5, in1=rstd[:, :],
                                 op0=ALU.mult, op1=ALU.mult))
        v.sem_inc(self.ready, 1)

    def act(self, act):
        act.wait_ge(self.summed, 1)
        act.activation(self.std[:, :], self.var[:, :], ACT.Sqrt, bias=self.env["eps_c"][:, 0:1])\
            .then_inc(self.rooted, 1)
        act.wait_ge(self.ready, 1)


def normed(env, act, out, t):
    return act.activation(out, tile_of(env["X"], t), ACT.Relu, bias=env["nmr"][:, bass.ds(t, 1)],
                          scale=env["rstd"][:, bass.ds(t, 1)])


def first_norm(env):
    nc, X, Hh = env["nc"], env["X"], env["Hh"]
    with Phase(nc, "n0") as ph:
        sc = Scales(env, ph)
        hn, put, st = ph.sem("rows_done"), ph.sem("put"), ph.sem("stats")
        with nc.Block() as block:
            @block.vector
            def _(v):
                with v.Fori(0, NT // 10) as j:
                    for u in range(10):
                        v.bn_stats(tile_of(env["stats"], 10 * j + u), tile_of(X, 10 * j + u)).then_inc(st, 1)
                v.wait_ge(st, NT)
                sc.dve(v)

            @block.scalar
            def _(act):
                sc.act(act)
                with act.Fori(0, NT // 10) as j:
                    for u in range(10):
                        normed(env, act, tile_of(Hh, 10 * j + u), 10 * j + u).then_inc(hn, 1)

            @block.sync
            def _(sp):
                for c in range(0, NT, 10):
                    sp.wait_ge(hn, c + 10)
                    sp.dma_start(env["h_d"][c * P:(c + 10) * P, :].rearrange("(t p) d -> p t d", p=P),
                                 Hh[:, c:c + 10, :]).then_inc(put, 16)
                sp.wait_ge(put, 80)


def tile_of(a, t):
    return a[:, bass.ds(t, 1), :].rearrange("p a d -> p (a d)")


def flat(ap):
    return ap.rearrange("p k q -> p (k q)")


def load_rows(sp, sem, pairs):
    for t, a in pairs:
        sp.dma_start(t, a.rearrange("(a n) -> a n", a=1).partition_broadcast(P)).then_inc(sem, 16)


class Tile:

    def __init__(self, un, j, k):
        if k < 0:
            j, k = j - 1, k + un
        if k >= un:
            j, k = j + 1, k - un
        self.j, self.k, self.u, self.t, self.h = j, k, k % 2, un * j + k, (un // 2) * j + k // 2
        self.first = isinstance(j, int) and j == 0 and k == 0


class Dense:

    def __init__(self, env, name, width, kt=2, un=2):
        self.env, self.nc, self.kt, self.width, self.un = env, env["nc"], kt, width, un
        self.ph = ph = Phase(env["nc"], name)
        self.rows = ph.sb("rows", [P, 2, kt, P])
        self.rowsT = ph.sb("rowsT", [P, 2, kt, P])
        self.psT = [ph.ps(f"psT{i}", [P, kt, P]) for i in range(2)]
        self.psO = [ph.ps(f"psO{i}", [P, width]) for i in range(2)]
        self.rows_ready, self.transposed, self.copied, self.products, self.taken, self.mid_done, self.link = (
            ph.sem(n) for n in ("rows_ready", "transposed", "copied", "products", "taken", "mid_done", "link"))

    def turns(self, engine, step):
        un, n = self.un, NT // self.un

        def body(j, last=False):
            for k in range(un):
                step(Tile(un, j, k), min(2, un - 1 - k) if last else 2)
        body(0)
        with engine.Fori(1, n - 1) as j:
            body(j)
        body(n - 1, last=True)

    def pe(self, pe, weights):
        ident = self.env["ident"]

        def transpose(a):
            pe.wait_ge(self.rows_ready, a.t + 1)
            wait(pe, self.copied, a.t - 1)
            for k in range(self.kt):
                last = pe.transpose(self.psT[a.u][:, k, :], self.rows[:, a.u, k, :], ident[:, :])
            last.then_inc(self.transposed, 1)

        def product(a):
            pe.wait_ge(self.copied, a.t + 1)
            wait(pe, self.taken, a.t - 1)
            for k in range(self.kt):
                last = pe.matmul(self.psO[a.u][:, :], self.rowsT[:, a.u, k, :], weights(k), start=(k == 0),
                                 stop=(k == self.kt - 1))
            last.then_inc(self.products, 1)

        def step(a, left):
            if left:
                transpose(Tile(self.un, a.j, a.k + 1))
            product(a)
        transpose(Tile(self.un, 0, 0))
        self.turns(pe, step)

    def act(self, act, mid=None, pre=None):
        def do_pre(a):
            wait(act, self.transposed, a.t - 1)
            pre(a).then_inc(self.rows_ready, 1)

        def do_mid(a):
            act.wait_ge(self.taken, a.t + 1)
            mid(a).then_inc(self.mid_done, 1)

        def step(a, left):
            if pre and left == 2:
                do_pre(Tile(self.un, a.j, a.k + 2))
            act.wait_ge(self.transposed, a.t + 1)
            wait(act, self.products, a.t - 1)
            act.copy(self.rowsT[:, a.u, :, :], self.psT[a.u][:, :, :]).then_inc(self.copied, 1)
            if mid and not a.first:
                do_mid(Tile(self.un, a.j, a.k - 1))
            if mid and not left:
                do_mid(a)
        if pre:
            do_pre(Tile(self.un, 0, 0))
            do_pre(Tile(self.un, 0, 1))
        self.turns(act, step)

    def dve(self, v, pre, post, npre, npost, end=None, nend=0):
        n = npre + npost + nend

        def do_pre(a, base):
            if pre is None:
                return
            wait(v, self.transposed, a.t - 1)
            c = Chain(v, self.link, base)
            pre(a, c).then_inc(self.rows_ready, 1)
            assert c.n == npre, (c.n, npre)

        def do_end(a, base):
            v.wait_ge(self.mid_done, a.t + 1)
            c = Chain(v, self.link, base)
            end(a, c)
            assert c.n == nend, (c.n, nend)

        def step(a, left):
            base = 2 * npre if a.first else n * a.t + 2 * npre - nend
            if left == 2:
                do_pre(Tile(self.un, a.j, a.k + 2), base)
                base = base + npre
            if not left:
                base = base - npre
            v.wait_ge(self.products, a.t + 1)
            c = Chain(v, self.link, base)
            post(a, c).then_inc(self.taken, 1)
            assert c.n == npost, (c.n, npost)
            if end and not a.first:
                do_end(Tile(self.un, a.j, a.k - 1), base + npost)
            if end and not left:
                do_end(a, base + npost + nend)

        do_pre(Tile(self.un, 0, 0), 0)
        do_pre(Tile(self.un, 0, 1), npre)
        self.turns(v, step)


GL = 5


def group_loads(d, sp, ring, sems, source):
    def body(j):
        for half in range(2):
            wait(sp, d.taken, 2 * GL * j - (2 - half - 1) * GL)
            sp.dma_start(ring[:, half * GL:(half + 1) * GL, :],
                         source[bass.ds((2 * GL * j + half * GL) * P, GL * P), :].rearrange("(t p) d -> p t d", p=P))\
                .then_inc(sems[half], 16)
    body(0)
    with sp.Fori(1, NT // (2 * GL)) as j:
        body(j)


def tile_loads(d, sp, slots, sems, source):
    def body(j):
        for u in range(2):
            t = 2 * j + u
            wait(sp, d.taken, t - 1)
            sp.dma_start(slots[:, u, :], source[bass.ds(t * P, P), :]).then_inc(sems[u], 16)
    body(0)
    with sp.Fori(1, NT // 2) as j:
        body(j)


def tile_stores(d, sp, parts):
    with sp.Fori(0, NT // 2) as j:
        for u in range(2):
            t = 2 * j + u
            sp.wait_ge(d.taken, t + 1)
            for slots, sems, target in parts:
                sp.dma_start(target(t), slots[:, u, :]).then_inc(sems[u], 16)
    for _, sems, _ in parts:
        for s in sems:
            sp.wait_ge(s, 16 * NT // 2)


def layer0(env):
    nc, A, X, Hh = env["nc"], env["A"], env["X"], env["Hh"]
    first_norm(env)
    d = Dense(env, "l0", D, kt=4, un=2 * GL)
    with d.ph as ph:
        wn = ph.sb("wn", [P, 2, 4, P])
        wT = ph.sb("wT", [P, 4, D])
        bias = ph.sb("bias", [P, D])
        nring = ph.sb("nring", [P, 2 * GL], I32)
        ag = ph.sb("ag", [P, 2 * GL, D])
        res = ph.sb("res", [P, 2, D])
        pw = ph.ps("pw", [P, 4, P])
        ld, wt, wc, nr, go = (ph.sem(n) for n in ("loaded", "w_transposed", "w_copied", "ring", "go"))
        turn = ph.sem("turn")
        sc = Scales(env, ph)
        gs = [ph.sem(f"gathered{i}") for i in range(2 * GL)]
        with nc.Block() as block:
            @block.sync
            def _(sp):
                for a in range(2):
                    sp.dma_start(wn[:, a, :, :], A["L0_gnn_W"][a * P:(a + 1) * P, :].rearrange("p (k q) -> p k q", q=P))\
                        .then_inc(ld, 16)
                load_rows(sp, ld, [(bias[:, :], A["L0_gnn_b"])])

            @block.vector
            def _(v):
                v.wait_ge(ld, 48)
                for a in range(2):
                    v.wait_ge(wt, a + 1)
                    v.tensor_copy(wT[:, :, a * P:(a + 1) * P], pw[:, :, :]).then_inc(wc, 1)

                def pre(a, c):
                    t, u = a.t, a.u
                    c(v.tensor_copy(flat(d.rows[:, u, 0:2, :]), tile_of(Hh, t)))
                    v.wait_ge(gs[a.k], 16 * (a.j + 1))
                    return v.tensor_copy(flat(d.rows[:, u, 2:4, :]), ag[:, a.k, :])

                def post(a, c):
                    t, u, h = a.t, a.u, a.h
                    c(v.tensor_tensor(res[:, u, :], d.psO[u][:, :], bias[:, :], ALU.add))
                    c(v.tensor_tensor(tile_of(X, t), tile_of(X, t), res[:, u, :], ALU.add))
                    v.sem_inc(turn, 1)
                    return v.bn_stats(tile_of(env["stats"], t), tile_of(X, t))
                d.dve(v, pre, post, 1, 2)
                v.wait_ge(d.taken, NT)
                sc.dve(v)

            @block.tensor
            def _(pe):
                pe.wait_ge(ld, 48)
                for a in range(2):
                    wait(pe, wc, a)
                    for k in range(4):
                        last = pe.transpose(pw[:, k, :], wn[:, a, k, :], env["ident"][:, :])
                    last.then_inc(wt, 1)
                pe.wait_ge(wc, 2)
                d.pe(pe, lambda k: wT[:, k, :])

            @block.scalar
            def _(act):
                d.act(act)
                sc.act(act)

            @block.gpsimd
            def _(pool):
                lim_n = pool.to_reg(N - 1)

                def body(j):
                    for half in range(2):
                        a, b = half * GL, (half + 1) * GL
                        wait(pool, d.rows_ready, 2 * GL * (j - 1) + b)
                        pool.sem_inc(go, 1)
                        pool.memset(ag[:, a:b, :], 0.0).then_inc(nr, 1)
                        pool.tensor_copy(nring[:, a:b], env["last_dst"][:, bass.ds(2 * GL * j + a, GL)])\
                            .then_inc(nr, 1)
                        pool.wait_ge(nr, 4 * j + 2 * half + 2)
                        pool.sem_inc(go, 1)
                        for k in range(a, b):
                            pool.indirect_dma_start(out=ag[:, k, :], out_offset=None, in_=env["h_d"][:, :],
                                                    in_offset=bass.IndirectOffsetOnAxis(ap=nring[:, k:k + 1], axis=0),
                                                    bounds_check=lim_n, oob_is_err=False).then_inc(gs[k], 16)
                body(0)
                with pool.Fori(1, NT // (2 * GL)) as j:
                    body(j)


def layer1_tables(env):
    nc, A = env["nc"], env["A"]
    q = R // 2
    with Phase(nc, "t1") as ph:
        w = ph.sb("w", [P, 2, R * D])
        rows, rowsT = ph.sb("rows", [P, 2, 2, P]), ph.sb("rowsT", [P, 2, 2, P])
        o = ph.sb("o", [P, 2, q * D])
        psT = [ph.ps(f"psT{i}", [P, 512]) for i in range(2)]
        psO = [ph.ps(f"psO{i}", [P, q * D]) for i in range(2)]
        ld, ready, trn, cpy = ph.sem("loaded"), ph.sem("rows_ready"), ph.sem("transposed"), ph.sem("copied")
        mm = [ph.sem(f"products{i}") for i in range(2)]
        out = [ph.sem(f"out{i}") for i in range(2)]
        st = [ph.sem(f"stored{i}") for i in range(2)]
        view = env["rel_t"].rearrange("(n r) d -> n (r d)", r=R)
        with nc.Block() as block:
            @block.sync
            def _(sp):
                for r in range(R):
                    sp.dma_start(w[:, :, r * D:(r + 1) * D],
                                 A["L1_gnn_W_rel"][r, :, :].rearrange("(k p) o -> p k o", p=P)).then_inc(ld, 16)
                with sp.Fori(0, NT) as t:
                    for s in range(2):
                        sp.wait_ge(out[s], t + 1)
                        sp.dma_start(view[bass.ds(t * P, P), s * q * D:(s + 1) * q * D], o[:, s, :]).then_inc(st[s], 16)
                for s in range(2):
                    sp.wait_ge(st[s], 16 * NT)

            @block.vector
            def _(v):
                def body(t):
                    v.wait_ge(mm[0], t + 1)
                    wait(v, st[0], 16 * t)
                    v.tensor_copy(o[:, 0, :], psO[0][:, :]).then_inc(out[0], 1)
                body(0)
                with v.Fori(1, NT) as t:
                    body(t)

            @block.tensor
            def _(pe):
                pe.wait_ge(ld, 16 * R)

                def transpose(t, u):
                    pe.wait_ge(ready, t + 1)
                    wait(pe, cpy, t - 1)
                    for k in range(2):
                        last = pe.transpose(psT[u][:, k * P:(k + 1) * P], rows[:, u, k, :], env["ident"][:, :])
                    last.then_inc(trn, 1)

                def product(t, u):
                    pe.wait_ge(cpy, t + 1)
                    for s in range(2):
                        wait(pe, out[s], t)
                        for a in range(s * q * D, (s + 1) * q * D, 512):
                            for k in range(2):
                                last = pe.matmul(psO[s][:, a - s * q * D:a - s * q * D + 512], rowsT[:, u, k, :],
                                                 w[:, k, a:a + 512], start=(k == 0), stop=(k == 1))
                        last.then_inc(mm[s], 1)

                def body(j):
                    transpose(2 * j + 1, 1)
                    product(2 * j, 0)
                    transpose(2 * j + 2, 0)
                    product(2 * j + 1, 1)
                transpose(0, 0)
                body(0)
                with pe.Fori(1, NT // 2 - 1) as j:
                    body(j)
                transpose(NT - 1, 1)
                product(NT - 2, 0)
                product(NT - 1, 1)

            @block.scalar
            def _(act):
                def norm(t, u):
                    wait(act, trn, t - 1)
                    normed(env, act, flat(rows[:, u, :, :]), t).then_inc(ready, 1)

                def copy(t, u):
                    act.wait_ge(trn, t + 1)
                    wait(act, mm[1], t - 1)
                    act.copy(flat(rowsT[:, u, :, :]), psT[u][:, 0:2 * P]).then_inc(cpy, 1)

                def half(t):
                    act.wait_ge(mm[1], t + 1)
                    wait(act, st[1], 16 * t)
                    act.copy(o[:, 1, :], psO[1][:, :]).then_inc(out[1], 1)

                def body(j):
                    for u in range(2):
                        t = 2 * j + u
                        norm(t + 2, u)
                        copy(t + 1, 1 - u)
                        half(t)
                norm(0, 0)
                norm(1, 1)
                copy(0, 0)
                body(0)
                with act.Fori(1, NT // 2 - 1) as j:
                    body(j)
                copy(NT - 1, 1)
                half(NT - 2)
                half(NT - 1)


def layer1_end(env):
    nc, A, X, Hh = env["nc"], env["A"], env["X"], env["Hh"]
    stats = env["stats"]
    d = Dense(env, "e1", D)
    with d.ph as ph:
        w = ph.sb("w", [P, 2, D])
        bias, gam, bet = ph.sb("bias", [P, D]), ph.sb("gam", [P, D]), ph.sb("bet", [P, D])
        ag = ph.sb("ag", [P, 2, D])
        cv, gl, y = ph.sb("cv", [P, 2, D]), ph.sb("gl", [P, 2, D]), ph.sb("y", [P, 2 * GL, D])
        ld, fin, turn, yr, yu, xa = (ph.sem(n) for n in ("loaded", "stats_in", "turn", "y_ready", "y_used", "x_beta"))
        lk2 = ph.sem("link2")
        got = [ph.sem(f"got{i}") for i in range(2)]
        sc = Scales(env, ph)
        with nc.Block() as block:
            @block.sync
            def _(sp):
                sp.dma_start(w[:, :, :], A["L1_gnn_W_root"].rearrange("(k p) o -> p k o", p=P)).then_inc(ld, 16)
                load_rows(sp, ld, [(bias[:, :], A["L1_gnn_bias"]), (gam[:, :], A["L1_gnn_ln_gamma"]),
                                   (bet[:, :], A["L1_gnn_ln_beta"])])
                tile_loads(d, sp, ag, got, env["agg_d"][0])

            @block.vector
            def _(v):
                v.wait_ge(ld, 64)

                def post(a, c):
                    t, u, h = a.t, a.u, a.h
                    v.wait_ge(got[u], 16 * (h + 1))
                    c(v.tensor_tensor(y[:, u, :], ag[:, u, :], bias[:, :], ALU.add))
                    return v.tensor_tensor(cv[:, u, :], d.psO[u][:, :], y[:, u, :], ALU.add)

                def end(a, c):
                    t, u = a.t, a.u
                    c(v.tensor_tensor(tile_of(Hh, t), tile_of(Hh, t), gl[:, u, :], ALU.add))
                    v.sem_inc(turn, 1)
                    v.bn_stats(tile_of(stats, t), tile_of(Hh, t)).then_inc(fin, 1)
                d.dve(v, None, post, 0, 1, end, 1)
                v.wait_ge(fin, NT)
                sc.dve(v)
                v.wait_ge(xa, NT)

                def update(g, half):
                    c = Chain(v, lk2, 2 * g)
                    yg = y[:, half * GL:(half + 1) * GL, :]
                    xg = X[:, bass.ds(GL * g, GL), :]
                    v.wait_ge(yr, g + 1)
                    c(v.tensor_tensor(yg, yg, gam[:, :].unsqueeze(1).to_broadcast([P, GL, D]), ALU.mult))
                    c(v.tensor_tensor(xg, xg, yg, ALU.add))
                    v.sem_inc(turn, 1)
                    for k in range(GL):
                        v.bn_stats(tile_of(stats, GL * g + k), tile_of(X, GL * g + k)).then_inc(fin, 1)
                with v.Fori(0, NT // (2 * GL)) as j:
                    for half in range(2):
                        update(2 * j + half, half)
                v.wait_ge(fin, 2 * NT)

            @block.tensor
            def _(pe):
                pe.wait_ge(ld, 64)
                d.pe(pe, lambda k: w[:, k, :])

            @block.gpsimd
            def _(pool):
                pool.wait_ge(ld, 64)

                def body(t):
                    pool.wait_ge(d.rows_ready, t + 1)
                    pool.tensor_tensor(tile_of(X, t), tile_of(X, t), bet[:, :], ALU.add).then_inc(xa, 1)
                with pool.Fori(0, NT) as t:
                    body(t)

            @block.scalar
            def _(act):
                def pre(a):
                    normed(env, act, tile_of(Hh, a.t), a.t)
                    return normed(env, act, flat(d.rows[:, a.u, :, :]), a.t)
                d.act(act, lambda a: act.activation(gl[:, a.u, :], cv[:, a.u, :], ACT.Gelu), pre)
                sc.act(act)

                def rows(g, half):
                    wait(act, lk2, 2 * g - 2)
                    for k in range(GL):
                        t = GL * g + k
                        last = act.activation(y[:, half * GL + k, :], tile_of(Hh, t), ACT.Identity,
                                              bias=env["nmr"][:, bass.ds(t, 1)], scale=env["rstd"][:, bass.ds(t, 1)])
                    last.then_inc(yr, 1)
                rows(0, 0)
                rows(1, 1)
                with act.Fori(1, NT // (2 * GL)) as j:
                    for half in range(2):
                        rows(2 * j + half, half)
    next_scales(env, "s2")


def next_scales(env, name):
    nc = env["nc"]
    with Phase(nc, name) as ph:
        sc = Scales(env, ph)
        with nc.Block() as block:
            @block.vector
            def _(v):
                sc.dve(v)

            @block.scalar
            def _(act):
                sc.act(act)


def layer2_tables(env):
    nc, A, X, Hh = env["nc"], env["A"], env["X"], env["Hh"]
    d = Dense(env, "t2", D)
    with d.ph as ph:
        w = ph.sb("w", [P, 2, D])
        att = ph.sb("att", [P, H, 2 * F])
        o = ph.sb("o", [P, 2, H * (F + 1) + H])
        pr = ph.sb("pr", [P, 2, 2, D])
        ld, ones = ph.sem("loaded"), ph.sem("ones")
        st = [ph.sem(f"stored{i}") for i in range(2)]
        heads = lambda ap, n=F: ap.rearrange("p (h f) -> p h f", f=n)
        with nc.Block() as block:
            @block.sync
            def _(sp):
                for h in range(H):
                    sp.dma_start(w[:, :, h * F:(h + 1) * F], A["L2_gnn_W"][h, :, :].rearrange("(k p) f -> p k f", p=P))\
                        .then_inc(ld, 16)
                sp.dma_start(att[:, :, :].rearrange("p h f -> p (h f)"),
                             A["L2_gnn_att"].rearrange("h f -> (h f)").rearrange("(a n) -> a n", a=1)
                             .partition_broadcast(P)).then_inc(ld, 16)
                sp.wait_ge(ld, 80)
                tile_stores(d, sp, [(o, st, lambda t: env["z_t"][bass.ds(t * P, P), :])])

            @block.vector
            def _(v):
                v.memset(o[:, :, :], 1.0).then_inc(ones, 1)
                v.memset(env["ed_sb"][:, :], 1.0).then_inc(ones, 1)
                v.wait_ge(ones, 2)
                v.wait_ge(ld, 80)

                def post(a, c):
                    t, u, h = a.t, a.u, a.h
                    wait(v, st[u], 16 * h)
                    z = heads(d.psO[u][:, :])
                    c(v.tensor_copy(heads(o[:, u, 0:H * (F + 1)], F + 1)[:, :, 0:F], z))
                    for k in range(2):
                        c(v.tensor_tensor(heads(pr[:, u, k, :]), z, att[:, :, k * F:(k + 1) * F], ALU.mult))
                    c(v.tensor_reduce(env["ed_sb"][:, bass.ds(t * (H + 1), H)], heads(pr[:, u, 1, :]), AX.X, ALU.add))
                    return v.tensor_reduce(o[:, u, H * (F + 1):], heads(pr[:, u, 0, :]), AX.X, ALU.add)
                d.dve(v, None, post, 0, 4)

            @block.tensor
            def _(pe):
                pe.wait_ge(ld, 80)
                d.pe(pe, lambda k: w[:, k, :])

            @block.scalar
            def _(act):
                d.act(act, pre=lambda a: normed(env, act, flat(d.rows[:, a.u, :, :]), a.t))


WZ = H * (F + 1)
WR = WZ + H
LW = P + 3
HS = H * U
NG = ITEMS // U
NA = 4
ALAG = 3


def item_links(env):
    nc = env["nc"]
    with Phase(nc, "lk") as ph:
        d = ph.sb("d", [P, IG, P + 2])
        l = ph.sb("l", [P, IG, LW])
        filled, loaded, dv, rdy, put = (ph.sem(n) for n in ("filled", "loaded", "link", "ready", "put"))
        src = env["item_gdst_d"]
        full = (IG - 1) * P
        with nc.Block() as block:
            @block.sync
            def _(sp):
                sp.wait_ge(filled, 1)
                sp.dma_start(d[:, 0:IG - 1, 1:P + 1], src[0:full, :].rearrange("(g p) e -> p g e", p=P)).then_inc(loaded, 16)
                sp.dma_start(d[0:ITEMS - full, IG - 1, 1:P + 1], src[full:ITEMS, :]).then_inc(loaded, 16)
                with nc.allow_non_contiguous_dma("one value per item"):
                    for g in range(IG):
                        a, b = max(g * P, 1), min(g * P + P, ITEMS)
                        sp.dma_start(d[a - g * P:b - g * P, g, 0:1], src[a - 1:b - 1, P - 1:P]).then_inc(loaded, 16)
                        b = min(g * P + P, ITEMS - 1)
                        sp.dma_start(d[0:b - g * P, g, P + 1:P + 2], src[g * P + 1:b + 1, 0:1]).then_inc(loaded, 16)
                sp.wait_ge(rdy, 2)
                sp.dma_start(env["link_d"][0:full, :].rearrange("(g p) e -> p g e", p=P), l[:, 0:IG - 1, :]).then_inc(put, 16)
                sp.dma_start(env["link_d"][full:ITEMS, :], l[0:ITEMS - full, IG - 1, :]).then_inc(put, 16)
                sp.wait_ge(put, 32)

            @block.vector
            def _(v):
                v.memset(d[:, :, :], -1.0).then_inc(filled, 1)
                v.wait_ge(loaded, 16 * (2 + 2 * IG))
                c = Chain(v, dv)
                links = l[:, :, 0:P + 1]
                c(v.tensor_tensor(links, d[:, :, 1:P + 2], d[:, :, 0:P + 1], ALU.is_equal))
                c(v.tensor_scalar(links, links, BIG, -BIG, ALU.mult, ALU.add))
                v.tensor_reduce(l[:, :, P + 1], l[:, :, 0:P], AX.X, ALU.min).then_inc(rdy, 1)
                v.tensor_reduce(l[:, :, P + 2], l[:, :, 1:P + 1], AX.X, ALU.min).then_inc(rdy, 1)


K_SCORE, K_SELECT, K_LOCAL, K_CARRY, K_MAX, K_EXP = 8, 9, 10, 12, 13, 14
Q = U // 4


def more(g, n):
    return not (isinstance(g, int) and g >= NG - n)


def groups(engine, step):
    for g in range(3):
        step(g, g % 2, g // 2)
    with engine.Fori(1, (NG - 1) // 2 - 1) as j:
        step(2 * j + 1, 1, j)
        step(2 * j + 2, 0, j + 1)
    for g in range(NG - 2, NG):
        step(g, g % 2, g // 2)


def tile_tables(env, ph, edi, b):
    nc = env["nc"]
    W = H + 1
    half = ITEMS // 2
    row, edT, parts, pt, ps, pidx = (b[n] for n in ("row", "edT", "parts", "pt", "ps", "pidx"))
    oh = ph.sb("oh_tiles", [P, ITEMS], BF16)
    loaded, iota_in, hot, turned, split, link, summed, one = (ph.sem(n) for n in (
        "tiles_in", "iota_in", "one_hot", "ed_turned", "ed_split", "split_link", "ed_items", "ones_in"))
    done = [ph.sem(f"ed_copied{i}") for i in range(2)]

    def copies(engine, copy, a):
        for w in range(3 * H):
            engine.wait_ge(summed, 2 * w + a + 1)
            copy(edi[:, a * half:(a + 1) * half, w], ps[(2 * w + a) % NA][:, 0:half]).then_inc(done[a], 1)
        engine.wait_ge(done[a], 3 * H)

    with nc.Block() as block:
        @block.gpsimd
        def _(pool):
            pool.iota(pidx[:, :], pattern=[[0, 1]], base=0, channel_multiplier=1,
                      allow_small_or_imprecise_dtypes=True).then_inc(iota_in, 1)

        @block.sync
        def _(sp):
            sp.dma_start(row[:, 0:ITEMS], env["item_d"][1:2, 0:ITEMS].partition_broadcast(P)).then_inc(loaded, 16)

        @block.tensor
        def _(pe):
            for w in range(H):
                last = pe.transpose(pt[0:NT, w * P:(w + 1) * P], env["ed_sb"][:, w:NT * W:W], env["ident"][:, :])
            last.then_inc(turned, 1)
            pe.wait_ge(split, 1)
            pe.wait_ge(hot, 1)
            for w in range(3 * H):
                for a in range(2):
                    wait(pe, done[a], w - 1)
                    pe.matmul(ps[(2 * w + a) % NA][:, 0:half], parts[0:NT, w * P:(w + 1) * P],
                              oh[0:NT, a * half:(a + 1) * half], start=True, stop=True).then_inc(summed, 1)

        @block.vector
        def _(v):
            c = Chain(v, link)
            v.memset(edi[:, :, 3 * H], 1.0).then_inc(one, 1)
            v.wait_ge(iota_in, 1)
            v.wait_ge(loaded, 16)
            v.tensor_scalar(oh[0:NT, :], row[0:NT, 0:ITEMS], pidx[0:NT, 0:1], None, ALU.is_equal).then_inc(hot, 1)
            v.wait_ge(turned, 1)
            rest = edT[0:NT, :, 0:P]
            part = lambda q: parts[0:NT, q * H * P:(q + 1) * H * P].rearrange("p (w n) -> p w n", w=H)
            c(v.tensor_copy(rest, pt[0:NT, :].rearrange("p (w n) -> p w n", w=H)))
            for q in range(2):
                c(v.tensor_copy(part(q), rest))
                c(v.tensor_tensor(rest, rest, part(q), ALU.subtract))
            v.tensor_copy(part(2), rest).then_inc(split, 1)
            v.wait_ge(one, 1)
            copies(v, v.tensor_copy, 0)

        @block.scalar
        def _(act):
            copies(act, act.copy, 1)


def attention(env):
    nc = env["nc"]
    target = env["agg_d"][1]
    W = 3 * H + 1
    with Phase(nc, "at") as ph:
        G = env["Hh"][:, :, :].rearrange("p t d -> p (t d)")[:, 0:2 * U * WR].rearrange("p (b k w) -> p b k w", b=2, k=U)
        r_idx = ph.sb("r_idx", [P, 2, U], I32)
        r_dst, r_keep = ph.sb("r_dst", [P, 2, U]), ph.sb("r_keep", [P, 2, U])
        drow, sel = ph.sb("drow", [P, 2, U * P]), ph.sb("sel", [P, U * P], BF16)
        pidx, oh = ph.sb("pidx", [P, 1]), ph.sb("oh", [P, 2])
        x, y, z = ph.sb("x", [P, U, H]), ph.sb("y", [P, U, H]), ph.sb("z", [P, U, H])
        pen = ph.sb("pen", [P, U])
        e = ph.sb("e", [P, H, U])
        lk = ph.sb("lk", [HS, 2, LW])
        ev, fw, bw, ex = (ph.sb(n, [HS, P]) for n in ("ev", "fw", "bw", "ex"))
        add_f, in_f, out_f, add_b, in_b, out_b = (ph.sb(n, [1, H, U + 1]) for n in (
            "add_f", "in_f", "out_f", "add_b", "in_b", "out_b"))
        enter = ph.sb("enter", [1, 2, H, U])
        cd = ph.sb("cd", [HS, 2])
        fd, fe, one = ph.sb("fd", [1, H]), ph.sb("fe", [1, H]), ph.sb("one", [1, P])
        noh, fac, accr = ph.sb("noh", [P, 1]), ph.sb("fac", [P, H]), ph.sb("accr", [P, WZ])
        r_ex = ph.sb("r_ex", [P, 2, H, U])
        tmp = ph.sb("tmp", [P, NA, P])
        S, gw, acc = ph.sb("S", [P, NA, P]), ph.sb("gw", [P, NA, WZ]), ph.sb("acc", [P, U, WZ])
        ps = [ph.ps(f"ps{i}", [P, 512]) for i in range(NA)]
        pd, pe_t, px, pm = (ph.ps(n, [P, 512]) for n in ("pd", "pe_t", "px", "pm"))
        ed = pd[:, 0:U * W].rearrange("p (k w) -> p k w", w=W)
        tots = pm[0:1, 0:4 * HS].rearrange("p (q h s) -> p q h s", q=4, h=H)
        back, facs = pm[0:HS, 4 * HS:4 * HS + 2], pm[:, 4 * HS + 4:4 * HS + 4 + H]
        const, past, go, staged, cols, link, selected, looked, scored, turned, ev_in = (ph.sem(n) for n in (
            "const", "past", "go", "staged", "columns", "link", "selected", "looked_up", "scored", "scores_turned",
            "scores_in"))
        local, tots_out, tots_in, carried, packed, carries_in, carries_out, differ, factor, factors_in = (
            ph.sem(n) for n in ("local_scans", "totals_out", "totals_in", "carries", "packed", "carries_in",
                                "carries_out", "difference", "factor", "factors_in"))
        shifted, exps, turned_back, ex_in, apart, built, scaled, products, added = (ph.sem(n) for n in (
            "shifted", "exps", "exps_turned", "exps_in", "distances", "selections", "scaled", "products", "added"))
        gs = [ph.sem(f"gathered{i}") for i in range(2)]
        rl = [ph.sem(f"rows_loaded{i}") for i in range(2)]
        st = [ph.sem(f"stored{k}") for k in range(U)]
        CN = 17
        edi = ph.sb("edi", [P, ITEMS, W], BF16)
        tile_tables(env, ph, edi, dict(row=drow[:, 0, :], edT=gw, parts=sel, pt=pm, ps=ps, pidx=pidx))
        with nc.Block() as block:
            @block.gpsimd
            def _(pool):
                lim = pool.to_reg(N - 1)
                pool.wait_ge(const, 9)

                def step(g, b, n):
                    for q in range(U // Q):
                        pool.wait_ge(staged, U // Q * g + q + 1)
                        pool.sem_inc(go, 1)
                        for k in range(q * Q, (q + 1) * Q):
                            pool.indirect_dma_start(out=G[:, b, k, :], out_offset=None, in_=env["z_t"][:, :],
                                                    in_offset=bass.IndirectOffsetOnAxis(ap=r_idx[:, b, k:k + 1], axis=0),
                                                    bounds_check=lim, oob_is_err=False).then_inc(gs[b], 16)
                groups(pool, step)

            @block.sync
            def _(sp):
                flat_dst = env["item_ldst_d"].rearrange("c e -> (c e)").rearrange("(a n) -> a n", a=1)

                def load(g, b):
                    sp.dma_start(drow[:, b, :], flat_dst[:, bass.ds(g * U * P, U * P)].partition_broadcast(P))\
                        .then_inc(rl[b], 16)
                    for h in range(H):
                        sp.dma_start(lk[h * U:(h + 1) * U, b, :], env["link_d"][bass.ds(g * U, U), :]).then_inc(rl[b], 16)

                def step(g, b, n):
                    if more(g, 2):
                        sp.wait_ge(shifted, g + 1)
                        load(g + 2, b)
                    for k in range(U):
                        i = U * g + k
                        row = sp.value_load(env["item_row"][0:1, bass.ds(i, 1)], min_val=0, max_val=NT - 1)
                        sp.wait_ge(added, i + 1)
                        sp.dma_start(target[bass.ds(row * P, P), :], acc[:, k, :], cond=row < RT).then_inc(st[k], 16)
                load(0, 0)
                load(1, 1)
                groups(sp, step)
                for k in range(U):
                    sp.wait_ge(st[k], 16 * NG)

            @block.scalar
            def _(act):
                def stage(g, b, q):
                    act.copy(r_idx[:, b, q * Q:(q + 1) * Q], env["item_src"][:, bass.ds(g * U + q * Q, Q)])\
                        .then_inc(staged, 1)

                def columns(g, b):
                    wait(act, added, U * (g - 1))
                    act.copy(r_dst[:, b, :], env["item_dst"][:, bass.ds(U * g, U)]).then_inc(cols, 1)
                    act.copy(r_keep[:, b, :], env["item_keep"][:, bass.ds(U * g, U)]).then_inc(cols, 1)

                def distance(i, k, b):
                    wait(act, built, i - NA + 1)
                    act.activation(tmp[:, k % NA, :], env["iota"][:, :], ACT.Abs, bias=r_dst[:, b, k:k + 1],
                                   scale=-1.0).then_inc(apart, 1)

                def select(i, k):
                    act.wait_ge(apart, i + 1)
                    wait(act, products, i - NA + 1)
                    act.activation(S[:, k % NA, :], tmp[:, k % NA, :], ACT.Relu, bias=env["one_c"][:, 0:1],
                                   scale=-1.0).then_inc(built, 1)

                def scores_in(g):
                    act.wait_ge(turned, g + 1)
                    act.copy(ev[:, :], pe_t[0:HS, 0:P]).then_inc(ev_in, 1)

                def totals_in(g):
                    act.wait_ge(tots_out, g + 1)
                    for q, a in enumerate((in_f[:, :, 1:U + 1], add_f[:, :, 1:U + 1], in_b[:, :, 0:U], add_b[:, :, 0:U])):
                        act.copy(a, tots[:, q, :, :]).then_inc(tots_in, 1)

                def exponentials(g, b):
                    act.wait_ge(differ, g + 1)
                    act.activation(fe[:, :], fd[:, :], ACT.Exp).then_inc(factor, 1)
                    act.wait_ge(shifted, g + 1)
                    act.activation(ex[:, :], ex[:, :], ACT.Exp).then_inc(exps, 1)
                    act.wait_ge(turned_back, g + 1)
                    act.copy(flat(r_ex[:, b, :, :]), px[:, 0:HS]).then_inc(ex_in, 1)

                def step(g, b, n):
                    i = U * g
                    act.wait_ge(cols, 2 * g + 2)
                    distance(i, 0, b)
                    for k in range(U):
                        if k + 1 < U:
                            distance(i + k + 1, k + 1, b)
                        select(i + k, k)
                        if k in (Q + 1, 2 * Q + 1, 3 * Q + 1) and more(g, 2):
                            act.wait_ge(scaled, i + k - 1)
                            stage(g + 2, b, k // Q - 1)
                        if k == K_LOCAL and more(g, 1):
                            scores_in(g + 1)
                            columns(g + 1, 1 - b)
                        if k == K_CARRY and more(g, 1):
                            totals_in(g + 1)
                    if more(g, 1):
                        exponentials(g + 1, 1 - b)
                    if more(g, 2):
                        act.wait_ge(scaled, i + U)
                        stage(g + 2, b, U // Q - 1)
                act.wait_ge(const, 9)
                for g in range(2):
                    for q in range(U // Q):
                        stage(g, g, q)
                columns(0, 0)
                scores_in(0)
                totals_in(0)
                exponentials(0, 0)
                groups(act, step)

            @block.vector
            def _(v):
                for a, value in ((G, 0.0), (acc[:, U - 1, :], 0.0), (add_f[:, :, :], -4 * BIG), (add_b[:, :, :], -4 * BIG),
                                 (in_f[:, :, :], -BIG), (in_b[:, :, :], -BIG), (out_f[:, :, :], -BIG), (one[:, :], 1.0),
                                 (env["one_c"][:, :], 1.0)):
                    v.memset(a, value).then_inc(const, 1)
                v.wait_ge(const, 9)

                def select(g, b, n):
                    v.wait_ge(rl[b], 16 * (H + 1) * (n + 1))
                    wait(v, looked, g)
                    v.tensor_scalar(sel[:, :], drow[:, b, :], pidx[:, 0:1], None, ALU.is_equal).then_inc(selected, 1)
                    v.tensor_scalar(oh[:, b:b + 1], drow[:, b, 0:1], pidx[:, 0:1], None, ALU.is_equal)\
                        .then_inc(selected, 1)

                def scale(i, k, b):
                    wait(v, products, i - NA + 1)
                    return v.tensor_tensor(gw[:, k % NA, :].rearrange("p (h f) -> p h f", h=H),
                                           G[:, b, k, 0:WZ].rearrange("p (h f) -> p h f", h=H),
                                           r_ex[:, b, :, k:k + 1].to_broadcast([P, H, F + 1]), ALU.mult)\
                        .then_inc(scaled, 1)

                def add(i, k, b, g):
                    v.wait_ge(products, i + 1)
                    wait(v, added, i)
                    wait(v, st[k], 16 * g)
                    before = acc[:, k - 1, :] if k else accr[:, :]
                    v.scalar_tensor_tensor(out=acc[:, k, :], in0=before, scalar=r_keep[:, b, k:k + 1],
                                           in1=ps[k % NA][:, 0:WZ], op0=ALU.mult, op1=ALU.add).then_inc(added, 1)

                C_LOCAL, C_CARRY, C_MAX, C_REBASE = 8, 9, 10, 14

                def score(g, b, n):
                    c = Chain(v, link, CN * g)
                    v.wait_ge(gs[b], 16 * U * (n + 1))
                    v.wait_ge(looked, g + 1)
                    c(v.tensor_copy(y[:, :, :], ed[:, :, 0:H]))
                    c(v.tensor_tensor(y[:, :, :], y[:, :, :], ed[:, :, H:2 * H], ALU.add))
                    c(v.tensor_tensor(y[:, :, :], y[:, :, :], ed[:, :, 2 * H:3 * H], ALU.add))
                    c(v.tensor_tensor(x[:, :, :], y[:, :, :], G[:, b, :, WZ:WR], ALU.add))
                    c(v.tensor_scalar(pen[:, :], ed[:, :, 3 * H], BIG, -BIG, ALU.mult, ALU.add))
                    xf = flat(x[:, :, :])
                    c(v.scalar_tensor_tensor(out=flat(y[:, :, :]), in0=xf, scalar=0.01, in1=xf, op0=ALU.mult,
                                             op1=ALU.max))
                    c(v.tensor_scalar(z[:, :, :], y[:, :, :], 0.0, -1000.0, ALU.is_equal, ALU.mult))
                    c(v.tensor_tensor(z[:, :, :], z[:, :, :], pen[:, :].unsqueeze(2).to_broadcast([P, U, H]), ALU.add))
                    v.tensor_tensor(e[:, :, :].rearrange("p h s -> p s h"), y[:, :, :], z[:, :, :], ALU.add)\
                        .then_inc(scored, 1)
                    assert c.n == C_LOCAL

                def local_scans(g, b):
                    c = Chain(v, link, CN * g + C_LOCAL)
                    v.wait_ge(ev_in, g + 1)
                    v.tensor_tensor_scan(fw[:, :], lk[:, b, 0:P], ev[:, :], -BIG, ALU.add, ALU.max).then_inc(local, 1)
                    v.tensor_tensor_scan(bw[:, ::-1], lk[:, b, P:0:-1], ev[:, ::-1], -BIG, ALU.add, ALU.max)\
                        .then_inc(local, 1)
                    c(v.tensor_copy(in_f[:, :, 0], out_f[:, :, U]))
                    assert c.n == C_CARRY - C_LOCAL

                def carries(g):
                    c = Chain(v, link, CN * g + C_CARRY)
                    v.wait_ge(tots_in, 4 * g + 4)
                    row = lambda a: a[:, :, :].rearrange("p h s -> p (h s)")
                    v.tensor_tensor_scan(row(out_f), row(add_f), row(in_f), -BIG, ALU.add, ALU.max).then_inc(carried, 1)
                    v.tensor_tensor_scan(row(out_b)[:, ::-1], row(add_b)[:, ::-1], row(in_b)[:, ::-1], -BIG,
                                         ALU.add, ALU.max).then_inc(carried, 1)
                    v.wait_ge(carried, 2 * g + 2)
                    v.tensor_copy(enter[:, 0, :, :], out_f[:, :, 0:U]).then_inc(packed, 1)
                    v.tensor_copy(enter[:, 1, :, :], out_b[:, :, 1:U + 1]).then_inc(packed, 1)
                    c(v.tensor_tensor(fd[:, :], in_f[:, :, 0], out_b[:, :, 0], ALU.subtract))
                    v.tensor_scalar(fd[:, :], fd[:, :], 0.0, None, ALU.min).then_inc(differ, 1)
                    assert c.n == C_MAX - C_CARRY

                def maxima(g, b):
                    c = Chain(v, link, CN * g + C_MAX)
                    v.wait_ge(carries_in, g + 1)
                    c(v.tensor_copy(cd[:, :], back))
                    v.sem_inc(carries_out, 1)
                    c(v.tensor_tensor_scan(fw[:, :], lk[:, b, 0:P], ev[:, :], cd[:, 0:1], ALU.add, ALU.max))
                    c(v.tensor_tensor_scan(bw[:, ::-1], lk[:, b, P:0:-1], ev[:, ::-1], cd[:, 1:2], ALU.add, ALU.max))
                    c(v.tensor_tensor(fw[:, :], fw[:, :], bw[:, :], ALU.max))
                    v.tensor_tensor(ex[:, :], ev[:, :], fw[:, :], ALU.subtract).then_inc(shifted, 1)
                    assert c.n == C_REBASE - C_MAX

                def rebase(g, b):
                    c = Chain(v, link, CN * g + C_REBASE)
                    v.wait_ge(selected, 2 * g + 2)
                    c(v.tensor_scalar(noh[:, :], oh[:, b:b + 1], -1.0, 1.0, ALU.mult, ALU.add))
                    v.wait_ge(factors_in, g + 1)
                    c(v.tensor_scalar(fac[:, :], facs, oh[:, b:b + 1], noh[:, 0:1], ALU.mult, ALU.add))
                    wait(v, added, U * g)
                    c(v.tensor_tensor(accr[:, :].rearrange("p (h f) -> p h f", h=H),
                                      acc[:, U - 1, :].rearrange("p (h f) -> p h f", h=H),
                                      fac[:, :].unsqueeze(2).to_broadcast([P, H, F + 1]), ALU.mult))
                    assert c.n == CN - C_REBASE

                def step(g, b, n):
                    v.wait_ge(ex_in, g + 1)
                    v.wait_ge(cols, 2 * g + 2)
                    for k in range(U):
                        scale(U * g + k, k, b)
                        if k >= ALAG:
                            add(U * g + k - ALAG, k - ALAG, b, g)
                        elif not (isinstance(g, int) and g == 0):
                            add(U * g + k - ALAG, U + k - ALAG, 1 - b, g - 1)
                        if k == ALAG - 1:
                            rebase(g, b)
                        if k == K_SCORE and more(g, 1):
                            score(g + 1, 1 - b, n + b)
                        if k == K_SELECT and more(g, 2):
                            select(g + 2, b, n + 1)
                        if k == K_LOCAL and more(g, 1):
                            local_scans(g + 1, 1 - b)
                        if k == K_CARRY and more(g, 1):
                            carries(g + 1)
                        if k == K_MAX and more(g, 1):
                            maxima(g + 1, 1 - b)
                select(0, 0, 0)
                score(0, 0, 0)
                local_scans(0, 0)
                carries(0)
                maxima(0, 0)
                select(1, 1, 0)
                groups(v, step)
                for k in range(U - ALAG, U):
                    add(U * (NG - 1) + k, k, (NG - 1) % 2, NG - 1)

            @block.tensor
            def _(pe):
                ident = env["ident"]

                def look(g, items):
                    for k in items:
                        if k == 0:
                            pe.wait_ge(selected, 2 * g + 2)
                        last = pe.matmul(pd[:, k * W:(k + 1) * W], sel[:, k * P:(k + 1) * P],
                                         edi[:, bass.ds(g * U + k, 1), :].rearrange("p a w -> p (a w)"),
                                         start=True, stop=True)
                        if k == U - 1:
                            last.then_inc(looked, 1)

                def turn(g):
                    pe.wait_ge(scored, g + 1)
                    pe.sem_inc(past, 1)
                    pe.transpose(pe_t[0:HS, 0:P], flat(e[:, :, :]), ident[:, :]).then_inc(turned, 1)

                def totals(g, b):
                    pe.wait_ge(local, 2 * g + 2)
                    pe.sem_inc(past, 1)
                    for q, a in enumerate((fw[:, P - 1:P], lk[:, b, P + 1:P + 2], bw[:, 0:1], lk[:, b, P + 2:P + 3])):
                        last = pe.transpose(pm[0:1, q * HS:(q + 1) * HS], a, ident[0:HS, 0:HS])
                    last.then_inc(tots_out, 1)

                def carries(g):
                    pe.wait_ge(packed, 2 * g + 2)
                    pe.sem_inc(past, 1)
                    for q in range(2):
                        last = pe.transpose(back[:, q:q + 1], enter[:, q, :, :].rearrange("p h s -> p (h s)"),
                                            ident[0:1, 0:1])
                    last.then_inc(carries_in, 1)

                def exponentials(g):
                    pe.wait_ge(factor, g + 1)
                    pe.wait_ge(carries_out, g + 1)
                    pe.matmul(facs, one[:, :], fe[:, :], start=True, stop=True).then_inc(factors_in, 1)
                    pe.wait_ge(exps, g + 1)
                    pe.sem_inc(past, 1)
                    pe.transpose(px[:, 0:HS], ex[:, :], ident[0:HS, 0:HS]).then_inc(turned_back, 1)

                def step(g, b, n):
                    for k in range(U):
                        i = U * g + k
                        pe.wait_ge(built, i + 1)
                        pe.wait_ge(scaled, i + 1)
                        wait(pe, added, i - NA + 1)
                        pe.matmul(ps[k % NA][:, 0:WZ], S[:, k % NA, :], gw[:, k % NA, :], start=True, stop=True)\
                            .then_inc(products, 1)
                        if more(g, 1) and k < U // 2:
                            look(g + 1, (U // 2 + k,))
                        if more(g, 2) and k >= U * 3 // 4:
                            look(g + 2, (2 * k - U * 3 // 2, 2 * k - U * 3 // 2 + 1))
                        if more(g, 1):
                            if k == K_SCORE:
                                turn(g + 1)
                            if k == K_LOCAL:
                                totals(g + 1, 1 - b)
                            if k == K_CARRY:
                                carries(g + 1)
                            if k == K_EXP:
                                exponentials(g + 1)
                look(0, range(U))
                turn(0)
                totals(0, 0)
                carries(0)
                exponentials(0)
                look(1, range(U // 2))
                groups(pe, step)


LAG = 4
NS = 8


def aggregate(env, name, layer, table, W, limit, idx, weight):
    nc = env["nc"]
    target = env["agg_d"][layer]
    with Phase(nc, name) as ph:
        G = ph.sb("G", [P, U, W])
        S = ph.sb("S", [P, NS, P])
        acc = ph.sb("acc", [P, U, W])
        r_idx = ph.sb("r_idx", [P, U], I32)
        r_dst, r_wgt, r_keep = (ph.sb(n, [P, U]) for n in ("r_dst", "r_wgt", "r_keep"))
        ps = [ph.ps(f"ps{i}", [P, W]) for i in range(NS)]
        staged, go, built, products, added, cleared = (ph.sem(n) for n in (
            "staged", "go", "selections", "products", "added", "cleared"))
        gs = [ph.sem(f"gathered{k}") for k in range(U)]
        st = [ph.sem(f"stored{k}") for k in range(U)]
        HU = U // 2
        with nc.Block() as block:
            @block.gpsimd
            def _(pool):
                lim = pool.to_reg(limit)
                pool.memset(G[:, :, :], 0.0).then_inc(cleared, 1)
                pool.wait_ge(cleared, 2)
                with pool.Fori(0, ITEMS // U) as j:
                    for half in range(2):
                        pool.wait_ge(staged, 2 * j + half + 1)
                        pool.sem_inc(go, 1)
                        for k in range(half * HU, (half + 1) * HU):
                            pool.indirect_dma_start(out=G[:, k, :], out_offset=None, in_=table[:, :],
                                                    in_offset=bass.IndirectOffsetOnAxis(ap=r_idx[:, k:k + 1], axis=0),
                                                    bounds_check=lim, oob_is_err=False).then_inc(gs[k], 16)

            @block.scalar
            def _(act):
                def body(j):
                    for half in range(2):
                        a, b = half * HU, (half + 1) * HU
                        wait(act, added, U * (j - 1) + b)
                        s = bass.ds(j * U + a, HU)
                        act.copy(r_dst[:, a:b], env["item_dst"][:, s])
                        act.copy(r_keep[:, a:b], env["item_keep"][:, s])
                        if weight == "wgt":
                            act.copy(r_wgt[:, a:b], env["item_wgt"][:, s])
                        act.copy(r_idx[:, a:b], idx[:, s]).then_inc(staged, 1)
                body(0)
                with act.Fori(1, ITEMS // U) as j:
                    body(j)

            @block.vector
            def _(v):
                v.memset(acc[:, U - 1, :], 0.0).then_inc(cleared, 1)
                v.wait_ge(cleared, 2)

                def select(i, k, j):
                    if k % HU == 0:
                        v.wait_ge(staged, 2 * j + k // HU + 1)
                    wait(v, products, i - NS + 1)
                    if weight == "wgt":
                        v.tensor_scalar(S[:, k % NS, :], env["iota"][:, :], r_dst[:, k:k + 1], r_wgt[:, k:k + 1],
                                        ALU.is_equal, ALU.mult).then_inc(built, 1)
                    else:
                        v.tensor_scalar(S[:, k % NS, :], env["iota"][:, :], r_dst[:, k:k + 1], None,
                                        ALU.is_equal).then_inc(built, 1)

                def add(i, k, h):
                    v.wait_ge(products, i + 1)
                    wait(v, added, i)
                    wait(v, st[k], 16 * h)
                    v.scalar_tensor_tensor(out=acc[:, k, :], in0=acc[:, (k - 1) % U, :], scalar=r_keep[:, k:k + 1],
                                           in1=ps[k % NS][:, :], op0=ALU.mult, op1=ALU.add).then_inc(added, 1)

                def body(j):
                    for k in range(U):
                        select(U * j + k, k, j)
                        if k >= LAG:
                            add(U * j + k - LAG, k - LAG, j)
                        elif not isinstance(j, int):
                            add(U * j + k - LAG, U + k - LAG, j - 1)
                body(0)
                with v.Fori(1, ITEMS // U) as j:
                    body(j)
                for k in range(U - LAG, U):
                    add(ITEMS - U + k, k, ITEMS // U - 1)

            @block.tensor
            def _(pe):
                def body(j):
                    for k in range(U):
                        i = U * j + k
                        pe.wait_ge(built, i + 1)
                        pe.wait_ge(gs[k], 16 * (j + 1))
                        wait(pe, added, i - NS + 1)
                        pe.matmul(ps[k % NS][:, :], S[:, k % NS, :], G[:, k, :],
                                  start=True, stop=True).then_inc(products, 1)
                body(0)
                with pe.Fori(1, ITEMS // U) as j:
                    body(j)

            @block.sync
            def _(sp):
                with sp.Fori(0, ITEMS // U) as j:
                    for k in range(U):
                        i = U * j + k
                        row = sp.value_load(env["item_row"][0:1, bass.ds(i, 1)], min_val=0, max_val=NT - 1)
                        sp.wait_ge(added, i + 1)
                        sp.dma_start(target[bass.ds(row * P, P), :], acc[:, k, :], cond=row < RT).then_inc(st[k], 16)
                for k in range(U):
                    sp.wait_ge(st[k], 16 * ITEMS // U)


def add_attention(env):
    nc, X = env["nc"], env["X"]
    W = H * (F + 1)
    with Phase(nc, "aa") as ph:
        g = ph.sb("g", [P, 2, GL, W])
        den, rec, o = ph.sb("den", [P, GL, H]), ph.sb("rec", [P, GL, H]), ph.sb("o", [P, GL, D])
        link, turn, fin = ph.sem("link"), ph.sem("turn"), ph.sem("stats_in")
        sc = Scales(env, ph)
        got = [ph.sem(f"got{i}") for i in range(2)]
        with nc.Block() as block:
            @block.sync
            def _(sp):
                def load(n, b):
                    wait(sp, link, 8 * (n - 2) + 7)
                    sp.dma_start(g[:, b, :, :], env["agg_d"][1][bass.ds(n * GL * P, GL * P), :]
                                 .rearrange("(t p) d -> p t d", p=P)).then_inc(got[b], 16)
                load(0, 0)
                load(1, 1)
                with sp.Fori(1, NT // (2 * GL)) as j:
                    for b in range(2):
                        load(2 * j + b, b)

            @block.vector
            def _(v):
                with v.Fori(0, NT // (2 * GL)) as j:
                    for b in range(2):
                        n = 2 * j + b
                        v.wait_ge(got[b], 16 * (j + 1))
                        gh = g[:, b, :, :].rearrange("p t (h f) -> p t h f", h=H)
                        c = Chain(v, link, 8 * n)
                        c(v.tensor_scalar(den[:, :, :], gh[:, :, :, F], 0.0, None, ALU.is_le))
                        c(v.tensor_tensor(den[:, :, :], den[:, :, :], gh[:, :, :, F], ALU.add))
                        c(v.reciprocal(rec[:, :, :], den[:, :, :]))
                        for h in range(H):
                            v.tensor_tensor(o[:, :, h * F:(h + 1) * F], gh[:, :, h, 0:F],
                                            rec[:, :, h:h + 1].to_broadcast([P, GL, F]), ALU.mult).then_inc(link, 1)
                        v.wait_ge(link, 8 * n + 7)
                        xg = X[:, bass.ds(GL * n, GL), :]
                        v.tensor_tensor(xg, xg, o[:, :, :], ALU.add).then_inc(link, 1)
                        v.wait_ge(link, 8 * n + 8)
                        v.sem_inc(turn, 1)
                        for k in range(GL):
                            v.bn_stats(tile_of(env["stats"], GL * n + k), tile_of(X, GL * n + k)).then_inc(fin, 1)
                v.wait_ge(fin, NT)
                sc.dve(v)

            @block.scalar
            def _(act):
                sc.act(act)


def prelu(v, c, out, x, alpha, tmp):
    c(v.scalar_tensor_tensor(out=tmp, in0=x, scalar=0.0, in1=alpha, op0=ALU.min, op1=ALU.mult))
    return v.scalar_tensor_tensor(out=out, in0=x, scalar=0.0, in1=tmp, op0=ALU.max, op1=ALU.add)


def layer3_tables(env):
    nc, A, X, Hh = env["nc"], env["A"], env["X"], env["Hh"]
    d = Dense(env, "p3", D)
    with d.ph as ph:
        w = ph.sb("w", [P, 2, D])
        bias, alpha = ph.sb("bias", [P, D]), ph.sb("alpha", [P, D])
        x, tmp = ph.sb("x", [P, 2, D]), ph.sb("tmp", [P, 2, D])
        ld = ph.sem("loaded")
        with nc.Block() as block:
            @block.sync
            def _(sp):
                sp.dma_start(w[:, :, :], A["L3_gnn_W_pre"].rearrange("(k p) o -> p k o", p=P)).then_inc(ld, 16)
                load_rows(sp, ld, [(bias[:, :], A["L3_gnn_b_pre"]), (alpha[:, :], A["L3_gnn_alpha_pre"])])

            @block.vector
            def _(v):
                v.wait_ge(ld, 48)

                def post(a, c):
                    t, u, h = a.t, a.u, a.h
                    c(v.tensor_tensor(x[:, u, :], d.psO[u][:, :], bias[:, :], ALU.add))
                    return prelu(v, c, tile_of(Hh, t), x[:, u, :], alpha[:, :], tmp[:, u, :])
                d.dve(v, None, post, 0, 2)

            @block.tensor
            def _(pe):
                pe.wait_ge(ld, 48)
                d.pe(pe, lambda k: w[:, k, :])

            @block.scalar
            def _(act):
                d.act(act, pre=lambda a: normed(env, act, flat(d.rows[:, a.u, :, :]), a.t))
    d = Dense(env, "m3", D)
    with d.ph as ph:
        w = ph.sb("w", [P, 2, D])
        bias, o = ph.sb("bias", [P, D]), ph.sb("o", [P, 2, D])
        ld = ph.sem("loaded")
        st = [ph.sem(f"stored{i}") for i in range(2)]
        with nc.Block() as block:
            @block.sync
            def _(sp):
                sp.dma_start(w[:, :, :], A["L3_gnn_W_mp"].rearrange("(k p) o -> p k o", p=P)).then_inc(ld, 16)
                load_rows(sp, ld, [(bias[:, :], A["L3_gnn_b_mp"])])
                tile_stores(d, sp, [(o, st, lambda t: env["m_t"][bass.ds(t * P, P), :])])

            @block.vector
            def _(v):
                v.wait_ge(ld, 32)

                def post(a, c):
                    t, u, h = a.t, a.u, a.h
                    wait(v, st[u], 16 * h)
                    return v.tensor_tensor(o[:, u, :], d.psO[u][:, :], bias[:, :], ALU.add)
                d.dve(v, None, post, 0, 0)

            @block.tensor
            def _(pe):
                pe.wait_ge(ld, 32)
                d.pe(pe, lambda k: w[:, k, :])

            @block.scalar
            def _(act):
                d.act(act, pre=lambda a: act.copy(flat(d.rows[:, a.u, :, :]), tile_of(Hh, a.t)))


def layer3_end(env):
    nc, A, X, Hh = env["nc"], env["A"], env["X"], env["Hh"]
    d = Dense(env, "e3", D, un=2 * GL)
    with d.ph as ph:
        w = ph.sb("w", [P, 2, D])
        bias, alpha = ph.sb("bias", [P, D]), ph.sb("alpha", [P, D])
        ag = ph.sb("ag", [P, 2 * GL, D])
        tmp, r, x = ph.sb("tmp", [P, 2, D]), ph.sb("r", [P, 2, D]), ph.sb("x", [P, 2, D])
        ld, put = ph.sem("loaded"), ph.sem("put")
        got = [ph.sem(f"got{i}") for i in range(2)]
        with nc.Block() as block:
            @block.sync
            def _(sp):
                sp.dma_start(w[:, :, :], A["L3_gnn_W_post"].rearrange("(k p) o -> p k o", p=P)).then_inc(ld, 16)
                load_rows(sp, ld, [(bias[:, :], A["L3_gnn_b_post"]), (alpha[:, :], A["L3_gnn_alpha_mp"])])
                group_loads(d, sp, ag, got, env["agg_d"][2])

            @block.gpsimd
            def _(pool):
                for t in range(0, RT - 1, 12):
                    pool.wait_ge(d.taken, t + 12)
                    pool.dma_start(env["out"][t * P:(t + 12) * P, :].rearrange("(t p) d -> p t d", p=P),
                                 X[:, t:t + 12, :]).then_inc(put, 16)
                pool.wait_ge(d.taken, NT)
                pool.dma_start(env["out"][(RT - 1) * P:N, :], X[0:LAST, RT - 1, :]).then_inc(put, 16)
                pool.wait_ge(put, 80)

            @block.vector
            def _(v):
                v.wait_ge(ld, 48)

                def pre(a, c):
                    t, u = a.t, a.u
                    if a.k % GL == 0:
                        v.wait_ge(got[a.k // GL], 16 * (a.j + 1))
                    c(prelu(v, c, r[:, u, :], ag[:, a.k, :], alpha[:, :], tmp[:, u, :]))
                    return v.tensor_tensor(flat(d.rows[:, u, :, :]), tile_of(Hh, t), r[:, u, :], ALU.add)

                def post(a, c):
                    t, u, h = a.t, a.u, a.h
                    c(v.tensor_tensor(x[:, u, :], d.psO[u][:, :], bias[:, :], ALU.add))
                    return v.scalar_tensor_tensor(out=tile_of(X, t), in0=x[:, u, :], scalar=0.0, in1=tile_of(X, t),
                                                  op0=ALU.max, op1=ALU.add)
                d.dve(v, pre, post, 2, 1)

            @block.tensor
            def _(pe):
                pe.wait_ge(ld, 48)
                d.pe(pe, lambda k: w[:, k, :])

            @block.scalar
            def _(act):
                d.act(act)


_INS = ['x', 'src', 'dst', 'edge_type_8', 'L0_gnn_W', 'L0_gnn_b', 'L1_gnn_W_rel', 'L1_gnn_W_root', 'L1_gnn_bias',
        'L1_gnn_ln_gamma', 'L1_gnn_ln_beta', 'L2_gnn_W', 'L2_gnn_att', 'L3_gnn_W_pre', 'L3_gnn_b_pre',
        'L3_gnn_alpha_pre', 'L3_gnn_W_mp', 'L3_gnn_b_mp', 'L3_gnn_alpha_mp', 'L3_gnn_W_post', 'L3_gnn_b_post']


def kernel(**inputs):
    import numpy as _np
    import concourse.bacc as _bacc
    from concourse import mybir as _mybir
    from concourse.bass_utils import run_bass_kernel_spmd as _run

    nc = _bacc.Bacc("TRN2", target_bir_lowering=False, num_devices=1)
    arrays, args = {}, {}
    for name in _INS:
        a = _np.ascontiguousarray(inputs[name])
        arrays[f"in_{name}"] = a
        args[name] = nc.dram_tensor(f"in_{name}", a.shape, _mybir.dt.from_np(a.dtype), kind="ExternalInput").ap()
    out = nc.dram_tensor("out_x", (N, D), _mybir.dt.float32, kind="ExternalOutput").ap()
    build(nc, args, out)
    r = _run(nc, [arrays], core_ids=[0])
    return r.results[0]["out_x"]
```
